# Optimizing a Trainium2 kernel written in Bass

```python
import numpy as np
import jax
import jax.numpy as jnp

def _softmax(x, axis=-1):
    return jax.nn.softmax(x, axis=axis)

def _gelu(x):
    return jax.nn.gelu(x, approximate=True)

def _silu(x):
    return jax.nn.silu(x)

def _sigmoid(x):
    return jax.nn.sigmoid(x)

def _layernorm(x, axis=-1, eps=1e-05):
    m = jnp.mean(x, axis=axis, keepdims=True)
    v = jnp.var(x, axis=axis, keepdims=True)
    return (x - m) / jnp.sqrt(v + eps)

def _scatter_add(tgt, idx, src, axis=0):
    return tgt.at[idx].add(src)

def _segment_sum(src, seg, n):
    return jax.ops.segment_sum(src, seg, n)
kernel_name = 'mk_decoder_preln_d1_seqx_r4_d82642'

def setup_inputs(seed: int=0):
    np.random.seed(seed)
    _w = jnp.asarray

    def _rec_inputs():
        import jax
        import jax.numpy as jnp
        _rk = jax.random.key(seed)
        x = -0.0005207 + 1.001 * jax.random.normal(jax.random.fold_in(_rk, 1), (128, 128, 256), jnp.float32)
        _lenS = 128 - jax.random.randint(jax.random.fold_in(_rk, 7), (128,), 0, max(1, 128 // 4) + 1, jnp.int32)
        _lenS2 = 128 - jax.random.randint(jax.random.fold_in(_rk, 8), (128,), 0, max(1, 128 // 4) + 1, jnp.int32)
        _ctx_1024P = jax.random.normal(jax.random.fold_in(_rk, 11), (128, 16, 256), jnp.float32)
        _ctx_1024c = jax.random.dirichlet(jax.random.fold_in(_rk, 511), 0.3 * jnp.ones((16,), jnp.float32), (128, 128))
        _ctx_1024t = jnp.einsum('bsk,bkd->bsd', _ctx_1024c, _ctx_1024P)
        _ctx_1024t = _ctx_1024t * jax.lax.rsqrt(jnp.mean(jnp.square(_ctx_1024t)) + 1e-12) * 0.953939
        ctx_1024 = -0.000514642 + 1.00011 * (_ctx_1024t + 0.3 * jax.random.normal(jax.random.fold_in(_rk, 611), (128, 128, 256), jnp.float32))
        return (x, ctx_1024)
    x, ctx_1024 = _rec_inputs()

    def _L0_attn_setup():
        import jax, jax.numpy as jnp
        import numpy as np
        SPS_AMPLIFY = 1.5
        SPS_DAMPEN = 0.3
        SPS_DEEP_QUESTION = 0.1
        SPS_EXCLAIM = 0.85
        SPS_QUESTION = 0.25
        SPS_SUPER_EXCLAIM = 0.95
        B, S, D = (4, 512, 256)
        NUM_HEADS = 16
        HEAD_DIM = D // NUM_HEADS
        SCALE = HEAD_DIM ** (-0.5)

        def sps_pro(x):
            xn = jax.nn.sigmoid(x)
            mult = jnp.where(xn > SPS_SUPER_EXCLAIM, 2.0, jnp.where(xn > SPS_EXCLAIM, SPS_AMPLIFY, jnp.where(xn < SPS_DEEP_QUESTION, 0.1, jnp.where(xn < SPS_QUESTION, SPS_DAMPEN, 1.0))))
            return x * mult
        key = jax.random.key(seed)
        k0, k1, k2, k3, k4 = jax.random.split(key, 5)
        s = 1.0 / np.sqrt(D)
        return {'x': jax.random.normal(k0, (B, S, D), dtype=jnp.float32), 'W_qkv': jax.random.uniform(k1, (D, 3 * D), dtype=jnp.float32, minval=-s, maxval=s), 'b_qkv': jax.random.uniform(k2, (3 * D,), dtype=jnp.float32, minval=-s, maxval=s), 'W_proj': jax.random.uniform(k3, (D, D), dtype=jnp.float32, minval=-s, maxval=s), 'b_proj': jax.random.uniform(k4, (D,), dtype=jnp.float32, minval=-s, maxval=s)}
    _L0_attn_all = _L0_attn_setup()
    _L0_attn_in = {k: v for k, v in _L0_attn_all.items() if k in ('W_qkv', 'b_qkv', 'W_proj', 'b_proj')}
    del _L0_attn_all

    def _L0_xattn_setup():
        import jax, jax.numpy as jnp
        import numpy as np
        DIM = 256
        HEADS = 8
        HEAD_DIM = DIM // HEADS
        TAU = HEAD_DIM ** 0.5
        BS, SEQ = (1, 512)
        key = jax.random.key(seed)
        kq, kk, kv, kb = jax.random.split(key, 4)
        q = jax.random.normal(kq, (BS, SEQ, DIM), jnp.float32)
        k = jax.random.normal(kk, (BS, SEQ, DIM), jnp.float32)
        v = jax.random.normal(kv, (BS, SEQ, DIM), jnp.float32)
        Wi_w = jnp.zeros((HEADS, 3 * DIM), jnp.float32)
        Wi_b = 0.1 * jax.random.normal(kb, (HEADS,), jnp.float32)
        Wf_w = jnp.zeros((HEADS, 3 * DIM), jnp.float32)
        Wf_b = jnp.linspace(3.0, 6.0, HEADS, dtype=jnp.float32)
        gn_w = jnp.ones((DIM,), jnp.float32)
        gn_b = jnp.zeros((DIM,), jnp.float32)
        return {'q': q, 'k': k, 'v': v, 'Wi_w': Wi_w, 'Wi_b': Wi_b, 'Wf_w': Wf_w, 'Wf_b': Wf_b, 'gn_w': gn_w, 'gn_b': gn_b}
    _L0_xattn_all = _L0_xattn_setup()
    _L0_xattn_in = {k: v for k, v in _L0_xattn_all.items() if k in ('Wi_w', 'Wi_b', 'Wf_w', 'Wf_b', 'gn_w', 'gn_b')}
    del _L0_xattn_all

    def _L0_ffn_setup():
        import jax, jax.numpy as jnp
        import numpy as np
        LORA_DIM = 16
        LORA_TOKEN_INDEX = 1
        B, S, D, H = (4, 512, 256, 1024)
        key = jax.random.key(seed)
        ks = jax.random.split(key, 6)
        x = jax.random.normal(ks[0], (B, S, D), dtype=jnp.float32)
        W1 = jax.random.normal(ks[1], (H, D), dtype=jnp.float32) * 0.02
        b1 = jnp.zeros((H,), dtype=jnp.float32)
        W2 = jax.random.normal(ks[2], (D, H), dtype=jnp.float32) * 0.02
        b2 = jnp.zeros((D,), dtype=jnp.float32)
        scale = jnp.asarray(0.001, dtype=jnp.float32)
        return {'x': x, 'W1': W1, 'b1': b1, 'W2': W2, 'b2': b2, 'scale': scale}
    _L0_ffn_all = _L0_ffn_setup()
    _L0_ffn_in = {k: v for k, v in _L0_ffn_all.items() if k in ('W1', 'b1', 'W2', 'b2', 'scale')}
    del _L0_ffn_all
    return {'x': x, 'ctx_1024': ctx_1024, 'L0_attn_W_qkv': _L0_attn_in['W_qkv'], 'L0_attn_b_qkv': _L0_attn_in['b_qkv'], 'L0_attn_W_proj': _L0_attn_in['W_proj'], 'L0_attn_b_proj': _L0_attn_in['b_proj'], 'L0_xattn_Wi_w': _L0_xattn_in['Wi_w'], 'L0_xattn_Wi_b': _L0_xattn_in['Wi_b'], 'L0_xattn_Wf_w': _L0_xattn_in['Wf_w'], 'L0_xattn_Wf_b': _L0_xattn_in['Wf_b'], 'L0_xattn_gn_w': _L0_xattn_in['gn_w'], 'L0_xattn_gn_b': _L0_xattn_in['gn_b'], 'L0_ffn_W1': _L0_ffn_in['W1'], 'L0_ffn_b1': _L0_ffn_in['b1'], 'L0_ffn_W2': _L0_ffn_in['W2'], 'L0_ffn_b2': _L0_ffn_in['b2'], 'L0_ffn_scale': _L0_ffn_in['scale']}

def reference(x, ctx_1024, L0_attn_W_qkv, L0_attn_b_qkv, L0_attn_W_proj, L0_attn_b_proj, L0_xattn_Wi_w, L0_xattn_Wi_b, L0_xattn_Wf_w, L0_xattn_Wf_b, L0_xattn_gn_w, L0_xattn_gn_b, L0_ffn_W1, L0_ffn_b1, L0_ffn_W2, L0_ffn_b2, L0_ffn_scale):
    import jax
    import jax.numpy as jnp

    def _L0_attn_ref(x, W_qkv, b_qkv, W_proj, b_proj):
        import jax, jax.numpy as jnp
        import numpy as np
        SPS_AMPLIFY = 1.5
        SPS_DAMPEN = 0.3
        SPS_DEEP_QUESTION = 0.1
        SPS_EXCLAIM = 0.85
        SPS_QUESTION = 0.25
        SPS_SUPER_EXCLAIM = 0.95
        B, S, D = (4, 512, 256)
        NUM_HEADS = 16
        HEAD_DIM = D // NUM_HEADS
        SCALE = HEAD_DIM ** (-0.5)

        def sps_pro(x):
            xn = jax.nn.sigmoid(x)
            mult = jnp.where(xn > SPS_SUPER_EXCLAIM, 2.0, jnp.where(xn > SPS_EXCLAIM, SPS_AMPLIFY, jnp.where(xn < SPS_DEEP_QUESTION, 0.1, jnp.where(xn < SPS_QUESTION, SPS_DAMPEN, 1.0))))
            return x * mult
        qkv = jnp.einsum('bsd,de->bse', x, W_qkv) + b_qkv
        q, k, v = jnp.split(qkv, 3, axis=-1)
        attn = jnp.einsum('bsd,btd->bst', q, k) * SCALE
        attn = sps_pro(attn)
        attn = jax.nn.softmax(attn, axis=-1)
        out = jnp.einsum('bst,btd->bsd', attn, v)
        out = jnp.einsum('bsd,de->bse', out, W_proj) + b_proj
        return out

    def _L0_xattn_ref(q, k, v, Wi_w, Wi_b, Wf_w, Wf_b, gn_w, gn_b):
        import jax, jax.numpy as jnp
        import numpy as np
        DIM = 256
        HEADS = 8
        HEAD_DIM = DIM // HEADS
        TAU = HEAD_DIM ** 0.5
        BS, SEQ = (1, 512)
        bs, seq, dim = q.shape
        gate_in = jnp.concatenate([q, k, v], axis=-1)
        itilde = jnp.einsum('bsd,hd->bhs', gate_in, Wi_w) + Wi_b[None, :, None]
        ftilde = jnp.einsum('bsd,hd->bhs', gate_in, Wf_w) + Wf_b[None, :, None]
        csum = jnp.cumsum(jax.nn.log_sigmoid(ftilde), axis=-1)
        Fmat = csum[..., :, None] - csum[..., None, :]
        mask = jnp.tril(jnp.ones((seq, seq), dtype=bool))
        F_act = jnp.where(mask, Fmat, -jnp.inf)
        Dtilde = F_act + itilde[..., None, :]
        max_d = jnp.max(Dtilde, axis=-1, keepdims=True)
        D = jnp.exp(Dtilde - max_d)
        qh = q.reshape(bs, seq, HEADS, HEAD_DIM).transpose(0, 2, 1, 3)
        kh = k.reshape(bs, seq, HEADS, HEAD_DIM).transpose(0, 2, 1, 3)
        vh = v.reshape(bs, seq, HEADS, HEAD_DIM).transpose(0, 2, 1, 3)
        Ctilde = jnp.einsum('bhid,bhjd->bhij', qh, kh) * D / TAU
        maxit = jnp.maximum(jnp.abs(jnp.sum(Ctilde, axis=-1, keepdims=True)), jnp.exp(-max_d))
        Htilde = jnp.einsum('bhij,bhjd->bhid', Ctilde, vh) / (maxit + 1e-06)
        x = Htilde.transpose(0, 2, 1, 3).reshape(bs * seq, HEADS, HEAD_DIM)
        mean = jnp.mean(x, axis=-1, keepdims=True)
        var = jnp.var(x, axis=-1, keepdims=True)
        xn = (x - mean) / jnp.sqrt(var + 1e-05)
        out = xn.reshape(bs * seq, DIM) * gn_w + gn_b
        return out.reshape(bs, seq, DIM)

    def _L0_ffn_ref(x, W1, b1, W2, b2, scale):
        import jax, jax.numpy as jnp
        import numpy as np
        LORA_DIM = 16
        LORA_TOKEN_INDEX = 1
        B, S, D, H = (4, 512, 256, 1024)
        Bx, Sx, Dx = x.shape
        Hx = W1.shape[0]
        lt = jax.lax.dynamic_slice_in_dim(x, LORA_TOKEN_INDEX, LORA_DIM, axis=1)
        even = lt[:, ::2, :]
        odd = lt[:, 1::2, :]
        m1 = (even[:, :4, :, None] * odd[:, :4, None, :]).reshape(Bx, Hx, Dx)
        m2 = (even[:, 4:, :, None] * odd[:, 4:, None, :]).reshape(Bx, Dx, Hx)
        h = jnp.einsum('bsd,hd->bsh', x, W1) + scale * jnp.einsum('bsd,bhd->bsh', x, m1) + b1
        h = jax.nn.gelu(h, approximate=False)
        out = jnp.einsum('bsh,oh->bso', h, W2) + scale * jnp.einsum('bsh,boh->bso', h, m2) + b2
        return out
    x = x + _L0_attn_ref(_layernorm(x, axis=-1), L0_attn_W_qkv, L0_attn_b_qkv, L0_attn_W_proj, L0_attn_b_proj)
    x = x + _L0_xattn_ref(_layernorm(x, axis=-1), ctx_1024, ctx_1024, L0_xattn_Wi_w, L0_xattn_Wi_b, L0_xattn_Wf_w, L0_xattn_Wf_b, L0_xattn_gn_w, L0_xattn_gn_b)
    x = x + _L0_ffn_ref(_layernorm(x, axis=-1), L0_ffn_W1, L0_ffn_b1, L0_ffn_W2, L0_ffn_b2, L0_ffn_scale)
    return x

_drawn_inputs = setup_inputs


def setup_inputs(seed=0):
    import zlib

    import numpy as np

    out = dict(_drawn_inputs(seed))
    spreads = {'L0_xattn_Wi_w': (0.0, 0.1),
     'L0_xattn_Wf_w': (0.0, 0.1),
     'L0_xattn_gn_w': (1.0, 0.2),
     'L0_xattn_gn_b': (0.0, 0.1),
     'L0_ffn_b1': (0.0, 0.365),
     'L0_ffn_b2': (0.0, 0.1)}
    factors = {'L0_xattn_Wi_b': 64.0}
    for name, (base, spread) in spreads.items():
        noise = np.random.default_rng([zlib.crc32(name.encode()), seed]).standard_normal(out[name].shape)
        drawn = base * np.exp(spread * noise) if base else spread * noise
        out[name] = jnp.asarray(drawn.astype(out[name].dtype))
    for name, factor in factors.items():
        out[name] = (out[name] * factor).astype(out[name].dtype)
    return out
```

```python
from contextlib import ExitStack
import math

import numpy as np
import concourse.bass as bass
from concourse import mybir

F32 = mybir.dt.float32
BF16 = mybir.dt.bfloat16
ACT = mybir.ActivationFunctionType
ALU = mybir.AluOpType
AX_X = mybir.AxisListType.X

P = 128
D = 256
S = 128
G = 4
N = G * S
KD = D // P
HID = 1024
KH = HID // P
HEADS = 8
HD = D // HEADS
R = 4
CB = 4
U = D // CB
EXTRA = CB * R
WD = D + EXTRA
EPS = 1e-5
SCALE = (D // 16) ** -0.5
TAU = math.sqrt(HD)
LN_TAU = math.log(TAU)
CLAMP = 1e12
BANDS = (-math.log(9.0), -math.log(3.0), math.log(17.0 / 3.0), math.log(19.0))
EXP_SET = "natural_log_exp_and_others"


class Counter:

    def __init__(self, handle, per, base=0):
        self.h, self.per, self.base = handle, per, base

    def wait(self, eng, it, k):
        eng.wait_ge(self.h, it * self.per + (self.base + k))


class Chain(Counter):

    def start(self, it):
        self.it, self.k = it, 0

    def link(self, eng, ins):
        self.k += 1
        ins.then_inc(self.h, 1)
        self.wait(eng, self.it, self.k)

    def end(self):
        assert self.k == self.per, (self.k, self.per)


def build(nc, x, ctx_in, W_qkv, b_qkv, W_proj, b_proj, Wi_w, Wi_b, Wf_w, Wf_b, gn_w, gn_b,
          W1, b1, W2, b2, scale, out):
    NG = x.shape[0] // G
    STEPS = NG + 2
    ctx = ExitStack()
    with ctx:
        def sb(name, shape, dt=F32):
            return ctx.enter_context(nc.sbuf_tensor(name, shape, dt))

        def sem(name):
            return ctx.enter_context(nc.semaphore(name))

        opened = []

        def per_step(name, per, base=None):
            c = Counter(sem(name), per, 1 if base is None else base)
            if base is None:
                opened.append(c)
            return c

        ident = sb("ident", [P, P])
        A_w = sb("A_w", [P, KD, D])
        Wvp = sb("Wvp", [P, KD, D])
        cq = sb("cq", [P, KD])
        wrow = sb("wrow", [P, D])
        c0 = sb("c0", [P, 1])
        cvp = sb("cvp", [P, D])
        gnw_b = sb("gnw_b", [P, D])
        gnb_b = sb("gnb_b", [P, D])
        b2_b = sb("b2_b", [P, D])
        sc_b = sb("sc_b", [P, 1])
        b1c = sb("b1c", [P, KH])
        WgT = sb("WgT", [P, 4, 32])
        gbias = sb("gbias", [P, 1])
        W1T = sb("W1T", [P, KD, HID])
        W2x = [sb(f"W2x{i}", [P, KH, WD]) for i in range(2)]
        pick = sb("pick", [96, 32, P], BF16)
        ident_h = sb("ident_h", [P, P], BF16)
        later = sb("later", [P, P], BF16)
        onehot = sb("onehot", [P, HEADS, 32])
        sel_i = sb("sel_i", [P, 32])
        sel_f = sb("sel_f", [P, 32])
        sel_nf = sb("sel_nf", [P, 32])
        ones = sb("ones", [P, P])
        lntau = sb("lntau", [P, 1])
        xin = sb("xin", [P, G, D])
        xb = sb("xb", [P, G, D])
        xn1 = sb("xn1", [P, G, D])
        xn1T = sb("xn1T", [P, KD, N])
        qT = sb("qT", [P, KD, N])
        dots = sb("dots", [P, G, D])
        rowterm = sb("rowterm", [P, G])
        sc = sb("sc", [P, N])
        band_a = sb("band_a", [P, N])
        band_b = sb("band_b", [P, N])
        y = sb("y", [P, N])
        nmx = sb("nmx", [P, G])
        probs = sb("probs", [P, N])
        psums = sb("psums", [P, G])
        rinv = sb("rinv", [P, G])
        PT = sb("PT", [P, N])
        pxT = sb("pxT", [P, KD, N])
        x2 = sb("x2", [P, G, D])
        xn2 = sb("xn2", [P, G, D])
        xn2T = sb("xn2T", [P, KD, N])
        qpad = sb("qpad", [P, KD, 4, N])
        ctxn = sb("ctxn", [P, G, D])
        ctxT = sb("ctxT", [P, KD, N])
        hmean = sb("hmean", [P, G * HEADS])
        vc = sb("vc", [P, G, D])
        xg = sb("xg", [P, G, D])
        gate = sb("gate", [P, P])
        gabs = sb("gabs", [P, P])
        lsig = sb("lsig", [P, P])
        csum = sb("csum", [P, P])
        acs = sb("acs", [32, 2 * P])
        am = sb("am", [32, 2, P])
        amr = sb("amr", [32, 2, P])
        am2 = sb("am2", [32, 2, P], BF16)
        parts = sb("parts", [96, 2, P], BF16)
        em = sb("em", [P, P])
        emT = sb("emT", [P, 32])
        dx = [sb(f"dx{i}", [P, 4, P]) for i in range(2)]
        C = sb("C", [P, HEADS, P])
        HS = sb("HS", [P, 3 * P])
        HT = sb("HT", [P, G, 3 * P])
        sq = sb("sq", [P, D])
        v32 = sb("v32", [P, G * HEADS])
        cden = sb("cden", [P, G * HEADS])
        harg = sb("harg", [P, G * HEADS])
        hrs0 = sb("hrs0", [P, G * HEADS])
        htmp = sb("htmp", [P, G * HEADS])
        hrs = sb("hrs", [P, G * HEADS])
        Ng = sb("Ng", [P, G, D])
        x3 = sb("x3", [P, G, D])
        xf = sb("xf", [P, G, D])
        xn3 = sb("xn3", [P, G, D])
        xn3T = sb("xn3T", [P, KD, N])
        tg = sb("tg", [P, S])
        Tt = sb("Tt", [P, N])
        Et = sb("Et", [P, HID])
        Ev = sb("Ev", [P, G, D])
        gs = sb("gs", [P, EXTRA])
        gsT = sb("gsT", [P, S])
        hT = sb("hT", [P, KH, N])
        ot = sb("ot", [P, G, D])
        stat = [sb(f"stat{i}", [P, G, 6]) for i in range(3)]
        mean = [sb(f"mean{i}", [P, G]) for i in range(3)]
        half_gap = [sb(f"half_gap{i}", [P, G]) for i in range(3)]
        ve = [sb(f"ve{i}", [P, G]) for i in range(3)]
        lv = [sb(f"lv{i}", [P, G]) for i in range(3)]
        rs0 = [sb(f"rs0{i}", [P, G]) for i in range(3)]
        nt = [sb(f"nt{i}", [P, G]) for i in range(3)]
        rs = [sb(f"rs{i}", [P, G]) for i in range(3)]

        def bank(name):
            return ctx.enter_context(nc.psum_tensor(name, [P, 512], F32))

        TAB = [bank("TA"), bank("TB")]
        UAB = [bank("UA"), bank("UB")]
        DD = bank("DD")
        QQ = bank("QQ")
        PV = bank("PV")
        GT = bank("GT")

        UP = [QQ, DD] + UAB

        w1n = hT[:, 0:4, :].rearrange("p a b -> p (a b)").rearrange("p (k d) -> p k d", k=KH)
        w2n = hT[:, 4:8, :].rearrange("p a b -> p (a b)").rearrange("p (k h) -> p k h", k=KD)
        stage = qpad[:, :, :, :].rearrange("p a b c -> p (a b c)")
        wn = stage[:, 0:1536].rearrange("p (k e) -> p k e", k=KD)
        wT = stage[:, 1536:3072].rearrange("p (w k d) -> p w k d", w=3, k=KD)
        wp = stage[:, 3072:3584].rearrange("p (k o) -> p k o", k=KD)
        bB = stage[:, 3584:4096].rearrange("p (w k n) -> p w k n", w=2, k=KD)
        bcol = sb("bcol", [P, 6])
        wgn = xn1T[:, 0, :].rearrange("p n -> p n")
        wg3 = xn2T[:, :, :].rearrange("p a b -> p (a b)")[0:16, 0:3 * D]
        bp_b = dots[:, 0, :]
        w1p = [t[:, 2 * j:2 * j + 2, :].rearrange("p a b -> p (a b)") for t in (Ng, ot) for j in range(2)]
        w2p = [C[:, 4 * j:4 * j + 4, :].rearrange("p a b -> p (a b)") for j in range(2)] + [pxT[:, j, :] for j in range(2)]

        s_load = sem("weights_loaded")
        s_zero = sem("zeroed")
        s_idz = sem("ident_step")
        s_set_pe = sem("setup_pe")
        s_set_v = sem("setup_dve")
        s_pre_a = sem("first_log")

        x_loaded = per_step("x_loaded", 16, 16)
        ctx_loaded = per_step("ctx_loaded", 16, 16)
        qpad_loaded = per_step("qpad_loaded", 8 * 16)
        t_loaded = per_step("t_loaded", G * 16)
        e_loaded = per_step("e_loaded", R * 16)
        ev_loaded = per_step("ev_loaded", R * G * 16)
        stored = per_step("stored", 16)
        xn1T_mm = per_step("xn1T_mm", 2)
        ctxT_mm = per_step("ctxT_mm", 2)
        xn2T_mm = per_step("xn2T_mm", 2)
        qT_mm = per_step("qT_mm", 2)
        gate_mm = per_step("gate_mm", 1)
        xn3T_mm = per_step("xn3T_mm", 2)
        score_mm = per_step("score_mm", 1)
        gram_mm = per_step("gram_mm", 1)
        up_mm = per_step("up_mm", KH)
        sel_mm = per_step("sel_mm", 1)
        PT_mm = per_step("PT_mm", 1)
        px_mm = per_step("px_mm", 2)
        wv_mm = per_step("wv_mm", 2)
        em_mm = per_step("em_mm", 1)
        d_mm = per_step("d_mm", 2 * G)
        qk_mm = per_step("qk_mm", 2 * G)
        pv_mm = per_step("pv_mm", G)
        ht_mm = per_step("ht_mm", G)
        down_mm = per_step("down_mm", G)
        gsT_mm = per_step("gsT_mm", G)
        adapt_mm = per_step("adapt_mm", G)
        xn1T_ok = per_step("xn1T_ok", 2)
        ctxT_ok = per_step("ctxT_ok", 2)
        xn2T_ok = per_step("xn2T_ok", 2)
        qT_ok = per_step("qT_ok", 2)
        xn3T_ok = per_step("xn3T_ok", 2)
        sc_ok = per_step("sc_ok", 1)
        h_ok = per_step("h_ok", KH)
        lnsig_ok = per_step("lnsig_ok", 1)
        probs_ok = per_step("probs_ok", 1)
        PT_ok = per_step("PT_ok", 1)
        px_ok = per_step("px_ok", 2)
        em_ok = per_step("em_ok", 1)
        dexp_ok = per_step("dexp_ok", 2 * G)
        HS_ok = per_step("HS_ok", G)
        HT_ok = per_step("HT_ok", G)
        sq_ok = per_step("sq_ok", G)
        gsT_ok = per_step("gsT_ok", G)
        hrs0_ok = per_step("hrs0_ok", 1)
        rs0_ok = [per_step("rs0_ok0", 1, 1), per_step("rs0_ok1", 1), per_step("rs0_ok2", 1)]
        ve_ok = [per_step("ve_ok0", 1, 1), per_step("ve_ok1", 1), per_step("ve_ok2", 1)]
        xn_ok = [per_step("xn1_ok", 1, 1), per_step("xn2_ok", 1), per_step("xn3_ok", 1)]
        rowterm_ok = per_step("rowterm_ok", 1)
        hmean_ok = per_step("hmean_ok", 1)
        gate_ok = per_step("gate_ok", 1)
        tg_ok = per_step("tg_ok", 1)
        y_ok = per_step("y_ok", 1)
        csum_ok = per_step("csum_ok", 1)
        acs_ok = per_step("acs_ok", 1)
        parts_ok = per_step("parts_ok", 1)
        md_ok = per_step("md_ok", 1)
        emT_ok = per_step("emT_ok", 1)
        gs_ok = per_step("gs_ok", G)
        c_ok = per_step("c_ok", 2 * G)
        x2_ok = per_step("x2_ok", G)
        hred_ok = per_step("hred_ok", G)
        harg_ok = per_step("harg_ok", 1)
        x3_ok = per_step("x3_ok", 1)
        ot_ok = per_step("ot_ok", G)
        xb_ok = per_step("xb_ok", 1)
        vc_ok = per_step("vc_ok", 1)
        xg_ok = per_step("xg_ok", 1)
        xf_ok = per_step("xf_ok", 1)
        fill_ok = per_step("fill_ok", G)
        ng_ok = per_step("ng_ok", G)
        v_chain = Chain(sem("dve_step"), 48)
        a_chain = Chain(sem("act_step"), 6)

        x_g = x.rearrange("(g b) s d -> g s b d", b=G)
        c_g = ctx_in.rearrange("(g b) s d -> g s b d", b=G)
        o_g = out.rearrange("(g b) s d -> g s b d", b=G)
        row = lambda a: a.rearrange("(o n) -> o n", o=1).broadcast_to([P, a.shape[0]])

        block = ctx.enter_context(nc.Block())

        @block.sync
        def _(sp):
            sp.wait_ge(s_zero, 1)
            for dst, src in (
                [(wn, W_qkv.rearrange("(k p) e -> p k e", p=P)),
                 (wp, W_proj.rearrange("(k p) o -> p k o", p=P)),
                 (bcol[:, :], b_qkv.rearrange("(n p) -> p n", p=P)),
                 (bp_b, row(b_proj)), (gnw_b[:, :], row(gn_w)), (gnb_b[:, :], row(gn_b)),
                 (b2_b[:, :], row(b2)), (sc_b[:, :], row(scale)),
                 (wg3[0:8, :], Wi_w), (wg3[8:16, :], Wf_w),
                 (w2n, W2.rearrange("(k p) h -> p k h", p=P))]
                + [(gbias[32 * b + 8 * t:32 * b + 8 * t + 8, 0:1], w.rearrange("(n o) -> n o", o=1))
                   for b in range(G) for t, w in enumerate((Wi_b, Wf_b))]
                + [(w1n[64 * (c % 2):64 * (c % 2) + 64, 2 * r + c // 2, :],
                    W1.rearrange("(r u c) d -> r c u d", r=R, c=CB)[r, c]) for r in range(R) for c in range(CB)]
                + [(b1c[64 * (c % 2):64 * (c % 2) + 64, 2 * r + c // 2:2 * r + c // 2 + 1],
                    b1.rearrange("(r u c o) -> r c u o", r=R, c=CB, o=1)[r, c]) for r in range(R) for c in range(CB)]
            ):
                sp.dma_start(dst, src, allow_slow_non_contiguous=True).then_inc(s_load, 16)
            sp.dma_start(xin[:, :, :], x_g[0]).then_inc(x_loaded.h, 16)
            sp.dma_start(ctxn[:, :, :], c_g[0]).then_inc(ctx_loaded.h, 16)
            sp.wait_ge(s_set_v, SETUP_V)

            def step(it, nxt, cur, f):
                qk_mm.wait(sp, it, 0)
                for c in range(KD):
                    xn2T_ok.wait(sp, it, c + 1)
                    for r in range(4):
                        sp.dma_start(qpad[32 * r:32 * r + 32, c, r, :], xn2T[32 * r:32 * r + 32, c, :])\
                          .then_inc(qpad_loaded.h, 16)
                xn_ok[2].wait(sp, it, 1)
                up_mm.wait(sp, it, 0)
                for r in range(R):
                    sp.dma_start(Et[r:4 * G:R, r * D:(r + 1) * D],
                                 xn3[1 + 2 * r:2 + 2 * r, :, :]).then_inc(e_loaded.h, 16)
                tg_ok.wait(sp, it, 1)
                for b in range(G):
                    sp.dma_start(Tt[R * b:R * b + R, b * S:(b + 1) * S], tg[32 * b:32 * b + R, :])\
                      .then_inc(t_loaded.h, 16)
                adapt_mm.wait(sp, it, 0)
                for r in range(R):
                    for b in range(G):
                        sp.dma_start(Ev[r:R * CB:R, b, r * U:(r + 1) * U],
                                     xn3[9 + 2 * r:10 + 2 * r, b, :].rearrange("o (c u) -> o c u", c=CB))\
                          .then_inc(ev_loaded.h, 16)
                xn_ok[0].wait(sp, it, 0)
                xb_ok.wait(sp, it, 1)
                sp.dma_start(xin[:, :, :], x_g[nxt]).then_inc(x_loaded.h, 16)
                vc_ok.wait(sp, it, 1)
                ctxT_mm.wait(sp, it, 2)
                sp.dma_start(ctxn[:, :, :], c_g[cur]).then_inc(ctx_loaded.h, 16)
                ot_ok.wait(sp, it, G)
                sp.dma_start(o_g[f], ot[:, :, :]).then_inc(stored.h, 16)

            for it in range(2):
                step(it, min(it + 1, NG - 1), it, 0)
            with sp.Fori(2, NG - 1) as it:
                step(it, it + 1, it, it - 2)
            for it in range(NG - 1, STEPS):
                step(it, NG - 1, min(it, NG - 1), it - 2)
            x_loaded.wait(sp, STEPS, 0)
            ctx_loaded.wait(sp, STEPS, 0)
            stored.wait(sp, STEPS, 0)

        @block.gpsimd
        def _(pool):
            for c in opened:
                pool.sem_inc(c.h, 1)
            for t in (x2, xn2, x3, xn3, ctxT, Tt, Et, Ev, gsT, em, W2x[0], W2x[1], WgT, gbias):
                flat = t[tuple([slice(None)] * len(t.shape))]
                last = pool.memset(flat, 0.0)
            last.then_inc(s_idz, 1)
            pool.memset(ident[:, :], 0.0)
            pool.memset(sel_i[:, :], 0.0)
            pool.memset(ident_h[:, :], 0.0)
            pool.memset(later[:, :], 0.0)
            pool.memset(sel_f[:, :], 0.0)
            pool.memset(sel_nf[:, :], 0.0)
            pool.memset(pick[:, :, :], 0.0)
            pool.memset(onehot[:, :, :], 0.0).then_inc(s_idz, 1)
            pool.wait_ge(s_idz, 2)
            pool.affine_select(out=ident[:, :], in_=ident[:, :], compare_op=ALU.not_equal, fill=1.0,
                               base=0, pattern=[[-1, P]], channel_multiplier=1)
            for t, base, val in ((sel_i, 0, 1.0), (sel_f, -8, 1.0), (sel_nf, -8, -1.0)):
                v = t[:, :].rearrange("p (b h) -> p b h", b=G)
                pool.affine_select(out=v, in_=v, compare_op=ALU.not_equal, fill=val, base=base,
                                   pattern=[[-32, G], [-1, 8]], channel_multiplier=1)
            pool.affine_select(out=pick[0:32, :, :], in_=pick[0:32, :, :], compare_op=ALU.not_equal, fill=1.0,
                               base=0, pattern=[[-1, 32], [0, P]], channel_multiplier=1)
            pool.affine_select(out=ident_h[:, :], in_=ident_h[:, :], compare_op=ALU.not_equal, fill=1.0,
                               base=0, pattern=[[-1, P]], channel_multiplier=1)
            pool.affine_select(out=later[:, :], in_=later[:, :], compare_op=ALU.is_ge, fill=-1e30,
                               base=0, pattern=[[1, P]], channel_multiplier=-1)
            pool.memset(onehot[:, 0:4, 0:1], 1.0)
            pool.memset(onehot[:, 4:8, 1:2], 1.0)
            pool.memset(ones[:, :], 1.0)
            pool.memset(lntau[:, :], LN_TAU).then_inc(s_zero, 1)

            pool.wait_ge(s_load, 16 * LOADS)
            pool.wait_ge(s_set_v, SETUP_V)

            def fill(it, b):
                if b >= 2:
                    down_mm.wait(pool, it, b - 1)
                else:
                    xn3T_ok.wait(pool, it, 2)
                    down_mm.wait(pool, it, 0)
                w = W2x[b % 2]
                for c in range(CB):
                    tokens = xn3T[:, :, b * S + 10:b * S + 10 + 2 * R:2]
                    ins = pool.tensor_tensor(w[:, 2 * c:2 * c + 2, D + R * c:D + R * c + R], tokens,
                                             ones[:, 0:2 * R].rearrange("p (k r) -> p k r", k=2), ALU.mult)
                ins.then_inc(fill_ok.h, 1)

            with pool.Fori(0, STEPS) as it:
                x_loaded.wait(pool, it, 0)
                x2_ok.wait(pool, it, 0)
                pool.tensor_tensor(xb[:, :, :], xin[:, :, :], cvp[:, :].unsqueeze(1).broadcast_to([P, G, D]),
                                   ALU.add).then_inc(xb_ok.h, 1)
                hmean_ok.wait(pool, it, 1)
                pv_mm.wait(pool, it, 0)
                pool.tensor_tensor(vc[:, :, :].rearrange("p b (h d) -> p (b h) d", h=HEADS),
                                   ctxn[:, :, :].rearrange("p b (h d) -> p (b h) d", h=HEADS),
                                   hmean[:, :].unsqueeze(2).broadcast_to([P, G * HEADS, HD]),
                                   ALU.subtract).then_inc(vc_ok.h, 1)
                x3_ok.wait(pool, it, 0)
                pool.tensor_tensor(xg[:, :, :], x2[:, :, :], gnb_b[:, :].unsqueeze(1).broadcast_to([P, G, D]),
                                   ALU.add).then_inc(xg_ok.h, 1)
                ot_ok.wait(pool, it, 0)
                pool.tensor_tensor(xf[:, :, :], x3[:, :, :], b2_b[:, :].unsqueeze(1).broadcast_to([P, G, D]),
                                   ALU.add).then_inc(xf_ok.h, 1)
                fill(it, 0)
                fill(it, 1)

                def weigh(b):
                    HT_ok.wait(pool, it, b + 1)
                    pool.tensor_tensor(Ng[:, b, :], HT[:, b, 0:D], gnw_b[:, :], ALU.mult).then_inc(ng_ok.h, 1)

                fill(it, 2)
                weigh(0)
                fill(it, 3)
                for b in range(1, G):
                    weigh(b)

        @block.scalar
        def _(act):
            a = a_chain

            def ln_root(i, it):
                ve_ok[i].wait(act, it, 1)
                a.link(act, act.activation(lv[i][:, :], ve[i][:, :], ACT.Ln))
                act.activation(rs0[i][:, :], lv[i][:, :], ACT.Exp, scale=-0.5).then_inc(rs0_ok[i].h, 1)

            act.preload_act_table_set(EXP_SET)
            act.wait_ge(ve_ok[0].h, 1)
            act.activation(lv[0][:, :], ve[0][:, :], ACT.Ln).then_inc(s_pre_a, 1)
            act.wait_ge(s_pre_a, 1)
            act.activation(rs0[0][:, :], lv[0][:, :], ACT.Exp, scale=-0.5).then_inc(rs0_ok[0].h, 1)
            act.wait_ge(s_set_v, SETUP_V)

            with act.Fori(0, STEPS) as it:
                a.start(it)

                def evac(mm, ok, dst, free, bias=None):
                    for c in range(KD):
                        mm.wait(act, it, c + 1)
                        if c == 0:
                            for f in free:
                                f.wait(act, it, 0)
                        if bias is None:
                            ins = act.activation(dst[:, c, :], TAB[c][:, :], ACT.Copy)
                        else:
                            ins = act.activation(dst[:, c, :], TAB[c][:, :], ACT.Identity, bias=bias[:, c:c + 1])
                        ins.then_inc(ok.h, 1)

                evac(xn1T_mm, xn1T_ok, xn1T, [])
                evac(ctxT_mm, ctxT_ok, ctxT, [qk_mm])
                qpad_loaded.wait(act, it, 0)
                evac(xn2T_mm, xn2T_ok, xn2T, [])
                ln_root(2, it)
                evac(qT_mm, qT_ok, qT, [], bias=cq)
                evac(xn3T_mm, xn3T_ok, xn3T, [down_mm])
                gate_ok.wait(act, it, 1)
                a.link(act, act.activation(gabs[:, :], gate[:, :], ACT.Abs))
                a.link(act, act.activation(lsig[:, :], gabs[:, :], ACT.Exp, scale=-1.0))
                act.activation(gabs[:, :], lsig[:, :], ACT.Ln, bias=1.0).then_inc(lnsig_ok.h, 1)
                act.preload_act_table(ACT.Gelu)
                score_mm.wait(act, it, 1)
                rowterm_ok.wait(act, it, 1)
                for b in range(G):
                    ins = act.activation(sc[:, b * S:(b + 1) * S], TAB[0][:, b * S:(b + 1) * S], ACT.Identity,
                                         bias=rowterm[:, b:b + 1], scale=SCALE)
                ins.then_inc(sc_ok.h, 1)
                for hc in range(KH):
                    up_mm.wait(act, it, hc + 1)
                    act.activation(hT[:, hc, :], UP[hc % 4][:, :], ACT.Gelu, bias=b1c[:, hc:hc + 1])\
                        .then_inc(h_ok.h, 1)

                act.preload_act_table_set(EXP_SET)

                def gsT_copy(b):
                    gsT_mm.wait(act, it, b + 1)
                    act.activation(gsT[0:EXTRA, :], GT[0:EXTRA, 0:S], ACT.Copy).then_inc(gsT_ok.h, 1)

                def dexp(b, hf):
                    d_mm.wait(act, it, 2 * b + hf + 1)
                    c_ok.wait(act, it, 2 * b + hf - 1) if 2 * b + hf >= 1 else c_ok.wait(act, it, 0)
                    act.activation(dx[hf][:, :, :].rearrange("p h i -> p (h i)"), DD[:, :], ACT.Exp)\
                        .then_inc(dexp_ok.h, 1)

                def hs(b):
                    pv_mm.wait(act, it, b + 1)
                    act.activation(HS[:, :], PV[:, 0:3 * P], ACT.Copy).then_inc(HS_ok.h, 1)

                def ht(b):
                    ht_mm.wait(act, it, b + 1)
                    if b == 0:
                        x3_ok.wait(act, it, 0)
                    act.activation(HT[:, b, :], PV[:, 0:3 * P], ACT.Copy).then_inc(HT_ok.h, 1)
                    HT_ok.wait(act, it, b + 1)
                    hred_ok.wait(act, it, b)
                    act.activation(sq[:, :], HT[:, b, 0:D], ACT.Square).then_inc(sq_ok.h, 1)

                dexp(0, 0)
                y_ok.wait(act, it, 1)
                for b in range(G):
                    ins = act.activation(probs[:, b * S:(b + 1) * S], y[:, b * S:(b + 1) * S], ACT.Exp,
                                         bias=nmx[:, b:b + 1], accum_out=psums[:, b:b + 1])
                ins.then_inc(probs_ok.h, 1)
                md_ok.wait(act, it, 1)
                act.activation(em[0:32, :], em[0:32, :], ACT.Exp, scale=-1.0, bias=lntau[0:32, :]).then_inc(em_ok.h, 1)
                PT_mm.wait(act, it, 1)
                act.activation(PT[:, :], TAB[1][:, :], ACT.Copy).then_inc(PT_ok.h, 1)
                dexp(0, 1)
                gsT_copy(0)
                for m in range(KD):
                    px_mm.wait(act, it, m + 1)
                    act.activation(pxT[:, m, :], TAB[m][:, :], ACT.Copy).then_inc(px_ok.h, 1)
                ln_root(0, it)
                dexp(1, 0)
                hs(0)
                ht(0)
                dexp(1, 1)
                gsT_copy(1)
                dexp(2, 0)
                ln_root(1, it)
                hs(1)
                dexp(2, 1)
                ht(1)
                dexp(3, 0)
                hs(2)
                ht(2)
                dexp(3, 1)
                hs(3)
                gsT_copy(2)
                ht(3)
                harg_ok.wait(act, it, 1)
                a.link(act, act.activation(htmp[:, :], harg[:, :], ACT.Ln))
                act.activation(hrs0[:, :], htmp[:, :], ACT.Exp, scale=-0.5).then_inc(hrs0_ok.h, 1)
                gsT_copy(3)
                a.end()

        @block.vector
        def _(dve):
            v = v_chain
            setup = [0]

            def done(ins):
                setup[0] += 1
                ins.then_inc(s_set_v, 1)
                dve.wait_ge(s_set_v, setup[0])

            def ln_stats(i, X, link, it, ok):
                for b in range(G):
                    ins = dve.bn_stats(stat[i][:, b, :], X[:, b, :])
                link(ins)
                even, odd = stat[i][:, :, 0:3], stat[i][:, :, 3:6]
                dve.tensor_tensor(mean[i][:, :], even[:, :, 1], odd[:, :, 1], ALU.add)
                dve.tensor_tensor(half_gap[i][:, :], even[:, :, 1], odd[:, :, 1], ALU.subtract)
                link(dve.tensor_tensor(ve[i][:, :], even[:, :, 2], odd[:, :, 2], ALU.add))
                dve.tensor_scalar(mean[i][:, :], mean[i][:, :], 0.5, None, ALU.mult)
                dve.tensor_scalar(ve[i][:, :], ve[i][:, :], 1.0 / D, EPS, ALU.mult, ALU.add)
                link(dve.scalar_tensor_tensor(half_gap[i][:, :], half_gap[i][:, :], 0.25, half_gap[i][:, :],
                                              ALU.mult, ALU.mult))
                dve.tensor_tensor(ve[i][:, :], ve[i][:, :], half_gap[i][:, :], ALU.add).then_inc(ve_ok[i].h, 1)

            def ln_apply(i, X, Xn, link):
                link(dve.tensor_tensor(nt[i][:, :], rs0[i][:, :], rs0[i][:, :], ALU.mult))
                link(dve.tensor_tensor(nt[i][:, :], nt[i][:, :], ve[i][:, :], ALU.mult))
                link(dve.tensor_scalar(nt[i][:, :], nt[i][:, :], -0.5, 1.5, ALU.mult, ALU.add))
                link(dve.tensor_tensor(rs[i][:, :], nt[i][:, :], rs0[i][:, :], ALU.mult))
                for b in range(G):
                    src, dst = X[:, b, :], Xn[:, b, :]
                    if i == 2:
                        src = src.rearrange("p (u c) -> p c u", c=CB)
                        dst = dst.rearrange("p (c u) -> p c u", c=CB)
                    ins = dve.tensor_scalar(dst, src, mean[i][:, b:b + 1], rs[i][:, b:b + 1], ALU.subtract, ALU.mult)
                ins.then_inc(xn_ok[i].h, 1)

            dve.wait_ge(x_loaded.h, 16)
            ln_stats(0, xin, done, 0, None)
            dve.wait_ge(rs0_ok[0].h, 1)
            ln_apply(0, xin, xn1, done)
            dve.wait_ge(s_zero, 1)
            dve.wait_ge(s_load, 16 * LOADS)
            done(dve.tensor_copy(pick[32:64, :, :], pick[0:32, :, :]))
            done(dve.tensor_copy(pick[64:96, :, :], pick[0:32, :, :]))
            done(dve.tensor_copy(bB, bcol[:, 2:6].rearrange("p (w k) -> p w k", w=2).unsqueeze(3)
                                 .broadcast_to([P, 2, KD, P])))
            done(dve.tensor_tensor(wgn[0:16, 0:D], wg3[:, D:2 * D], wg3[:, 2 * D:3 * D], ALU.add))
            for i in range(4):
                done(dve.tensor_copy(
                    w1p[i].rearrange("p (q c u) -> p q c u", q=4, c=2),
                    w1n[:, 4 * (i % 2):4 * (i % 2) + 4, :].rearrange("p q (u c) -> p q c u", c=CB)
                    [:, :, 2 * (i // 2):2 * (i // 2) + 2, :]))
                done(dve.tensor_copy(
                    w2p[i].rearrange("p (o c u) -> p o c u", o=KD, c=CB),
                    w2n[:, :, i * D:(i + 1) * D].rearrange("p o (u c) -> p o c u", c=CB)))
            n = 0
            for w in range(3):
                n += 1
                dve.wait_ge(s_set_pe, n)
                done(dve.tensor_copy(wT[:, w, :, :].rearrange("p k d -> p (k d)"), TAB[w % 2][:, :]))
            for k in range(KD):
                n += 1
                dve.wait_ge(s_set_pe, n)
                done(dve.tensor_copy(A_w[:, k, :], UAB[k][:, 0:D]))
            for k in range(KD):
                n += 1
                dve.wait_ge(s_set_pe, n)
                done(dve.tensor_copy(Wvp[:, k, :], UAB[k][:, 0:D]))
            n += 1
            dve.wait_ge(s_set_pe, n)
            done(dve.tensor_scalar(wrow[:, :], DD[:, 0:D], SCALE, None, ALU.mult))
            done(dve.tensor_tensor(cvp[:, :], DD[:, D:2 * D], bp_b, ALU.add))
            done(dve.tensor_copy(cq[:, :], QQ[:, 0:KD]))
            done(dve.tensor_scalar(c0[:, :], QQ[:, KD:KD + 1], SCALE, None, ALU.mult))
            n += 1
            dve.wait_ge(s_set_pe, n)
            done(dve.tensor_copy(WgT[:, :, 0:16], PV[:, 0:64].rearrange("p (k n) -> p k n", k=4)))
            for i in range(4):
                n += 1
                dve.wait_ge(s_set_pe, n)
                done(dve.tensor_copy(W1T[:, i // 2, (i % 2) * 512:(i % 2) * 512 + 512], TAB[i % 2][:, :]))
            for i in range(4):
                n += 1
                dve.wait_ge(s_set_pe, n)
                src = TAB[i % 2][:, :].rearrange("p (k o) -> p k o", k=2)
                dve.tensor_copy(W2x[0][:, 2 * i:2 * i + 2, 0:D], src)
                done(dve.tensor_copy(W2x[1][:, 2 * i:2 * i + 2, 0:D], src))
            done(dve.memset(stage, 0.0))
            assert setup[0] == SETUP_V, setup[0]

            with dve.Fori(0, STEPS) as it:
                v.start(it)
                link = lambda ins: v.link(dve, ins)
                x3_ok.wait(dve, it, 0)
                ln_stats(2, x3, link, it, None)
                ctx_loaded.wait(dve, it, 0)
                vc_ok.wait(dve, it, 0)
                link(dve.tensor_reduce(hmean[:, :], ctxn[:, :, :].rearrange("p b (h d) -> p (b h) d", h=HEADS),
                                       AX_X, ALU.add))
                dve.tensor_scalar(hmean[:, :], hmean[:, :], 1.0 / HD, None, ALU.mult).then_inc(hmean_ok.h, 1)
                rs0_ok[2].wait(dve, it, 1)
                e_loaded.wait(dve, it, 0)
                ev_loaded.wait(dve, it, 0)
                ln_apply(2, x3, xn3, link)
                for b in range(G):
                    ins = dve.tensor_tensor_reduce(dots[:, b, :], xn1[:, b, :], wrow[:, :], 1.0, 0.0, ALU.mult, ALU.add,
                                                   rowterm[:, b:b + 1])
                link(ins)
                sc_ok.wait(dve, it, 0)
                dve.tensor_scalar(rowterm[:, :], rowterm[:, :], c0[:, 0:1], None, ALU.add).then_inc(rowterm_ok.h, 1)
                gate_mm.wait(dve, it, 1)
                dve.tensor_scalar(gate[:, :], GT[:, 0:P], gbias[:, 0:1], None, ALU.add).then_inc(gate_ok.h, 1)
                gram_mm.wait(dve, it, 1)
                t_loaded.wait(dve, it, 0)
                dve.tensor_scalar(tg[:, :], GT[:, 0:P], sc_b[:, 0:1], None, ALU.mult).then_inc(tg_ok.h, 1)
                lnsig_ok.wait(dve, it, 1)
                link(dve.scalar_tensor_tensor(lsig[:, :], gate[:, :], 0.0, gabs[:, :], ALU.min, ALU.subtract))
                dve.tensor_tensor_scan(csum[:, :], ones[:, :], lsig[:, :], 0.0, ALU.mult, ALU.add)\
                   .then_inc(csum_ok.h, 1)
                sc_ok.wait(dve, it, 1)
                link(dve.tensor_scalar(band_a[:, :], sc[:, :], BANDS[0], 0.3, ALU.is_ge, ALU.mult))
                dve.tensor_scalar(band_b[:, :], sc[:, :], BANDS[3], None, ALU.is_gt)
                link(dve.scalar_tensor_tensor(band_a[:, :], sc[:, :], BANDS[1], band_a[:, :], ALU.is_ge, ALU.max))
                link(dve.scalar_tensor_tensor(band_b[:, :], sc[:, :], BANDS[2], band_b[:, :], ALU.is_gt, ALU.add))
                link(dve.scalar_tensor_tensor(band_a[:, :], band_b[:, :], 0.5, band_a[:, :], ALU.mult, ALU.add))
                link(dve.scalar_tensor_tensor(y[:, :], band_a[:, :], 0.1, sc[:, :], ALU.max, ALU.mult))
                link(dve.tensor_reduce(nmx[:, :], y[:, :].rearrange("p (b t) -> p b t", b=G), AX_X, ALU.max))
                dve.tensor_scalar(nmx[:, :], nmx[:, :], -1.0, None, ALU.mult).then_inc(y_ok.h, 1)
                sel_mm.wait(dve, it, 1)
                dve.tensor_copy(acs[:, :], GT[0:32, 0:2 * P]).then_inc(acs_ok.h, 1)
                acs_ok.wait(dve, it, 1)
                link(dve.tensor_tensor_scan(am[:, 1, :], acs[:, 0:P], acs[:, 0:P], -3e38, ALU.max, ALU.max))
                dve.tensor_copy(am[:, 0, :], acs[:, 0:P])
                em_mm.wait(dve, it, 0)
                link(dve.tensor_tensor(em[0:32, :], am[:, 1, :], acs[:, P:2 * P], ALU.add))
                dve.tensor_scalar(em[0:32, :], em[0:32, :], -25.0, None, ALU.max).then_inc(md_ok.h, 1)
                link(dve.tensor_scalar(am[:, 1, :], am[:, 1, :], -1.0, None, ALU.mult))
                d_mm.wait(dve, it, 0)
                link(dve.tensor_copy(parts[0:32, :, :], am[:, :, :]))
                link(dve.tensor_tensor(amr[:, :, :], am[:, :, :], parts[0:32, :, :], ALU.subtract))
                link(dve.tensor_copy(am2[:, :, :], amr[:, :, :]))
                dve.tensor_copy(parts[32:64, :, :], am2[:, :, :])
                dve.tensor_tensor(parts[64:96, :, :], amr[:, :, :], am2[:, :, :], ALU.subtract)\
                   .then_inc(parts_ok.h, 1)

                def g_out(b):
                    down_mm.wait(dve, it, b + 1)
                    gsT_mm.wait(dve, it, b)
                    dve.tensor_scalar(gs[:, :], UAB[b % 2][:, D:WD], sc_b[:, 0:1], None, ALU.mult)\
                        .then_inc(gs_ok.h, 1)

                def o_out(b):
                    adapt_mm.wait(dve, it, b + 1)
                    if b == 0:
                        stored.wait(dve, it, 0)
                        xf_ok.wait(dve, it, 1)
                    dve.tensor_tensor(ot[:, b, :], UAB[b % 2][:, 0:D], xf[:, b, :], ALU.add).then_inc(ot_ok.h, 1)

                def weigh_qk(b, hf):
                    k = 2 * b + hf
                    dexp_ok.wait(dve, it, k + 1)
                    qk_mm.wait(dve, it, k + 1)
                    pv_mm.wait(dve, it, b)
                    dve.tensor_tensor(C[:, 4 * hf:4 * hf + 4, :].rearrange("p h i -> p (h i)"),
                                      dx[hf][:, :, :].rearrange("p h i -> p (h i)"), QQ[:, :], ALU.mult)\
                        .then_inc(c_ok.h, 1)

                def head_sums(b):
                    HT_ok.wait(dve, it, b + 1)
                    cd = cden[:, 8 * b:8 * b + 8].rearrange("p (e g) -> p e g", e=2)
                    sums = HT[:, b, D:D + P].rearrange("p (g e) -> p e g", g=4)[:, 0:2, :]
                    link(dve.scalar_tensor_tensor(cd, sums, -1.0,
                                                  emT[:, 8 * b:8 * b + 8].rearrange("p (e g) -> p e g", e=2),
                                                  ALU.mult, ALU.max))
                    dve.tensor_tensor(cd, cd, sums, ALU.max)
                    sq_ok.wait(dve, it, b + 1)
                    dve.tensor_reduce(v32[:, 8 * b:8 * b + 8], sq[:, :].rearrange("p (h d) -> p h d", h=HEADS),
                                      AX_X, ALU.add).then_inc(hred_ok.h, 1)

                weigh_qk(0, 0)
                probs_ok.wait(dve, it, 1)
                link(dve.reciprocal(rinv[:, :], psums[:, :]))
                g_out(0)
                weigh_qk(0, 1)
                em_mm.wait(dve, it, 1)
                dve.tensor_copy(emT[:, :], GT[:, 0:32]).then_inc(emT_ok.h, 1)
                emT_ok.wait(dve, it, 1)
                x_loaded.wait(dve, it, 16)
                ln_stats(0, xin, link, it, None)
                o_out(0)
                rs0_ok[0].wait(dve, it, 1)
                score_mm.wait(dve, it, 1)
                px_mm.wait(dve, it, 2)
                ln_apply(0, xin, xn1, link)
                weigh_qk(1, 0)
                g_out(1)
                xb_ok.wait(dve, it, 1)
                xg_ok.wait(dve, it, 1)
                for b in range(G):
                    wv_mm.wait(dve, it, b // 2 + 1)
                    ins = dve.scalar_tensor_tensor(x2[:, b, :], TAB[b // 2][:, (b % 2) * D:(b % 2) * D + D],
                                                   rinv[:, b:b + 1], xb[:, b, :], ALU.mult, ALU.add)
                    ins.then_inc(x2_ok.h, 1)
                head_sums(0)
                weigh_qk(1, 1)
                x2_ok.wait(dve, it, G)
                ln_stats(1, x2, link, it, None)
                weigh_qk(2, 0)
                rs0_ok[1].wait(dve, it, 1)
                ln_apply(1, x2, xn2, link)
                weigh_qk(2, 1)
                head_sums(1)
                o_out(1)
                weigh_qk(3, 0)
                head_sums(2)
                weigh_qk(3, 1)
                g_out(2)
                head_sums(3)
                hred_ok.wait(dve, it, G)
                link(dve.tensor_scalar(cden[:, :], cden[:, :], TAU * 1e-6, CLAMP, ALU.add, ALU.min))
                link(dve.scalar_tensor_tensor(cden[:, :], cden[:, :], EPS, cden[:, :], ALU.mult, ALU.mult))
                dve.scalar_tensor_tensor(harg[:, :], v32[:, :], 1.0 / HD, cden[:, :], ALU.mult, ALU.add)\
                   .then_inc(harg_ok.h, 1)
                o_out(2)
                g_out(3)
                hrs0_ok.wait(dve, it, 1)
                link(dve.tensor_tensor(hrs[:, :], hrs0[:, :], hrs0[:, :], ALU.mult))
                link(dve.tensor_tensor(hrs[:, :], hrs[:, :], harg[:, :], ALU.mult))
                link(dve.tensor_scalar(hrs[:, :], hrs[:, :], -0.5, 1.5, ALU.mult, ALU.add))
                link(dve.tensor_tensor(hrs[:, :], hrs[:, :], hrs0[:, :], ALU.mult))
                ng_ok.wait(dve, it, G)
                xf_ok.wait(dve, it, 1)
                link(dve.tensor_tensor(x3[:, :, :].rearrange("p b (h d) -> p (b h) d", h=HEADS),
                                       Ng[:, :, :].rearrange("p b (h d) -> p (b h) d", h=HEADS),
                                       hrs[:, :].unsqueeze(2).broadcast_to([P, G * HEADS, HD]), ALU.mult))
                dve.tensor_tensor(x3[:, :, :], x3[:, :, :], xg[:, :, :], ALU.add).then_inc(x3_ok.h, 1)
                o_out(3)
                v.end()

        @block.tensor
        def _(pe):
            def transposes(src, it, mm, waits):
                for c in range(KD):
                    for w, k in waits:
                        w.wait(pe, it, k)
                    for b in range(G):
                        ins = pe.transpose(TAB[c][:, b * S:(b + 1) * S], src[:, b, c * P:(c + 1) * P], ident[:, :])
                    ins.then_inc(mm.h, 1)

            pe.wait_ge(s_zero, 1)
            pe.wait_ge(s_load, 16 * LOADS)
            for w in range(3):
                if w == 2:
                    pe.wait_ge(s_set_v, V_WT)
                for ec in range(KD):
                    for kd in range(KD):
                        ins = pe.transpose(TAB[w % 2][:, ec * D + kd * P:ec * D + kd * P + P],
                                           wn[:, kd, w * D + ec * P:w * D + ec * P + P], ident[:, :])
                ins.then_inc(s_set_pe, 1)
            pe.wait_ge(s_set_v, V_WT + 2)
            for k in range(KD):
                for ec in range(KD):
                    ins = pe.matmul(UAB[k][:, 0:D], wT[:, 0, ec, k * P:(k + 1) * P], wT[:, 1, ec, :],
                                    start=(ec == 0), stop=(ec == 1))
                ins.then_inc(s_set_pe, 1)
            for k in range(KD):
                pe.wait_ge(s_set_v, V_WT + 3 + k)
                for ec in range(KD):
                    ins = pe.matmul(UAB[k][:, 0:D], wT[:, 2, ec, k * P:(k + 1) * P], wp[:, ec, :],
                                    start=(ec == 0), stop=(ec == 1))
                ins.then_inc(s_set_pe, 1)
            for ec in range(KD):
                pe.matmul(DD[:, 0:D], bB[:, 0, ec, :], wT[:, 0, ec, :], start=(ec == 0), stop=(ec == 1))
            for ec in range(KD):
                pe.matmul(DD[:, D:2 * D], bB[:, 1, ec, :], wp[:, ec, :], start=(ec == 0), stop=(ec == 1))
            for m in range(KD):
                for ec in range(KD):
                    pe.matmul(QQ[:, m:m + 1], wT[:, 1, ec, m * P:(m + 1) * P], bcol[:, ec:ec + 1],
                              start=(ec == 0), stop=(ec == 1))
            for ec in range(KD):
                ins = pe.matmul(QQ[:, KD:KD + 1], bB[:, 0, ec, :], bcol[:, ec:ec + 1], start=(ec == 0), stop=(ec == 1))
            ins.then_inc(s_set_pe, 1)
            for k in range(4):
                src = wg3[0:16, k * P:(k + 1) * P] if k < 2 else wgn[0:16, (k - 2) * P:(k - 1) * P]
                ins = pe.transpose(PV[:, 16 * k:16 * k + 16], src, ident[0:16, 0:16])
            ins.then_inc(s_set_pe, 1)
            for i in range(4):
                pe.wait_ge(s_set_v, V_TAB + i)
                for q in range(4):
                    src = w1p[i][:, q * P:(q + 1) * P]
                    ins = pe.transpose(TAB[i % 2][:, q * P:(q + 1) * P], src, ident[:, :])
                ins.then_inc(s_set_pe, 1)
            for i in range(4):
                pe.wait_ge(s_set_v, V_TAB + 4 + i)
                for kk in range(2):
                    for oc in range(KD):
                        src = w2p[i][:, oc * D + kk * P:oc * D + kk * P + P]
                        ins = pe.transpose(TAB[i % 2][:, kk * D + oc * P:kk * D + oc * P + P], src, ident[:, :])
                ins.then_inc(s_set_pe, 1)
            pe.wait_ge(s_set_v, SETUP_V)

            with pe.Fori(0, STEPS) as it:
                transposes(xn1, it, xn1T_mm, [(xn_ok[0], 0), (x2_ok, 0)])
                ctx_loaded.wait(pe, it, 0)
                transposes(ctxn, it, ctxT_mm, [(xn1T_ok, 2)])
                xn_ok[1].wait(pe, it, 0)
                transposes(xn2, it, xn2T_mm, [(ctxT_ok, 2)])
                for m in range(KD):
                    xn2T_ok.wait(pe, it, m + 1)
                    for k in range(KD):
                        ins = pe.matmul(TAB[m][:, :], A_w[:, k, m * P:(m + 1) * P], xn1T[:, k, :],
                                        start=(k == 0), stop=(k == 1))
                    ins.then_inc(qT_mm.h, 1)
                gsT_ok.wait(pe, it, 0)
                for k in range(4):
                    src = xn2T if k < 2 else ctxT
                    for b in range(G):
                        ins = pe.matmul(GT[32 * b:32 * b + 32, 0:S], WgT[:, k, :], src[:, k % 2, b * S:(b + 1) * S],
                                        start=(k == 0), stop=(k == 3))
                ins.then_inc(gate_mm.h, 1)
                xn_ok[2].wait(pe, it, 1)
                transposes(xn3, it, xn3T_mm, [(qT_ok, 2)])
                xn3T_ok.wait(pe, it, 2)
                gate_ok.wait(pe, it, 1)
                for k in range(KD):
                    for b in range(G):
                        ins = pe.matmul(GT[32 * b:32 * b + 32, 0:S], xn3T[:, k, b * S + 2:b * S + 66:2],
                                        xn3T[:, k, b * S:(b + 1) * S], start=(k == 0), stop=(k == 1))
                ins.then_inc(gram_mm.h, 1)
                for b in range(G):
                    for k in range(KD):
                        ins = pe.matmul(TAB[0][:, b * S:(b + 1) * S], qT[:, k, b * S:(b + 1) * S],
                                        xn1T[:, k, b * S:(b + 1) * S], start=(k == 0), stop=(k == 1))
                ins.then_inc(score_mm.h, 1)

                def up(hc):
                    if hc == 0:
                        c_ok.wait(pe, it, 0)
                    elif hc == 1:
                        dexp_ok.wait(pe, it, 0)
                    elif hc == 2:
                        ot_ok.wait(pe, it, 0)
                    elif hc >= 4:
                        h_ok.wait(pe, it, hc - 3)
                    for k in range(KD):
                        pe.matmul(UP[hc % 4][:, :], W1T[:, k, hc * P:(hc + 1) * P], xn3T[:, k, :],
                                  start=(k == 0), stop=False)

                def up_adapter(hc):
                    if hc == 0:
                        e_loaded.wait(pe, it, R * 16)
                        t_loaded.wait(pe, it, G * 16)
                    pe.matmul(UP[hc % 4][:, :], Et[:, hc * P:(hc + 1) * P], Tt[:, :], start=False, stop=True)\
                      .then_inc(up_mm.h, 1)

                up(0)
                up(1)
                tg_ok.wait(pe, it, 1)
                csum_ok.wait(pe, it, 1)
                pe.matmul(GT[0:32, 0:P], sel_i[:, :], gate[:, :], start=True, stop=False)
                pe.matmul(GT[0:32, 0:P], sel_nf[:, :], csum[:, :], start=False, stop=True)
                pe.matmul(GT[0:32, P:2 * P], sel_f[:, :], csum[:, :], start=True, stop=True).then_inc(sel_mm.h, 1)
                up(2)
                up(3)
                up_adapter(0)
                up_adapter(1)
                for hc in range(4, KH):
                    up(hc)
                    up_adapter(hc - 2)
                up_adapter(KH - 2)
                up_adapter(KH - 1)

                def down(b):
                    fill_ok.wait(pe, it, b + 1)
                    if b < 2:
                        h_ok.wait(pe, it, KH)
                    else:
                        ot_ok.wait(pe, it, b - 1)
                    for k in range(KH):
                        ins = pe.matmul(UAB[b % 2][:, 0:WD], hT[:, k, b * S:(b + 1) * S], W2x[b % 2][:, k, :],
                                        start=(k == 0), stop=(k == KH - 1))
                    ins.then_inc(down_mm.h, 1)

                def turn_g(b, w, k):
                    w.wait(pe, it, k)
                    gs_ok.wait(pe, it, b + 1)
                    pe.transpose(GT[0:EXTRA, 0:S], gs[:, :], ident[:, :]).then_inc(gsT_mm.h, 1)

                def adapt(b):
                    gsT_ok.wait(pe, it, b + 1)
                    if b == 0:
                        ev_loaded.wait(pe, it, R * G * 16)
                    pe.matmul(UAB[b % 2][:, 0:D], gsT[:, :], Ev[:, b, :], start=False, stop=True,
                              skip_group_check=True).then_inc(adapt_mm.h, 1)

                def decay(b, hf):
                    k = 2 * b + hf
                    dexp_ok.wait(pe, it, k)
                    if k == 0:
                        parts_ok.wait(pe, it, 1)
                    h0 = HEADS * b + 4 * hf
                    pe.matmul(DD[:, :], parts[:, 0, :], pick[:, h0:h0 + 4, :], start=True, stop=True)
                    pe.matmul(DD[:, :], ident_h[:, :], later[:, :].unsqueeze(1).broadcast_to([P, 4, P]),
                              start=False, stop=True, skip_group_check=True)
                    for h in range(4):
                        ins = pe.matmul(DD[:, h * P:(h + 1) * P], pick[:, h0 + h, :], parts[:, 1, :],
                                        start=False, stop=True, skip_group_check=True)
                    ins.then_inc(d_mm.h, 1)

                def qk(b, hf):
                    c_ok.wait(pe, it, 2 * b + hf)
                    if b == 0 and hf == 0:
                        qpad_loaded.wait(pe, it, 8 * 16)
                    pe.matmul(QQ[:, :], ctxT[:, hf, b * S:(b + 1) * S], qpad[:, hf, :, b * S:(b + 1) * S],
                              start=True, stop=True).then_inc(qk_mm.h, 1)

                def pv(b):
                    HT_ok.wait(pe, it, b)
                    c_ok.wait(pe, it, 2 * b + 2)
                    if b == 0:
                        vc_ok.wait(pe, it, 1)
                    for h in range(HEADS):
                        q = 32 * (h % 4)
                        pe.matmul(PV[q:q + 32, 2 * P:3 * P], onehot[:, h, :], C[:, h, :],
                                  start=(h < 4), stop=(h >= 4))
                    for h in range(HEADS):
                        q = 32 * (h % 4)
                        ins = pe.matmul(PV[q:q + 32, (h // 4) * P:(h // 4 + 1) * P], vc[:, b, HD * h:HD * h + HD],
                                        C[:, h, :], start=True, stop=True)
                    ins.then_inc(pv_mm.h, 1)

                def turn_h(b):
                    HS_ok.wait(pe, it, b + 1)
                    for k in range(3):
                        ins = pe.transpose(PV[:, k * P:(k + 1) * P], HS[:, k * P:(k + 1) * P], ident[:, :])
                    ins.then_inc(ht_mm.h, 1)

                h_ok.wait(pe, it, 6)
                decay(0, 0)
                qk(0, 0)
                down(0)
                probs_ok.wait(pe, it, 1)
                for b in range(G):
                    ins = pe.transpose(TAB[1][:, b * S:(b + 1) * S], probs[:, b * S:(b + 1) * S], ident[:, :])
                ins.then_inc(PT_mm.h, 1)
                decay(0, 1)
                qk(0, 1)
                turn_g(0, acs_ok, 1)
                PT_ok.wait(pe, it, 1)
                sc_ok.wait(pe, it, 1)
                for m in range(KD):
                    for b in range(G):
                        ins = pe.matmul(TAB[m][:, b * S:(b + 1) * S], xn1[:, b, m * P:(m + 1) * P],
                                        PT[:, b * S:(b + 1) * S], start=True, stop=True)
                    ins.then_inc(px_mm.h, 1)
                em_ok.wait(pe, it, 1)
                gsT_ok.wait(pe, it, 1)
                pe.transpose(GT[:, 0:P], em[:, :], ident[:, :]).then_inc(em_mm.h, 1)
                adapt(0)
                decay(1, 0)
                pv(0)
                qk(1, 0)
                down(1)
                px_ok.wait(pe, it, 2)
                for b in range(G):
                    for k in range(KD):
                        ins = pe.matmul(TAB[b // 2][:, (b % 2) * D:(b % 2) * D + D], pxT[:, k, b * S:(b + 1) * S],
                                        Wvp[:, k, :], start=(k == 0), stop=(k == 1))
                    if b % 2 == 1:
                        ins.then_inc(wv_mm.h, 1)
                turn_h(0)
                decay(1, 1)
                qk(1, 1)
                turn_g(1, emT_ok, 1)
                decay(2, 0)
                pv(1)
                qk(2, 0)
                adapt(1)
                decay(2, 1)
                turn_h(1)
                qk(2, 1)
                decay(3, 0)
                pv(2)
                qk(3, 0)
                turn_h(2)
                decay(3, 1)
                qk(3, 1)
                down(2)
                pv(3)
                turn_g(2, gsT_ok, 2)
                turn_h(3)
                adapt(2)
                down(3)
                turn_g(3, gsT_ok, 3)
                adapt(3)


LOADS = 11 + 8 + 16 + 16
SETUP_V = 7 + 4 + 8 + 3 + 2 + 2 + 4 + 1 + 4 + 4 + 1
V_WT = 7 + 4 + 8 + 1
V_TAB = 7 + 4 + 8 + 3 + 2 + 2 + 4 + 1


def kernel(**inputs):
    import concourse.bacc as bacc
    from concourse.bass_utils import run_bass_kernel_spmd

    nc = bacc.Bacc("TRN2", target_bir_lowering=False, num_devices=1)
    names = ["x", "ctx_1024", "L0_attn_W_qkv", "L0_attn_b_qkv", "L0_attn_W_proj", "L0_attn_b_proj",
             "L0_xattn_Wi_w", "L0_xattn_Wi_b", "L0_xattn_Wf_w", "L0_xattn_Wf_b", "L0_xattn_gn_w",
             "L0_xattn_gn_b", "L0_ffn_W1", "L0_ffn_b1", "L0_ffn_W2", "L0_ffn_b2", "L0_ffn_scale"]
    arrays, args = {}, []
    for name in names:
        a = np.ascontiguousarray(inputs[name])
        if a.ndim == 0:
            a = a.reshape(1)
        arrays[name] = a
        args.append(nc.dram_tensor(name, a.shape, mybir.dt.from_np(a.dtype), kind="ExternalInput").ap())
    out = nc.dram_tensor("out", arrays["x"].shape, F32, kind="ExternalOutput").ap()
    build(nc, *args, out)
    r = run_bass_kernel_spmd(nc, [arrays], core_ids=[0])
    return r.results[0]["out"]
```

```python
from contextlib import ExitStack
import math

import numpy as np
import concourse.bass as bass
from concourse import mybir

F32 = mybir.dt.float32
BF16 = mybir.dt.bfloat16
F32R = mybir.dt.float32r
ACT = mybir.ActivationFunctionType
ALU = mybir.AluOpType
AX_X = mybir.AxisListType.X

P = 128
D = 256
S = 128
G = 4
N = G * S
KD = D // P
HID = 1024
KH = HID // P
HEADS = 8
HD = D // HEADS
R = 4
CB = 4
U = D // CB
EXTRA = CB * R
WD = D + EXTRA
EPS = 1e-5
SCALE = (D // 16) ** -0.5
TAU = math.sqrt(HD)
LN_TAU = math.log(TAU)
CLAMP = 1e12
BANDS = (-math.log(9.0), -math.log(3.0), math.log(17.0 / 3.0), math.log(19.0))
EXP_SET = "natural_log_exp_and_others"


class Counter:

    def __init__(self, handle, per, base=0):
        self.h, self.per, self.base = handle, per, base

    def wait(self, eng, it, k):
        eng.wait_ge(self.h, it * self.per + (self.base + k))


class Chain(Counter):

    def start(self, it):
        self.it, self.k = it, 0

    def link(self, eng, ins):
        self.k += 1
        ins.then_inc(self.h, 1)
        self.wait(eng, self.it, self.k)

    def end(self):
        assert self.k == self.per, (self.k, self.per)


def build(nc, x, ctx_in, W_qkv, b_qkv, W_proj, b_proj, Wi_w, Wi_b, Wf_w, Wf_b, gn_w, gn_b,
          W1, b1, W2, b2, scale, out):
    NG = x.shape[0] // G
    STEPS = NG + 2
    ctx = ExitStack()
    with ctx:
        def sb(name, shape, dt=F32):
            return ctx.enter_context(nc.sbuf_tensor(name, shape, dt))

        def sem(name):
            return ctx.enter_context(nc.semaphore(name))

        opened = []

        def per_step(name, per, base=None):
            c = Counter(sem(name), per, 1 if base is None else base)
            if base is None:
                opened.append(c)
            return c

        ident = sb("ident", [P, P])
        A_w = sb("A_w", [P, KD, D])
        Wvp = sb("Wvp", [P, KD, D])
        cq = sb("cq", [P, KD])
        wrow = sb("wrow", [P, D])
        c0 = sb("c0", [P, 1])
        cvp = sb("cvp", [P, D])
        gnw_b = sb("gnw_b", [P, D])
        gnb_b = sb("gnb_b", [P, D])
        b2_b = sb("b2_b", [P, D])
        sc_b = sb("sc_b", [P, 1])
        b1c = sb("b1c", [P, KH])
        WgT = sb("WgT", [P, 4, 32])
        gbias = sb("gbias", [P, 1])
        W1h = sb("W1h", [P, KD, HID], F32R)
        W1l = sb("W1l", [P, KD, HID], F32R)
        W2x = sb("W2x", [P, KH, WD])
        pick = sb("pick", [96, 32], BF16)
        ident_h = sb("ident_h", [P, P], BF16)
        later = sb("later", [P, P], BF16)
        onehot = sb("onehot", [P, HEADS, 32])
        sel_i = sb("sel_i", [P, 32])
        sel_f = sb("sel_f", [P, 32])
        sel_nf = sb("sel_nf", [P, 32])
        ones = sb("ones", [P, P])
        lntau = sb("lntau", [P, 1])
        xin = sb("xin", [P, G, D])
        xn1 = sb("xn1", [P, G, D])
        xn1T = sb("xn1T", [P, KD, N])
        qT = sb("qT", [P, KD, N])
        dots = sb("dots", [P, G, D])
        rowterm = sb("rowterm", [P, G])
        sc = sb("sc", [P, N])
        band_a = sb("band_a", [P, N])
        band_b = sb("band_b", [P, N])
        y = sb("y", [P, N])
        nmx = sb("nmx", [P, G])
        probs = sb("probs", [P, N])
        psums = sb("psums", [P, G])
        rinv = sb("rinv", [P, G])
        PT = sb("PT", [P, N])
        pxT = sb("pxT", [P, KD, N])
        x2 = sb("x2", [P, G, D])
        xn2 = sb("xn2", [P, G, D])
        xn2T = sb("xn2T", [P, KD, N])
        qpad = sb("qpad", [P, KD, 4, N])
        ctxn = sb("ctxn", [P, G, D])
        ctxT = sb("ctxT", [P, KD, N])
        hmean = sb("hmean", [P, G * HEADS])
        vc = sb("vc", [P, G, D])
        xg = sb("xg", [P, G, D])
        gate = sb("gate", [P, P])
        gabs = sb("gabs", [P, P])
        lsig = sb("lsig", [P, P])
        csum = sb("csum", [P, P])
        acs = sb("acs", [32, 2 * P])
        am = sb("am", [32, 2, P])
        amr = sb("amr", [32, 2, P])
        am2 = sb("am2", [32, 2, P], BF16)
        parts = sb("parts", [96, 2, P], BF16)
        em = sb("em", [P, P])
        emT = sb("emT", [P, 32])
        dx = [qT[:, i, :] for i in range(2)]
        C = sb("C", [P, HEADS, P])
        HS = sb("HS", [P, 3 * P])
        HT = sb("HT", [P, G, 3 * P])
        sq = sb("sq", [P, D])
        v32 = sb("v32", [P, G * HEADS])
        cden = sb("cden", [P, G * HEADS])
        harg = sb("harg", [P, G * HEADS])
        hrs0 = sb("hrs0", [P, G * HEADS])
        htmp = sb("htmp", [P, G * HEADS])
        hrs = sb("hrs", [P, G * HEADS])
        Ng = sb("Ng", [P, G, D])
        x3 = sb("x3", [P, G, D])
        xf = sb("xf", [P, G, D])
        xn3 = sb("xn3", [P, G, D])
        xn3T = sb("xn3T", [P, KD, N])
        xn3h = sb("xn3h", [P, KD, N], F32R)
        xn3l = sb("xn3l", [P, KD, N], F32R)
        Z = sb("Z", [P, KD, G, 32])
        Eraw = sb("Eraw", [G * R, HID])
        Et = sb("Et", [P, HID], F32R)
        Tt = sb("Tt", [P, N], F32R)
        Ev = sb("Ev", [P, G, D])
        gs = sb("gs", [P, EXTRA])
        gsT = sb("gsT", [P, S])
        hT = sb("hT", [P, KH, N])
        ot = sb("ot", [P, G, D])
        stat = [sb(f"stat{i}", [P, G, 6]) for i in range(3)]
        mean = [sb(f"mean{i}", [P, G]) for i in range(3)]
        half_gap = [sb(f"half_gap{i}", [P, G]) for i in range(3)]
        ve = [sb(f"ve{i}", [P, G]) for i in range(3)]
        lv = [sb(f"lv{i}", [P, G]) for i in range(3)]
        rs0 = [sb(f"rs0{i}", [P, G]) for i in range(3)]
        nt = [sb(f"nt{i}", [P, G]) for i in range(3)]
        rs = [sb(f"rs{i}", [P, G]) for i in range(3)]

        def bank(name):
            return ctx.enter_context(nc.psum_tensor(name, [P, 512], F32))

        TAB = [bank("TA"), bank("TB")]
        UAB = [bank("UA"), bank("UB")]
        DD = bank("DD")
        QQ = bank("QQ")
        PV = bank("PV")
        GT = bank("GT")

        UP = [PV, TAB[1]] + UAB

        w1n = hT[:, 0:4, :].rearrange("p a b -> p (a b)").rearrange("p (k d) -> p k d", k=KH)
        w2n = hT[:, 4:8, :].rearrange("p a b -> p (a b)").rearrange("p (k h) -> p k h", k=KD)
        stage = qpad[:, :, :, :].rearrange("p a b c -> p (a b c)")
        wn = stage[:, 0:1536].rearrange("p (k e) -> p k e", k=KD)
        wT = stage[:, 1536:3072].rearrange("p (w k d) -> p w k d", w=3, k=KD)
        wp = stage[:, 3072:3584].rearrange("p (k o) -> p k o", k=KD)
        bB = stage[:, 3584:4096].rearrange("p (w k n) -> p w k n", w=2, k=KD)
        bcol = sb("bcol", [P, 6])
        wgn = xn1T[:, 0, :].rearrange("p n -> p n")
        wg3 = xn2T[:, :, :].rearrange("p a b -> p (a b)")[0:16, 0:3 * D]
        bp_b = sc[:, 0:D]
        w1p = [t[:, 2 * j:2 * j + 2, :].rearrange("p a b -> p (a b)") for t in (Ng, ot) for j in range(2)]
        w2p = [C[:, 4 * j:4 * j + 4, :].rearrange("p a b -> p (a b)") for j in range(2)] + [pxT[:, j, :] for j in range(2)]

        s_load = sem("weights_loaded")
        s_zero = sem("zeroed")
        s_idz = sem("ident_step")
        s_set_pe = sem("setup_pe")
        s_set_v = sem("setup_dve")
        s_pre_a = sem("first_log")

        x_loaded = per_step("x_loaded", 16, 16)
        ctx_loaded = per_step("ctx_loaded", 16, 16)
        qpad_loaded = per_step("qpad_loaded", 8 * 16)
        e_loaded = per_step("e_loaded", R * 16)
        ev_loaded = per_step("ev_loaded", R * G * 16)
        stored = per_step("stored", 16)
        xn1T_mm = per_step("xn1T_mm", 2, 2)
        ctxT_mm = per_step("ctxT_mm", 2, 2)
        xn2T_mm = per_step("xn2T_mm", 2, 2)
        qT_mm = per_step("qT_mm", 2, 2)
        gate_mm = per_step("gate_mm", 1)
        xn3T_mm = per_step("xn3T_mm", 2)
        score_mm = per_step("score_mm", 1)
        gram_mm = per_step("gram_mm", 1)
        up_mm = per_step("up_mm", KH)
        sel_mm = per_step("sel_mm", 1)
        PT_mm = per_step("PT_mm", 1)
        px_mm = per_step("px_mm", 2)
        wv_mm = per_step("wv_mm", 2)
        em_mm = per_step("em_mm", 1)
        d_mm = per_step("d_mm", 2 * G)
        qk_mm = per_step("qk_mm", 2 * G)
        pv_mm = per_step("pv_mm", G)
        ht_mm = per_step("ht_mm", G)
        down_mm = per_step("down_mm", G)
        gsT_mm = per_step("gsT_mm", G)
        adapt_mm = per_step("adapt_mm", G)
        xn1T_ok = per_step("xn1T_ok", 2, 2)
        ctxT_ok = per_step("ctxT_ok", 2, 2)
        xn2T_ok = per_step("xn2T_ok", 2, 2)
        qT_ok = per_step("qT_ok", 2, 2)
        xn3T_ok = per_step("xn3T_ok", 2)
        xn3h_ok = per_step("xn3h_ok", 2)
        sc_ok = per_step("sc_ok", 1)
        h_ok = per_step("h_ok", KH)
        lnsig_ok = per_step("lnsig_ok", 1)
        adapter_ok = per_step("adapter_ok", 1)
        probs_ok = per_step("probs_ok", 1)
        PT_ok = per_step("PT_ok", 1)
        px_ok = per_step("px_ok", 2)
        em_ok = per_step("em_ok", 1)
        dexp_ok = per_step("dexp_ok", 2 * G)
        HS_ok = per_step("HS_ok", G)
        HT_ok = per_step("HT_ok", G)
        sq_ok = per_step("sq_ok", G)
        gsT_ok = per_step("gsT_ok", G)
        hrs0_ok = per_step("hrs0_ok", 1)
        rs0_ok = [per_step("rs0_ok0", 1, 1), per_step("rs0_ok1", 1), per_step("rs0_ok2", 1)]
        ve_ok = [per_step("ve_ok0", 1, 1), per_step("ve_ok1", 1), per_step("ve_ok2", 1)]
        xn_ok = [per_step("xn1_ok", 1, 1), per_step("xn2_ok", 1), per_step("xn3_ok", 1)]
        rowterm_ok = per_step("rowterm_ok", 1, 1)
        hmean_ok = per_step("hmean_ok", 1, 1)
        gate_ok = per_step("gate_ok", 1)
        z_ok = per_step("z_ok", 1)
        xn3l_ok = per_step("xn3l_ok", 2)
        e_ok = per_step("e_ok", 2)
        t_ok = per_step("t_ok", 2)
        y_ok = per_step("y_ok", 1)
        csum_ok = per_step("csum_ok", 1)
        acs_ok = per_step("acs_ok", 1)
        parts_ok = per_step("parts_ok", 1)
        md_ok = per_step("md_ok", 1)
        emT_ok = per_step("emT_ok", 1)
        gs_ok = per_step("gs_ok", G)
        c_ok = per_step("c_ok", 2 * G)
        x2_ok = per_step("x2_ok", G)
        hred_ok = per_step("hred_ok", G)
        harg_ok = per_step("harg_ok", 1)
        x3_ok = per_step("x3_ok", 1)
        ot_ok = per_step("ot_ok", G)
        xb_ok = per_step("xb_ok", 1)
        vc_ok = per_step("vc_ok", 1)
        xg_ok = per_step("xg_ok", 1)
        xf_ok = per_step("xf_ok", 1)
        fill_ok = per_step("fill_ok", G)
        ng_ok = per_step("ng_ok", G)
        v_chain = Chain(sem("dve_step"), 48)
        a_chain = Chain(sem("act_step"), 6)

        x_g = x.rearrange("(g b) s d -> g s b d", b=G)
        c_g = ctx_in.rearrange("(g b) s d -> g s b d", b=G)
        o_g = out.rearrange("(g b) s d -> g s b d", b=G)
        row = lambda a: a.rearrange("(o n) -> o n", o=1).broadcast_to([P, a.shape[0]])

        block = ctx.enter_context(nc.Block())

        @block.sync
        def _(sp):
            sp.wait_ge(s_zero, 1)
            for dst, src in (
                [(wn, W_qkv.rearrange("(k p) e -> p k e", p=P)),
                 (wp, W_proj.rearrange("(k p) o -> p k o", p=P)),
                 (bcol[:, :], b_qkv.rearrange("(n p) -> p n", p=P)),
                 (bp_b, row(b_proj)), (gnw_b[:, :], row(gn_w)), (gnb_b[:, :], row(gn_b)),
                 (b2_b[:, :], row(b2)), (sc_b[:, :], row(scale)),
                 (wg3[0:8, :], Wi_w), (wg3[8:16, :], Wf_w),
                 (w2n, W2.rearrange("(k p) h -> p k h", p=P))]
                + [(gbias[32 * b + 8 * t:32 * b + 8 * t + 8, 0:1], w.rearrange("(n o) -> n o", o=1))
                   for b in range(G) for t, w in enumerate((Wi_b, Wf_b))]
                + [(w1n[64 * (c % 2):64 * (c % 2) + 64, 2 * r + c // 2, :],
                    W1.rearrange("(r u c) d -> r c u d", r=R, c=CB)[r, c]) for r in range(R) for c in range(CB)]
                + [(b1c[64 * (c % 2):64 * (c % 2) + 64, 2 * r + c // 2:2 * r + c // 2 + 1],
                    b1.rearrange("(r u c o) -> r c u o", r=R, c=CB, o=1)[r, c]) for r in range(R) for c in range(CB)]
            ):
                sp.dma_start(dst, src, allow_slow_non_contiguous=True).then_inc(s_load, 16)
            sp.dma_start(xin[:, :, :], x_g[0]).then_inc(x_loaded.h, 16)
            sp.dma_start(ctxn[:, :, :], c_g[0]).then_inc(ctx_loaded.h, 16)
            sp.wait_ge(s_set_v, SETUP_V)

            def step(it, nxt, cur, f):
                def q_rows(c):
                    for r in range(4):
                        sp.dma_start(qpad[32 * r:32 * r + 32, c, r, :], xn2T[32 * r:32 * r + 32, c, :])\
                          .then_inc(qpad_loaded.h, 16)

                xn_ok[2].wait(sp, it, 0)
                adapter_ok.wait(sp, it, 0)
                for r in range(R):
                    sp.dma_start(Eraw[r::R, r * D:(r + 1) * D], xn3[1 + 2 * r:2 + 2 * r, :, :])\
                      .then_inc(e_loaded.h, 16)
                qk_mm.wait(sp, it, 0)
                xn2T_ok.wait(sp, it, 0)
                q_rows(0)
                q_rows(1)
                adapt_mm.wait(sp, it, 0)
                for r in range(R):
                    for b in range(G):
                        sp.dma_start(Ev[r:R * CB:R, b, r * U:(r + 1) * U],
                                     xn3[9 + 2 * r:10 + 2 * r, b, :].rearrange("o (c u) -> o c u", c=CB))\
                          .then_inc(ev_loaded.h, 16)
                xb_ok.wait(sp, it, 1)
                xn_ok[0].wait(sp, it, 0)
                sp.dma_start(xin[:, :, :], x_g[nxt]).then_inc(x_loaded.h, 16)
                ctxT_mm.wait(sp, it, 0)
                vc_ok.wait(sp, it, 1)
                sp.dma_start(ctxn[:, :, :], c_g[cur]).then_inc(ctx_loaded.h, 16)
                ot_ok.wait(sp, it, G)
                sp.dma_start(o_g[f], ot[:, :, :]).then_inc(stored.h, 16)

            for it in range(2):
                step(it, min(it + 1, NG - 1), it, 0)
            with sp.Fori(2, NG - 1) as it:
                step(it, it + 1, it, it - 2)
            for it in range(NG - 1, STEPS):
                step(it, NG - 1, min(it, NG - 1), it - 2)
            x_loaded.wait(sp, STEPS, 0)
            ctx_loaded.wait(sp, STEPS, 0)
            stored.wait(sp, STEPS, 0)

        @block.gpsimd
        def _(pool):
            for c in opened:
                pool.sem_inc(c.h, 1)
            for t in (x2, xn2, x3, xn3, ctxT, Z, Tt, Eraw, Et, Ev, gsT, em, W2x, WgT, gbias):
                flat = t[tuple([slice(None)] * len(t.shape))]
                last = pool.memset(flat.bitcast(F32) if t in (Et, Tt) else flat, 0.0)
            last.then_inc(s_idz, 1)
            pool.memset(ident[:, :], 0.0)
            pool.memset(sel_i[:, :], 0.0)
            pool.memset(ident_h[:, :], 0.0)
            pool.memset(later[:, :], 0.0)
            pool.memset(sel_f[:, :], 0.0)
            pool.memset(sel_nf[:, :], 0.0)
            pool.memset(pick[:, :], 0.0)
            pool.memset(onehot[:, :, :], 0.0).then_inc(s_idz, 1)
            pool.wait_ge(s_idz, 2)
            pool.affine_select(out=ident[:, :], in_=ident[:, :], compare_op=ALU.not_equal, fill=1.0,
                               base=0, pattern=[[-1, P]], channel_multiplier=1)
            for t, base, val in ((sel_i, 0, 1.0), (sel_f, -8, 1.0), (sel_nf, -8, -1.0)):
                v = t[:, :].rearrange("p (b h) -> p b h", b=G)
                pool.affine_select(out=v, in_=v, compare_op=ALU.not_equal, fill=val, base=base,
                                   pattern=[[-32, G], [-1, 8]], channel_multiplier=1)
            pool.affine_select(out=pick[0:32, :], in_=pick[0:32, :], compare_op=ALU.not_equal, fill=1.0,
                               base=0, pattern=[[-1, 32]], channel_multiplier=1)
            pool.affine_select(out=ident_h[:, :], in_=ident_h[:, :], compare_op=ALU.not_equal, fill=1.0,
                               base=0, pattern=[[-1, P]], channel_multiplier=1)
            pool.affine_select(out=later[:, :], in_=later[:, :], compare_op=ALU.is_ge, fill=-1e30,
                               base=0, pattern=[[1, P]], channel_multiplier=-1)
            pool.memset(onehot[:, 0:4, 0:1], 1.0)
            pool.memset(onehot[:, 4:8, 1:2], 1.0)
            pool.memset(ones[:, :], 1.0)
            pool.memset(lntau[:, :], LN_TAU).then_inc(s_zero, 1)

            pool.wait_ge(s_load, 16 * LOADS)
            pool.wait_ge(s_set_v, SETUP_V)

            def fill(it, b):
                if b == 0:
                    xn3T_ok.wait(pool, it, 2)
                down_mm.wait(pool, it, b)
                for c in range(CB):
                    tokens = xn3T[:, :, b * S + 10:b * S + 10 + 2 * R:2]
                    ins = pool.tensor_tensor(W2x[:, 2 * c:2 * c + 2, D + R * c:D + R * c + R], tokens,
                                             ones[:, 0:2 * R].rearrange("p (k r) -> p k r", k=2), ALU.mult)
                ins.then_inc(fill_ok.h, 1)

            with pool.Fori(0, STEPS) as it:
                x2_ok.wait(pool, it, 0)
                x3_ok.wait(pool, it, 0)
                pool.tensor_tensor(xg[:, :, :], x2[:, :, :], gnb_b[:, :].unsqueeze(1).broadcast_to([P, G, D]),
                                   ALU.add).then_inc(xg_ok.h, 1)
                x_loaded.wait(pool, it, 0)
                xn_ok[1].wait(pool, it, 0)
                xg_ok.wait(pool, it, 1)
                pool.tensor_tensor(x2[:, :, :], xin[:, :, :], cvp[:, :].unsqueeze(1).broadcast_to([P, G, D]),
                                   ALU.add).then_inc(xb_ok.h, 1)
                hmean_ok.wait(pool, it, 0)
                pv_mm.wait(pool, it, 0)
                pool.tensor_tensor(vc[:, :, :].rearrange("p b (h d) -> p (b h) d", h=HEADS),
                                   ctxn[:, :, :].rearrange("p b (h d) -> p (b h) d", h=HEADS),
                                   hmean[:, :].unsqueeze(2).broadcast_to([P, G * HEADS, HD]),
                                   ALU.subtract).then_inc(vc_ok.h, 1)
                ot_ok.wait(pool, it, 0)
                pool.tensor_tensor(xf[:, :, :], x3[:, :, :], b2_b[:, :].unsqueeze(1).broadcast_to([P, G, D]),
                                   ALU.add).then_inc(xf_ok.h, 1)
                fill(it, 0)
                fill(it, 1)

                def weigh(b):
                    HT_ok.wait(pool, it, b + 1)
                    pool.tensor_tensor(Ng[:, b, :], HT[:, b, 0:D], gnw_b[:, :], ALU.mult).then_inc(ng_ok.h, 1)

                fill(it, 2)
                weigh(0)
                weigh(1)
                weigh(2)
                fill(it, 3)
                weigh(3)

        @block.scalar
        def _(act):
            a = a_chain

            def ln_root(i, it):
                ve_ok[i].wait(act, it, 1)
                a.link(act, act.activation(lv[i][:, :], ve[i][:, :], ACT.Ln))
                act.activation(rs0[i][:, :], lv[i][:, :], ACT.Exp, scale=-0.5).then_inc(rs0_ok[i].h, 1)

            act.preload_act_table_set(EXP_SET)
            act.wait_ge(ve_ok[0].h, 1)
            act.activation(lv[0][:, :], ve[0][:, :], ACT.Ln).then_inc(s_pre_a, 1)
            act.wait_ge(s_pre_a, 1)
            act.activation(rs0[0][:, :], lv[0][:, :], ACT.Exp, scale=-0.5).then_inc(rs0_ok[0].h, 1)
            act.wait_ge(s_set_v, SETUP_V)

            def evac(it, mm, ok, banks, dst, free):
                for c in range(KD):
                    mm.wait(act, it, c + 1)
                    if c == 0:
                        for f in free:
                            f.wait(act, it, f.per)
                    act.activation(dst[:, c, :], banks[c][:, :], ACT.Copy).then_inc(ok.h, 1)

            def evac_xn1T(it):
                evac(it, xn1T_mm, xn1T_ok, TAB, xn1T, [score_mm])

            def evac_xn2T(it):
                evac(it, xn2T_mm, xn2T_ok, TAB, xn2T, [gate_mm, qpad_loaded])

            def evac_ctxT(it):
                evac(it, ctxT_mm, ctxT_ok, [QQ, DD], ctxT, [qk_mm])

            def evac_qT(it, m):
                qT_mm.wait(act, it, m + 1)
                score_mm.wait(act, it, 1)
                c_ok.wait(act, it, 2 * G)
                act.activation(qT[:, m, :], TAB[m][:, :], ACT.Identity, bias=cq[:, m:m + 1]).then_inc(qT_ok.h, 1)

            evac_xn1T(-1)
            evac_xn2T(-1)
            evac_ctxT(-1)
            evac_qT(-1, 0)
            evac_qT(-1, 1)

            with act.Fori(0, STEPS) as it:
                a.start(it)
                for c in range(KD):
                    xn3T_mm.wait(act, it, c + 1)
                    if c == 0:
                        down_mm.wait(act, it, 0)
                    act.activation(xn3T[:, c, :], (QQ, DD)[c][:, :], ACT.Copy).then_inc(xn3T_ok.h, 1)
                    act.activation(xn3h[:, c, :], (QQ, DD)[c][:, :], ACT.Copy).then_inc(xn3h_ok.h, 1)
                score_mm.wait(act, it, 1)
                rowterm_ok.wait(act, it, 0)
                for b in range(G):
                    ins = act.activation(sc[:, b * S:(b + 1) * S], TAB[0][:, b * S:(b + 1) * S], ACT.Identity,
                                         bias=rowterm[:, b:b + 1], scale=SCALE)
                ins.then_inc(sc_ok.h, 1)
                gate_ok.wait(act, it, 1)
                a.link(act, act.activation(gabs[:, :], gate[:, :], ACT.Abs))
                a.link(act, act.activation(lsig[:, :], gabs[:, :], ACT.Exp, scale=-1.0))
                act.activation(gabs[:, :], lsig[:, :], ACT.Ln, bias=1.0).then_inc(lnsig_ok.h, 1)
                act.preload_act_table(ACT.Gelu)
                e_ok.wait(act, it, 1)
                act.activation(Et[64:80, :], Et[0:16, :].bitcast(F32), ACT.Copy)
                e_ok.wait(act, it, 2)
                act.activation(Et[96:112, :], Et[32:48, :].bitcast(F32), ACT.Copy)
                t_ok.wait(act, it, 1)
                act.activation(Tt[32:48, :], Tt[0:16, :].bitcast(F32), ACT.Copy)
                t_ok.wait(act, it, 2)
                act.activation(Tt[96:112, :], Tt[64:80, :].bitcast(F32), ACT.Copy).then_inc(adapter_ok.h, 1)
                for hc in range(KH):
                    up_mm.wait(act, it, hc + 1)
                    act.activation(hT[:, hc, :], UP[hc % 4][:, :], ACT.Gelu, bias=b1c[:, hc:hc + 1])\
                        .then_inc(h_ok.h, 1)

                act.preload_act_table_set(EXP_SET)

                def gsT_copy(b):
                    gsT_mm.wait(act, it, b + 1)
                    act.activation(gsT[0:EXTRA, :], GT[0:EXTRA, 0:S], ACT.Copy).then_inc(gsT_ok.h, 1)

                def dexp(b, hf):
                    d_mm.wait(act, it, 2 * b + hf + 1)
                    c_ok.wait(act, it, 2 * b + hf - 1) if 2 * b + hf >= 1 else c_ok.wait(act, it, 0)
                    act.activation(dx[hf], DD[:, :], ACT.Exp)\
                        .then_inc(dexp_ok.h, 1)

                def hs(b):
                    pv_mm.wait(act, it, b + 1)
                    act.activation(HS[:, :], PV[:, 0:3 * P], ACT.Copy).then_inc(HS_ok.h, 1)

                def ht(b):
                    ht_mm.wait(act, it, b + 1)
                    if b == 0:
                        x3_ok.wait(act, it, 0)
                    act.activation(HT[:, b, :], PV[:, 0:3 * P], ACT.Copy).then_inc(HT_ok.h, 1)
                    HT_ok.wait(act, it, b + 1)
                    hred_ok.wait(act, it, b)
                    act.activation(sq[:, :], HT[:, b, 0:D], ACT.Square).then_inc(sq_ok.h, 1)

                dexp(0, 0)
                y_ok.wait(act, it, 1)
                for b in range(G):
                    ins = act.activation(probs[:, b * S:(b + 1) * S], y[:, b * S:(b + 1) * S], ACT.Exp,
                                         bias=nmx[:, b:b + 1], accum_out=psums[:, b:b + 1])
                ins.then_inc(probs_ok.h, 1)
                md_ok.wait(act, it, 1)
                act.activation(em[0:32, :], em[0:32, :], ACT.Exp, scale=-1.0, bias=lntau[0:32, :]).then_inc(em_ok.h, 1)
                PT_mm.wait(act, it, 1)
                act.activation(PT[:, :], TAB[1][:, :], ACT.Copy).then_inc(PT_ok.h, 1)
                dexp(0, 1)
                gsT_copy(0)
                for m in range(KD):
                    px_mm.wait(act, it, m + 1)
                    act.activation(pxT[:, m, :], TAB[m][:, :], ACT.Copy).then_inc(px_ok.h, 1)
                ln_root(0, it)
                dexp(1, 0)
                hs(0)
                ht(0)
                dexp(1, 1)
                gsT_copy(1)
                dexp(2, 0)
                ln_root(1, it)
                hs(1)
                dexp(2, 1)
                ht(1)
                dexp(3, 0)
                hs(2)
                ht(2)
                dexp(3, 1)
                evac_xn1T(it)
                hs(3)
                evac_xn2T(it)
                ht(3)
                harg_ok.wait(act, it, 1)
                a.link(act, act.activation(htmp[:, :], harg[:, :], ACT.Ln))
                act.activation(hrs0[:, :], htmp[:, :], ACT.Exp, scale=-0.5).then_inc(hrs0_ok.h, 1)
                evac_ctxT(it)
                gsT_copy(2)
                evac_qT(it, 0)
                gsT_copy(3)
                ln_root(2, it)
                evac_qT(it, 1)
                a.end()

        @block.vector
        def _(dve):
            v = v_chain
            setup = [0]

            def done(ins):
                setup[0] += 1
                ins.then_inc(s_set_v, 1)
                dve.wait_ge(s_set_v, setup[0])

            def ln_stats(i, X, link, between=None):
                for b in range(G):
                    ins = dve.bn_stats(stat[i][:, b, :], X[:, b, :])
                link(ins)
                if between:
                    between(G - 1)
                even, odd = stat[i][:, :, 0:3], stat[i][:, :, 3:6]
                dve.tensor_tensor(mean[i][:, :], even[:, :, 1], odd[:, :, 1], ALU.add)
                dve.tensor_tensor(half_gap[i][:, :], even[:, :, 1], odd[:, :, 1], ALU.subtract)
                link(dve.tensor_tensor(ve[i][:, :], even[:, :, 2], odd[:, :, 2], ALU.add))
                dve.tensor_scalar(mean[i][:, :], mean[i][:, :], 0.5, None, ALU.mult)
                dve.tensor_scalar(ve[i][:, :], ve[i][:, :], 1.0 / D, EPS, ALU.mult, ALU.add)
                link(dve.scalar_tensor_tensor(half_gap[i][:, :], half_gap[i][:, :], 0.25, half_gap[i][:, :],
                                              ALU.mult, ALU.mult))
                dve.tensor_tensor(ve[i][:, :], ve[i][:, :], half_gap[i][:, :], ALU.add).then_inc(ve_ok[i].h, 1)

            def ln_apply(i, X, Xn, link):
                link(dve.tensor_tensor(nt[i][:, :], rs0[i][:, :], rs0[i][:, :], ALU.mult))
                link(dve.tensor_tensor(nt[i][:, :], nt[i][:, :], ve[i][:, :], ALU.mult))
                link(dve.tensor_scalar(nt[i][:, :], nt[i][:, :], -0.5, 1.5, ALU.mult, ALU.add))
                link(dve.tensor_tensor(rs[i][:, :], nt[i][:, :], rs0[i][:, :], ALU.mult))
                for b in range(G):
                    src, dst = X[:, b, :], Xn[:, b, :]
                    if i == 2:
                        src = src.rearrange("p (u c) -> p c u", c=CB)
                        dst = dst.rearrange("p (c u) -> p c u", c=CB)
                    ins = dve.tensor_scalar(dst, src, mean[i][:, b:b + 1], rs[i][:, b:b + 1], ALU.subtract, ALU.mult)
                ins.then_inc(xn_ok[i].h, 1)

            dve.wait_ge(x_loaded.h, 16)
            ln_stats(0, xin, done)
            dve.wait_ge(rs0_ok[0].h, 1)
            ln_apply(0, xin, xn1, done)
            dve.wait_ge(s_zero, 1)
            dve.wait_ge(s_load, 16 * LOADS)
            done(dve.tensor_copy(pick[32:64, :], pick[0:32, :]))
            done(dve.tensor_copy(pick[64:96, :], pick[0:32, :]))
            done(dve.tensor_copy(bB, bcol[:, 2:6].rearrange("p (w k) -> p w k", w=2).unsqueeze(3)
                                 .broadcast_to([P, 2, KD, P])))
            done(dve.tensor_tensor(wgn[0:16, 0:D], wg3[:, D:2 * D], wg3[:, 2 * D:3 * D], ALU.add))
            for i in range(4):
                done(dve.tensor_copy(
                    w1p[i].rearrange("p (q c u) -> p q c u", q=4, c=2),
                    w1n[:, 4 * (i % 2):4 * (i % 2) + 4, :].rearrange("p q (u c) -> p q c u", c=CB)
                    [:, :, 2 * (i // 2):2 * (i // 2) + 2, :]))
                done(dve.tensor_copy(
                    w2p[i].rearrange("p (o c u) -> p o c u", o=KD, c=CB),
                    w2n[:, :, i * D:(i + 1) * D].rearrange("p o (u c) -> p o c u", c=CB)))
            n = 0
            for w in range(3):
                n += 1
                dve.wait_ge(s_set_pe, n)
                done(dve.tensor_copy(wT[:, w, :, :].rearrange("p k d -> p (k d)"), TAB[w % 2][:, :]))
            for k in range(KD):
                n += 1
                dve.wait_ge(s_set_pe, n)
                done(dve.tensor_copy(A_w[:, k, :], UAB[k][:, 0:D]))
            for k in range(KD):
                n += 1
                dve.wait_ge(s_set_pe, n)
                done(dve.tensor_copy(Wvp[:, k, :], UAB[k][:, 0:D]))
            n += 1
            dve.wait_ge(s_set_pe, n)
            done(dve.tensor_scalar(wrow[:, :], DD[:, 0:D], SCALE, None, ALU.mult))
            done(dve.tensor_tensor(cvp[:, :], DD[:, D:2 * D], bp_b, ALU.add))
            done(dve.tensor_copy(cq[:, :], QQ[:, 0:KD]))
            done(dve.tensor_scalar(c0[:, :], QQ[:, KD:KD + 1], SCALE, None, ALU.mult))
            n += 1
            dve.wait_ge(s_set_pe, n)
            done(dve.tensor_copy(WgT[:, :, 0:16], PV[:, 0:64].rearrange("p (k n) -> p k n", k=4)))
            for i in range(4):
                n += 1
                dve.wait_ge(s_set_pe, n)
                hi = W1h[:, i // 2, (i % 2) * 512:(i % 2) * 512 + 512]
                done(dve.tensor_copy(hi, TAB[i % 2][:, :]))
                done(dve.tensor_tensor(W1l[:, i // 2, (i % 2) * 512:(i % 2) * 512 + 512], TAB[i % 2][:, :],
                                       hi.bitcast(F32), ALU.subtract))
            for i in range(4):
                n += 1
                dve.wait_ge(s_set_pe, n)
                src = TAB[i % 2][:, :].rearrange("p (k o) -> p k o", k=2)
                done(dve.tensor_copy(W2x[:, 2 * i:2 * i + 2, 0:D], src))
            done(dve.memset(stage, 0.0))

            def value_means(it, link):
                ctx_loaded.wait(dve, it, 16)
                vc_ok.wait(dve, it, 1)
                link(dve.tensor_reduce(hmean[:, :], ctxn[:, :, :].rearrange("p b (h d) -> p (b h) d", h=HEADS),
                                       AX_X, ALU.add))
                dve.tensor_scalar(hmean[:, :], hmean[:, :], 1.0 / HD, None, ALU.mult).then_inc(hmean_ok.h, 1)

            def row_terms(it, link):
                sc_ok.wait(dve, it, 1)
                for b in range(G):
                    ins = dve.tensor_tensor_reduce(dots[:, b, :], xn1[:, b, :], wrow[:, :], 1.0, 0.0, ALU.mult, ALU.add,
                                                   rowterm[:, b:b + 1])
                link(ins)
                dve.tensor_scalar(rowterm[:, :], rowterm[:, :], c0[:, 0:1], None, ALU.add).then_inc(rowterm_ok.h, 1)

            value_means(-1, done)
            row_terms(-1, done)
            assert setup[0] == SETUP_V, setup[0]

            with dve.Fori(0, STEPS) as it:
                v.start(it)
                link = lambda ins: v.link(dve, ins)
                gate_mm.wait(dve, it, 1)
                dve.tensor_scalar(gate[:, :], GT[:, 0:P], gbias[:, 0:1], None, ALU.add).then_inc(gate_ok.h, 1)
                xn3T_ok.wait(dve, it, 2)
                for b in range(G):
                    ins = dve.tensor_copy(Z[:, :, b, R * b:R * b + R],
                                          xn3T[:, :, b * S + 2:b * S + 2 + 2 * R:2])
                ins.then_inc(z_ok.h, 1)
                for c in range(KD):
                    xn3h_ok.wait(dve, it, c + 1)
                    dve.tensor_tensor(xn3l[:, c, :], xn3T[:, c, :], xn3h[:, c, :].bitcast(F32), ALU.subtract)\
                       .then_inc(xn3l_ok.h, 1)
                e_loaded.wait(dve, it, R * 16)
                up_mm.wait(dve, it, 0)
                dve.tensor_copy(Et[0:16, :], Eraw[:, :]).then_inc(e_ok.h, 1)
                e_ok.wait(dve, it, 1)
                dve.tensor_tensor(Et[32:48, :], Eraw[:, :], Et[0:16, :].bitcast(F32), ALU.subtract)\
                   .then_inc(e_ok.h, 1)
                gram_mm.wait(dve, it, 1)
                dve.tensor_scalar(Tt[0:16, :], GT[0:16, :], sc_b[0:16, 0:1], None, ALU.mult).then_inc(t_ok.h, 1)
                t_ok.wait(dve, it, 1)
                dve.scalar_tensor_tensor(Tt[64:80, :], GT[0:16, :], sc_b[0:16, 0:1], Tt[0:16, :].bitcast(F32),
                                         ALU.mult, ALU.subtract).then_inc(t_ok.h, 1)
                lnsig_ok.wait(dve, it, 1)
                link(dve.scalar_tensor_tensor(lsig[:, :], gate[:, :], 0.0, gabs[:, :], ALU.min, ALU.subtract))
                dve.tensor_tensor_scan(csum[:, :], ones[:, :], lsig[:, :], 0.0, ALU.mult, ALU.add)\
                   .then_inc(csum_ok.h, 1)
                sc_ok.wait(dve, it, 1)
                link(dve.tensor_scalar(band_a[:, :], sc[:, :], BANDS[0], 0.3, ALU.is_ge, ALU.mult))
                dve.tensor_scalar(band_b[:, :], sc[:, :], BANDS[3], None, ALU.is_gt)
                link(dve.scalar_tensor_tensor(band_a[:, :], sc[:, :], BANDS[1], band_a[:, :], ALU.is_ge, ALU.max))
                link(dve.scalar_tensor_tensor(band_b[:, :], sc[:, :], BANDS[2], band_b[:, :], ALU.is_gt, ALU.add))
                link(dve.scalar_tensor_tensor(band_a[:, :], band_b[:, :], 0.5, band_a[:, :], ALU.mult, ALU.add))
                link(dve.scalar_tensor_tensor(y[:, :], band_a[:, :], 0.1, sc[:, :], ALU.max, ALU.mult))
                link(dve.tensor_reduce(nmx[:, :], y[:, :].rearrange("p (b t) -> p b t", b=G), AX_X, ALU.max))
                dve.tensor_scalar(nmx[:, :], nmx[:, :], -1.0, None, ALU.mult).then_inc(y_ok.h, 1)
                sel_mm.wait(dve, it, 1)
                dve.tensor_copy(acs[:, :], GT[0:32, 0:2 * P]).then_inc(acs_ok.h, 1)
                acs_ok.wait(dve, it, 1)
                link(dve.tensor_tensor_scan(am[:, 1, :], acs[:, 0:P], acs[:, 0:P], -3e38, ALU.max, ALU.max))
                dve.tensor_copy(am[:, 0, :], acs[:, 0:P])
                em_mm.wait(dve, it, 0)
                link(dve.tensor_tensor(em[0:32, :], am[:, 1, :], acs[:, P:2 * P], ALU.add))
                dve.tensor_scalar(em[0:32, :], em[0:32, :], -25.0, None, ALU.max).then_inc(md_ok.h, 1)
                link(dve.tensor_scalar(am[:, 1, :], am[:, 1, :], -1.0, None, ALU.mult))
                d_mm.wait(dve, it, 0)
                link(dve.tensor_copy(parts[0:32, :, :], am[:, :, :]))
                link(dve.tensor_tensor(amr[:, :, :], am[:, :, :], parts[0:32, :, :], ALU.subtract))
                link(dve.tensor_copy(am2[:, :, :], amr[:, :, :]))
                dve.tensor_copy(parts[32:64, :, :], am2[:, :, :])
                dve.tensor_tensor(parts[64:96, :, :], amr[:, :, :], am2[:, :, :], ALU.subtract)\
                   .then_inc(parts_ok.h, 1)

                def g_out(b):
                    down_mm.wait(dve, it, b + 1)
                    gsT_mm.wait(dve, it, b)
                    dve.tensor_scalar(gs[:, :], UAB[b % 2][:, D:WD], sc_b[:, 0:1], None, ALU.mult)\
                        .then_inc(gs_ok.h, 1)

                def o_out(b):
                    adapt_mm.wait(dve, it, b + 1)
                    if b == 0:
                        stored.wait(dve, it, 0)
                        xf_ok.wait(dve, it, 1)
                    dve.tensor_tensor(ot[:, b, :], UAB[b % 2][:, 0:D], xf[:, b, :], ALU.add).then_inc(ot_ok.h, 1)

                def weigh_qk(b, hf):
                    k = 2 * b + hf
                    dexp_ok.wait(dve, it, k + 1)
                    qk_mm.wait(dve, it, k + 1)
                    pv_mm.wait(dve, it, b)
                    dve.tensor_tensor(C[:, 4 * hf:4 * hf + 4, :].rearrange("p h i -> p (h i)"),
                                      dx[hf], QQ[:, :], ALU.mult)\
                        .then_inc(c_ok.h, 1)

                def head_sums(b):
                    HT_ok.wait(dve, it, b + 1)
                    cd = cden[:, 8 * b:8 * b + 8].rearrange("p (e g) -> p e g", e=2)
                    sums = HT[:, b, D:D + P].rearrange("p (g e) -> p e g", g=4)[:, 0:2, :]
                    link(dve.scalar_tensor_tensor(cd, sums, -1.0,
                                                  emT[:, 8 * b:8 * b + 8].rearrange("p (e g) -> p e g", e=2),
                                                  ALU.mult, ALU.max))
                    dve.tensor_tensor(cd, cd, sums, ALU.max)
                    sq_ok.wait(dve, it, b + 1)
                    dve.tensor_reduce(v32[:, 8 * b:8 * b + 8], sq[:, :].rearrange("p (h d) -> p h d", h=HEADS),
                                      AX_X, ALU.add).then_inc(hred_ok.h, 1)

                weigh_qk(0, 0)
                probs_ok.wait(dve, it, 1)
                link(dve.reciprocal(rinv[:, :], psums[:, :]))
                g_out(0)
                weigh_qk(0, 1)
                em_mm.wait(dve, it, 1)
                dve.tensor_copy(emT[:, :], GT[:, 0:32]).then_inc(emT_ok.h, 1)
                emT_ok.wait(dve, it, 1)
                x_loaded.wait(dve, it, 16)
                ln_stats(0, xin, link)
                o_out(0)
                rs0_ok[0].wait(dve, it, 1)
                score_mm.wait(dve, it, 1)
                px_mm.wait(dve, it, 2)
                ln_apply(0, xin, xn1, link)
                weigh_qk(1, 0)
                g_out(1)
                xb_ok.wait(dve, it, 1)
                xg_ok.wait(dve, it, 1)
                for b in range(G):
                    wv_mm.wait(dve, it, b // 2 + 1)
                    ins = dve.scalar_tensor_tensor(x2[:, b, :], TAB[b // 2][:, (b % 2) * D:(b % 2) * D + D],
                                                   rinv[:, b:b + 1], x2[:, b, :], ALU.mult, ALU.add)
                    ins.then_inc(x2_ok.h, 1)
                head_sums(0)
                weigh_qk(1, 1)
                x2_ok.wait(dve, it, G)
                ln_stats(1, x2, link)
                weigh_qk(2, 0)
                weigh_qk(2, 1)
                head_sums(1)
                o_out(1)
                weigh_qk(3, 0)
                rs0_ok[1].wait(dve, it, 1)
                ln_apply(1, x2, xn2, link)
                head_sums(2)
                weigh_qk(3, 1)
                row_terms(it, link)
                value_means(it, link)
                head_sums(3)
                hred_ok.wait(dve, it, G)
                link(dve.tensor_scalar(cden[:, :], cden[:, :], TAU * 1e-6, CLAMP, ALU.add, ALU.min))
                link(dve.scalar_tensor_tensor(cden[:, :], cden[:, :], EPS, cden[:, :], ALU.mult, ALU.mult))
                dve.scalar_tensor_tensor(harg[:, :], v32[:, :], 1.0 / HD, cden[:, :], ALU.mult, ALU.add)\
                   .then_inc(harg_ok.h, 1)
                g_out(2)
                hrs0_ok.wait(dve, it, 1)
                link(dve.tensor_tensor(hrs[:, :], hrs0[:, :], hrs0[:, :], ALU.mult))
                link(dve.tensor_tensor(hrs[:, :], hrs[:, :], harg[:, :], ALU.mult))
                link(dve.tensor_scalar(hrs[:, :], hrs[:, :], -0.5, 1.5, ALU.mult, ALU.add))
                link(dve.tensor_tensor(hrs[:, :], hrs[:, :], hrs0[:, :], ALU.mult))
                ng_ok.wait(dve, it, G)
                xf_ok.wait(dve, it, 1)
                link(dve.tensor_tensor(x3[:, :, :].rearrange("p b (h d) -> p (b h) d", h=HEADS),
                                       Ng[:, :, :].rearrange("p b (h d) -> p (b h) d", h=HEADS),
                                       hrs[:, :].unsqueeze(2).broadcast_to([P, G * HEADS, HD]), ALU.mult))
                dve.tensor_tensor(x3[:, :, :], x3[:, :, :], xg[:, :, :], ALU.add).then_inc(x3_ok.h, 1)
                x3_ok.wait(dve, it, 1)
                ln_stats(2, x3, link, g_out)
                o_out(2)
                rs0_ok[2].wait(dve, it, 1)
                e_loaded.wait(dve, it, R * 16)
                ev_loaded.wait(dve, it, R * G * 16)
                ln_apply(2, x3, xn3, link)
                o_out(3)
                v.end()

        @block.tensor
        def _(pe):
            def transposes(it, src, banks, mm, waits):
                for w, k in waits:
                    w.wait(pe, it, k)
                for c in range(KD):
                    for b in range(G):
                        ins = pe.transpose(banks[c][:, b * S:(b + 1) * S], src[:, b, c * P:(c + 1) * P], ident[:, :])
                    ins.then_inc(mm.h, 1)

            def turn_xn1(it):
                transposes(it, xn1, TAB, xn1T_mm, [(xn_ok[0], 1), (x2_ok, G)])

            def turn_xn2(it):
                transposes(it, xn2, TAB, xn2T_mm, [(xn_ok[1], 1), (xn1T_ok, 2)])

            def turn_ctx(it):
                transposes(it, ctxn, [QQ, DD], ctxT_mm, [(ctx_loaded, 16), (dexp_ok, 2 * G), (c_ok, 2 * G)])

            def project_q(it, m):
                xn2T_ok.wait(pe, it, m + 1)
                for k in range(KD):
                    ins = pe.matmul(TAB[m][:, :], A_w[:, k, m * P:(m + 1) * P], xn1T[:, k, :],
                                    start=(k == 0), stop=(k == 1))
                ins.then_inc(qT_mm.h, 1)

            pe.wait_ge(s_zero, 1)
            pe.wait_ge(s_load, 16 * LOADS)
            for w in range(3):
                if w == 2:
                    pe.wait_ge(s_set_v, V_WT)
                for ec in range(KD):
                    for kd in range(KD):
                        ins = pe.transpose(TAB[w % 2][:, ec * D + kd * P:ec * D + kd * P + P],
                                           wn[:, kd, w * D + ec * P:w * D + ec * P + P], ident[:, :])
                ins.then_inc(s_set_pe, 1)
            pe.wait_ge(s_set_v, V_WT + 2)
            for k in range(KD):
                for ec in range(KD):
                    ins = pe.matmul(UAB[k][:, 0:D], wT[:, 0, ec, k * P:(k + 1) * P], wT[:, 1, ec, :],
                                    start=(ec == 0), stop=(ec == 1))
                ins.then_inc(s_set_pe, 1)
            for k in range(KD):
                pe.wait_ge(s_set_v, V_WT + 3 + k)
                for ec in range(KD):
                    ins = pe.matmul(UAB[k][:, 0:D], wT[:, 2, ec, k * P:(k + 1) * P], wp[:, ec, :],
                                    start=(ec == 0), stop=(ec == 1))
                ins.then_inc(s_set_pe, 1)
            for ec in range(KD):
                pe.matmul(DD[:, 0:D], bB[:, 0, ec, :], wT[:, 0, ec, :], start=(ec == 0), stop=(ec == 1))
            for ec in range(KD):
                pe.matmul(DD[:, D:2 * D], bB[:, 1, ec, :], wp[:, ec, :], start=(ec == 0), stop=(ec == 1))
            for m in range(KD):
                for ec in range(KD):
                    pe.matmul(QQ[:, m:m + 1], wT[:, 1, ec, m * P:(m + 1) * P], bcol[:, ec:ec + 1],
                              start=(ec == 0), stop=(ec == 1))
            for ec in range(KD):
                ins = pe.matmul(QQ[:, KD:KD + 1], bB[:, 0, ec, :], bcol[:, ec:ec + 1], start=(ec == 0), stop=(ec == 1))
            ins.then_inc(s_set_pe, 1)
            for k in range(4):
                src = wg3[0:16, k * P:(k + 1) * P] if k < 2 else wgn[0:16, (k - 2) * P:(k - 1) * P]
                ins = pe.transpose(PV[:, 16 * k:16 * k + 16], src, ident[0:16, 0:16])
            ins.then_inc(s_set_pe, 1)
            for i in range(4):
                pe.wait_ge(s_set_v, V_TAB + 2 * i)
                for q in range(4):
                    src = w1p[i][:, q * P:(q + 1) * P]
                    ins = pe.transpose(TAB[i % 2][:, q * P:(q + 1) * P], src, ident[:, :])
                ins.then_inc(s_set_pe, 1)
            for i in range(4):
                pe.wait_ge(s_set_v, V_TAB + 8 + i)
                for kk in range(2):
                    for oc in range(KD):
                        src = w2p[i][:, oc * D + kk * P:oc * D + kk * P + P]
                        ins = pe.transpose(TAB[i % 2][:, kk * D + oc * P:kk * D + oc * P + P], src, ident[:, :])
                ins.then_inc(s_set_pe, 1)
            pe.wait_ge(s_set_v, SETUP_V)

            turn_xn1(-1)
            turn_xn2(-1)
            turn_ctx(-1)
            project_q(-1, 0)
            project_q(-1, 1)

            with pe.Fori(0, STEPS) as it:
                gsT_ok.wait(pe, it, 0)
                xn2T_ok.wait(pe, it, 0)
                ctxT_ok.wait(pe, it, 0)
                for k in range(4):
                    src = xn2T if k < 2 else ctxT
                    for b in range(G):
                        ins = pe.matmul(GT[32 * b:32 * b + 32, 0:S], WgT[:, k, :], src[:, k % 2, b * S:(b + 1) * S],
                                        start=(k == 0), stop=(k == 3))
                ins.then_inc(gate_mm.h, 1)
                transposes(it, xn3, [QQ, DD], xn3T_mm, [(xn_ok[2], 0)])
                qT_ok.wait(pe, it, 0)
                for b in range(G):
                    for k in range(KD):
                        ins = pe.matmul(TAB[0][:, b * S:(b + 1) * S], qT[:, k, b * S:(b + 1) * S],
                                        xn1T[:, k, b * S:(b + 1) * S], start=(k == 0), stop=(k == 1))
                ins.then_inc(score_mm.h, 1)
                gate_ok.wait(pe, it, 1)
                z_ok.wait(pe, it, 1)
                for b in range(G):
                    for k in range(KD):
                        ins = pe.matmul(GT[0:32, b * S:(b + 1) * S], Z[:, k, b, :], xn3T[:, k, b * S:(b + 1) * S],
                                        start=(k == 0), stop=(k == 1))
                ins.then_inc(gram_mm.h, 1)

                def up(hc):
                    if hc == 0:
                        HT_ok.wait(pe, it, 0)
                        xn3h_ok.wait(pe, it, 2)
                    elif hc == 2:
                        ot_ok.wait(pe, it, 0)
                    elif hc >= 4:
                        h_ok.wait(pe, it, hc - 3)
                    for w, xt in ((W1h, xn3h), (W1l, xn3h), (W1h, xn3l)):
                        for k in range(KD):
                            if hc == 0 and xt is xn3l:
                                xn3l_ok.wait(pe, it, k + 1)
                            pe.matmul(UP[hc % 4][:, :], w[:, k, hc * P:(hc + 1) * P], xt[:, k, :],
                                      start=(w is W1h and xt is xn3h and k == 0), stop=False)

                def up_adapter(hc):
                    if hc == 0:
                        adapter_ok.wait(pe, it, 1)
                    pe.matmul(UP[hc % 4][:, :], Et[:, hc * P:(hc + 1) * P], Tt[:, :], start=False, stop=True)\
                      .then_inc(up_mm.h, 1)

                up(0)
                up(1)
                up(2)
                up(3)
                up_adapter(0)
                up_adapter(1)
                t_ok.wait(pe, it, 2)
                csum_ok.wait(pe, it, 1)
                pe.matmul(GT[0:32, 0:P], sel_i[:, :], gate[:, :], start=True, stop=False)
                pe.matmul(GT[0:32, 0:P], sel_nf[:, :], csum[:, :], start=False, stop=True)
                pe.matmul(GT[0:32, P:2 * P], sel_f[:, :], csum[:, :], start=True, stop=True).then_inc(sel_mm.h, 1)
                for hc in range(4, KH):
                    up(hc)
                    up_adapter(hc - 2)
                up_adapter(KH - 2)
                up_adapter(KH - 1)

                def down(b):
                    fill_ok.wait(pe, it, b + 1)
                    if b < 2:
                        h_ok.wait(pe, it, KH)
                    else:
                        ot_ok.wait(pe, it, b - 1)
                    for k in range(KH):
                        ins = pe.matmul(UAB[b % 2][:, 0:WD], hT[:, k, b * S:(b + 1) * S], W2x[:, k, :],
                                        start=(k == 0), stop=(k == KH - 1))
                    ins.then_inc(down_mm.h, 1)

                def turn_g(b, w, k):
                    w.wait(pe, it, k)
                    gs_ok.wait(pe, it, b + 1)
                    pe.transpose(GT[0:EXTRA, 0:S], gs[:, :], ident[:, :]).then_inc(gsT_mm.h, 1)

                def adapt(b):
                    gsT_ok.wait(pe, it, b + 1)
                    if b == 0:
                        ev_loaded.wait(pe, it, R * G * 16)
                    pe.matmul(UAB[b % 2][:, 0:D], gsT[:, :], Ev[:, b, :], start=False, stop=True,
                              skip_group_check=True).then_inc(adapt_mm.h, 1)

                def decay(b, hf):
                    k = 2 * b + hf
                    dexp_ok.wait(pe, it, k)
                    if k == 0:
                        parts_ok.wait(pe, it, 1)
                    h0 = HEADS * b + 4 * hf
                    pe.matmul(DD[:, :], parts[:, 0, :], pick[:, h0:h0 + 4].unsqueeze(2).broadcast_to([96, 4, P]),
                              start=True, stop=True)
                    pe.matmul(DD[:, :], ident_h[:, :], later[:, :].unsqueeze(1).broadcast_to([P, 4, P]),
                              start=False, stop=True, skip_group_check=True)
                    for h in range(4):
                        ins = pe.matmul(DD[:, h * P:(h + 1) * P], pick[:, h0 + h:h0 + h + 1].broadcast_to([96, P]), parts[:, 1, :],
                                        start=False, stop=True, skip_group_check=True)
                    ins.then_inc(d_mm.h, 1)

                def qk(b, hf):
                    c_ok.wait(pe, it, 2 * b + hf)
                    if b == 0 and hf == 0:
                        qpad_loaded.wait(pe, it, 8 * 16)
                    pe.matmul(QQ[:, :], ctxT[:, hf, b * S:(b + 1) * S], qpad[:, hf, :, b * S:(b + 1) * S],
                              start=True, stop=True).then_inc(qk_mm.h, 1)

                def pv(b):
                    HT_ok.wait(pe, it, b)
                    c_ok.wait(pe, it, 2 * b + 2)
                    if b == 0:
                        vc_ok.wait(pe, it, 1)
                    for h in range(HEADS):
                        q = 32 * (h % 4)
                        pe.matmul(PV[q:q + 32, 2 * P:3 * P], onehot[:, h, :], C[:, h, :],
                                  start=(h < 4), stop=(h >= 4))
                    for h in range(HEADS):
                        q = 32 * (h % 4)
                        ins = pe.matmul(PV[q:q + 32, (h // 4) * P:(h // 4 + 1) * P], vc[:, b, HD * h:HD * h + HD],
                                        C[:, h, :], start=True, stop=True)
                    ins.then_inc(pv_mm.h, 1)

                def turn_h(b):
                    HS_ok.wait(pe, it, b + 1)
                    for k in range(3):
                        ins = pe.transpose(PV[:, k * P:(k + 1) * P], HS[:, k * P:(k + 1) * P], ident[:, :])
                    ins.then_inc(ht_mm.h, 1)

                decay(0, 0)
                qk(0, 0)
                down(0)
                probs_ok.wait(pe, it, 1)
                for b in range(G):
                    ins = pe.transpose(TAB[1][:, b * S:(b + 1) * S], probs[:, b * S:(b + 1) * S], ident[:, :])
                ins.then_inc(PT_mm.h, 1)
                decay(0, 1)
                qk(0, 1)
                turn_g(0, acs_ok, 1)
                PT_ok.wait(pe, it, 1)
                sc_ok.wait(pe, it, 1)
                for m in range(KD):
                    for b in range(G):
                        ins = pe.matmul(TAB[m][:, b * S:(b + 1) * S], xn1[:, b, m * P:(m + 1) * P],
                                        PT[:, b * S:(b + 1) * S], start=True, stop=True)
                    ins.then_inc(px_mm.h, 1)
                em_ok.wait(pe, it, 1)
                gsT_ok.wait(pe, it, 1)
                pe.transpose(GT[:, 0:P], em[:, :], ident[:, :]).then_inc(em_mm.h, 1)
                adapt(0)
                decay(1, 0)
                pv(0)
                qk(1, 0)
                down(1)
                px_ok.wait(pe, it, 2)
                for b in range(G):
                    for k in range(KD):
                        ins = pe.matmul(TAB[b // 2][:, (b % 2) * D:(b % 2) * D + D], pxT[:, k, b * S:(b + 1) * S],
                                        Wvp[:, k, :], start=(k == 0), stop=(k == 1))
                    if b % 2 == 1:
                        ins.then_inc(wv_mm.h, 1)
                turn_h(0)
                decay(1, 1)
                qk(1, 1)
                turn_g(1, emT_ok, 1)
                decay(2, 0)
                pv(1)
                qk(2, 0)
                adapt(1)
                decay(2, 1)
                turn_h(1)
                qk(2, 1)
                decay(3, 0)
                pv(2)
                qk(3, 0)
                turn_h(2)
                decay(3, 1)
                qk(3, 1)
                turn_xn1(it)
                pv(3)
                turn_xn2(it)
                turn_h(3)
                down(2)
                turn_ctx(it)
                turn_g(2, gsT_ok, 2)
                down(3)
                adapt(2)
                project_q(it, 0)
                turn_g(3, gsT_ok, 3)
                project_q(it, 1)
                adapt(3)


LOADS = 11 + 8 + 16 + 16
SETUP_V = 7 + 4 + 8 + 3 + 2 + 2 + 4 + 1 + 8 + 4 + 1 + 2
V_WT = 7 + 4 + 8 + 1
V_TAB = 7 + 4 + 8 + 3 + 2 + 2 + 4 + 1


def kernel(**inputs):
    import concourse.bacc as bacc
    from concourse.bass_utils import run_bass_kernel_spmd

    nc = bacc.Bacc("TRN2", target_bir_lowering=False, num_devices=1)
    names = ["x", "ctx_1024", "L0_attn_W_qkv", "L0_attn_b_qkv", "L0_attn_W_proj", "L0_attn_b_proj",
             "L0_xattn_Wi_w", "L0_xattn_Wi_b", "L0_xattn_Wf_w", "L0_xattn_Wf_b", "L0_xattn_gn_w",
             "L0_xattn_gn_b", "L0_ffn_W1", "L0_ffn_b1", "L0_ffn_W2", "L0_ffn_b2", "L0_ffn_scale"]
    arrays, args = {}, []
    for name in names:
        a = np.ascontiguousarray(inputs[name])
        if a.ndim == 0:
            a = a.reshape(1)
        arrays[name] = a
        args.append(nc.dram_tensor(name, a.shape, mybir.dt.from_np(a.dtype), kind="ExternalInput").ap())
    out = nc.dram_tensor("out", arrays["x"].shape, F32, kind="ExternalOutput").ap()
    build(nc, *args, out)
    r = run_bass_kernel_spmd(nc, [arrays], core_ids=[0])
    return r.results[0]["out"]
```

```python
from contextlib import ExitStack
import math

import numpy as np
import concourse.bass as bass
from concourse import mybir

F32 = mybir.dt.float32
BF16 = mybir.dt.bfloat16
F32R = mybir.dt.float32r
ACT = mybir.ActivationFunctionType
ALU = mybir.AluOpType
AX_X = mybir.AxisListType.X

P = 128
D = 256
S = 128
G = 4
N = G * S
KD = D // P
HID = 1024
KH = HID // P
HEADS = 8
HD = D // HEADS
R = 4
CB = 4
U = D // CB
EXTRA = CB * R
WD = D + EXTRA
EPS = 1e-5
SCALE = (D // 16) ** -0.5
TAU = math.sqrt(HD)
LN_TAU = math.log(TAU)
HI_ACT = 4
LO_POOL = 5
CLAMP = 1e12
BANDS = (-math.log(9.0), -math.log(3.0), math.log(17.0 / 3.0), math.log(19.0))
EXP_SET = "natural_log_exp_and_others"


class Counter:

    def __init__(self, handle, per, base=0):
        self.h, self.per, self.base = handle, per, base

    def at(self, it, k):
        return it * self.per + (self.base + k)


class Chain(Counter):

    def start(self, it):
        self.it, self.k = it, 0

    def link(self, eng, ins):
        self.k += 1
        ins.then_inc(self.h, 1)
        eng.wait_ge(self.h, self.at(self.it, self.k))

    def mark(self, ins):
        self.k += 1
        ins.then_inc(self.h, 1)
        return self.k

    def upto(self, *marks):
        return self.at(self.it, max(marks))

    def end(self):
        assert self.k == self.per, (self.k, self.per)


def build(nc, x, ctx_in, W_qkv, b_qkv, W_proj, b_proj, Wi_w, Wi_b, Wf_w, Wf_b, gn_w, gn_b,
          W1, b1, W2, b2, scale, out):
    NG = x.shape[0] // G
    STEPS = NG + 2
    LAST = STEPS - 1
    ctx = ExitStack()
    with ctx:
        def sb(name, shape, dt=F32):
            return ctx.enter_context(nc.sbuf_tensor(name, shape, dt))

        def sem(name):
            return ctx.enter_context(nc.semaphore(name))

        opened = []

        def per_step(name, per, base=None):
            c = Counter(sem(name), per, 1 if base is None else base)
            if base is None:
                opened.append(c)
            return c

        ident = sb("ident", [P, P])
        A_w = sb("A_w", [P, KD, D])
        Wvp = sb("Wvp", [P, KD, D])
        cq = sb("cq", [P, KD])
        wrow = sb("wrow", [P, D])
        c0 = sb("c0", [P, 1])
        cvp = sb("cvp", [P, D])
        gnw_b = sb("gnw_b", [P, D])
        gnb_b = sb("gnb_b", [P, D])
        b2_b = sb("b2_b", [P, D])
        sc_b = sb("sc_b", [P, 1])
        b1c = sb("b1c", [P, KH])
        WgT = sb("WgT", [P, 4, 32])
        gbias = sb("gbias", [P, 1])
        W1h = sb("W1h", [P, KD, HID], F32R)
        W1l = sb("W1l", [P, KD, HID], F32R)
        W2h = sb("W2h", [P, KH, WD], F32R)
        W2l = sb("W2l", [P, KH, WD], F32R)
        pick = sb("pick", [96, 32], BF16)
        ident_h = sb("ident_h", [P, P], BF16)
        later = sb("later", [P, P], BF16)
        onehot = sb("onehot", [P, HEADS, 32])
        sel_i = sb("sel_i", [P, 32])
        sel_f = sb("sel_f", [P, 32])
        sel_nf = sb("sel_nf", [P, 32])
        ones = sb("ones", [P, P])
        lntau = sb("lntau", [P, 1])
        xin = sb("xin", [P, G, D])
        xn1 = sb("xn1", [P, G, D])
        xn1T = sb("xn1T", [P, KD, N])
        qT = sb("qT", [P, KD, N])
        rowterm = sb("rowterm", [P, G])
        sc = sb("sc", [P, N])
        band_a = sb("band_a", [P, N])
        band_b = sb("band_b", [P, N])
        y = sb("y", [P, N])
        nmx = sb("nmx", [P, G])
        psums = sb("psums", [P, G])
        rinv = sb("rinv", [P, G])
        PT = sb("PT", [P, N])
        pxT = sb("pxT", [P, KD, N])
        x2 = sb("x2", [P, G, D])
        xn2 = sb("xn2", [P, G, D])
        xn2T = sb("xn2T", [P, KD, N])
        qpad = sb("qpad", [P, KD, 4, N])
        ctxn = sb("ctxn", [P, G, D])
        ctxT = sb("ctxT", [P, KD, N])
        hmean = sb("hmean", [P, G * HEADS])
        vc = sb("vc", [P, G, D])
        xg = sb("xg", [P, G, D])
        gate = sb("gate", [P, P])
        gabs = sb("gabs", [P, P])
        lsig = sb("lsig", [P, P])
        csum = sb("csum", [P, P])
        acs = sb("acs", [32, 2 * P])
        am = sb("am", [32, 2, P])
        amr = sb("amr", [32, 2, P])
        am2 = sb("am2", [32, 2, P], BF16)
        parts = sb("parts", [96, 2, P], BF16)
        em = sb("em", [P, P])
        emT = sb("emT", [P, 32])
        dx = [qT[:, i, :] for i in range(2)]
        C = sb("C", [P, HEADS, P])
        HS = sb("HS", [P, 3 * P])
        HT = sb("HT", [P, 2, 3 * P])
        hraw = [pxT[:, 0, :], pxT[:, 1, :], PT[:, :], HT[:, :, :].rearrange("p a b -> p (a b)")[:, 0:N]]
        sq = sb("sq", [P, D])
        v32 = sb("v32", [P, G * HEADS])
        cden = sb("cden", [P, G * HEADS])
        harg = sb("harg", [P, G * HEADS])
        hrs0 = sb("hrs0", [P, G * HEADS])
        htmp = sb("htmp", [P, G * HEADS])
        hrs = sb("hrs", [P, G * HEADS])
        Ng = sb("Ng", [P, G, D])
        x3 = xg
        xn3 = xn2
        xn3T = sb("xn3T", [P, KD, N])
        xn3h = sb("xn3h", [P, KD, N], F32R)
        xn3l = sb("xn3l", [P, KD, N], F32R)
        Z = sb("Z", [P, KD, G, 32])
        Eraw = sb("Eraw", [G * R, HID])
        Et = sb("Et", [P, HID], F32R)
        Tt = sb("Tt", [P, N], F32R)
        Ev = sb("Ev", [P, G, D])
        gs = sb("gs", [P, EXTRA])
        gsT = sb("gsT", [P, S])
        hh = sb("hh", [P, KH, N], F32R)
        hl = sb("hl", [P, KH, N], F32R)
        ot = sb("ot", [P, G, D])
        stat = [sb(f"stat{i}", [P, G, 6]) for i in range(3)]
        mean = [sb(f"mean{i}", [P, G]) for i in range(3)]
        half_gap = [sb(f"half_gap{i}", [P, G]) for i in range(3)]
        ve = [sb(f"ve{i}", [P, G]) for i in range(3)]
        lv = [sb(f"lv{i}", [P, G]) for i in range(3)]
        rs0 = [sb(f"rs0{i}", [P, G]) for i in range(3)]
        nt = [sb(f"nt{i}", [P, G]) for i in range(3)]
        rs = [sb(f"rs{i}", [P, G]) for i in range(3)]

        def bank(name):
            return ctx.enter_context(nc.psum_tensor(name, [P, 512], F32))

        TAB = [bank("TA"), bank("TB")]
        UAB = [bank("UA"), bank("UB")]
        DD = bank("DD")
        QQ = bank("QQ")
        PV = bank("PV")
        GT = bank("GT")

        UP = [PV, TAB[1]] + UAB + [QQ, GT]

        w1n = [xn3T[:, :, :].rearrange("p a b -> p (a b)").rearrange("p (q d) -> p q d", q=4), vc[:, :, :]]
        w2n = [t[:, :, :].rearrange("p a b -> p (a b)") for t in (ctxT, qT)]
        stage = qpad[:, :, :, :].rearrange("p a b c -> p (a b c)")
        wn = stage[:, 0:1536].rearrange("p (k e) -> p k e", k=KD)
        wT = stage[:, 1536:3072].rearrange("p (w k d) -> p w k d", w=3, k=KD)
        wp = stage[:, 3072:3584].rearrange("p (k o) -> p k o", k=KD)
        bB = stage[:, 3584:4096].rearrange("p (w k n) -> p w k n", w=2, k=KD)
        bcol = sb("bcol", [P, 6])
        wgn = xn1T[:, 0, :].rearrange("p n -> p n")
        wg3 = xn2T[:, :, :].rearrange("p a b -> p (a b)")[0:16, 0:3 * D]
        bp_b = sc[:, 0:D]
        w1p = [t[:, 2 * j:2 * j + 2, :].rearrange("p a b -> p (a b)") for t in (Ng, ot) for j in range(2)]
        w2p = [C[:, 4 * j:4 * j + 4, :].rearrange("p a b -> p (a b)") for j in range(2)] + [pxT[:, j, :] for j in range(2)]

        s_load_a = sem("attention_weights_loaded")
        s_load = sem("other_weights_loaded")
        s_gbias = sem("gate_biases_loaded")
        s_ident = sem("ident_made")
        s_zero = sem("zeroed")
        s_qpad = sem("qpad_zeroed")
        s_idz = sem("ident_step")
        s_set_pe = sem("setup_pe")
        s_set_v = sem("setup_dve")
        s_pre_a = sem("first_log")

        x_loaded = per_step("x_loaded", 16, 16)
        ctx_loaded = per_step("ctx_loaded", 16, 16)
        qpad_loaded = per_step("qpad_loaded", 8 * 16)
        e_loaded = per_step("e_loaded", R * 16, R * 16)
        ev_loaded = per_step("ev_loaded", R * G * 16)
        stored = per_step("stored", 16)
        xn1T_mm = per_step("xn1T_mm", 2, 2)
        ctxT_mm = per_step("ctxT_mm", 2, 2)
        xn2T_mm = per_step("xn2T_mm", 2, 2)
        qT_mm = per_step("qT_mm", 2, 2)
        gate_mm = per_step("gate_mm", 1)
        xn3T_mm = per_step("xn3T_mm", 2)
        score_mm = per_step("score_mm", 1)
        gram_mm = per_step("gram_mm", 1)
        up_mm = per_step("up_mm", KH)
        sel_mm = per_step("sel_mm", 1)
        PT_mm = per_step("PT_mm", 1)
        px_mm = per_step("px_mm", 2)
        wv_mm = per_step("wv_mm", 2)
        em_mm = per_step("em_mm", 1)
        d_mm = per_step("d_mm", 2 * G)
        qk_mm = per_step("qk_mm", 2 * G)
        pv_mm = per_step("pv_mm", G)
        ht_mm = per_step("ht_mm", G)
        down_mm = per_step("down_mm", G)
        gsT_mm = per_step("gsT_mm", G)
        adapt_mm = per_step("adapt_mm", G)
        xn1T_ok = per_step("xn1T_ok", 2, 2)
        ctxT_ok = per_step("ctxT_ok", 2, 2)
        xn2T_ok = per_step("xn2T_ok", 2, 2)
        qT_ok = per_step("qT_ok", 2, 2)
        xn3T_ok = per_step("xn3T_ok", 2)
        xn3h_ok = per_step("xn3h_ok", 2)
        sc_ok = per_step("sc_ok", 1)
        h_ok = per_step("h_ok", KH)
        lnsig_ok = per_step("lnsig_ok", 1)
        adapter_ok = per_step("adapter_ok", 1)
        probs_ok = per_step("probs_ok", 1)
        PT_ok = per_step("PT_ok", 1)
        px_ok = per_step("px_ok", 2)
        em_ok = per_step("em_ok", 1)
        dexp_ok = per_step("dexp_ok", 2 * G)
        HS_ok = per_step("HS_ok", G)
        HT_ok = per_step("HT_ok", G)
        sq_ok = per_step("sq_ok", G)
        gsT_ok = per_step("gsT_ok", G)
        hrs0_ok = per_step("hrs0_ok", 1)
        rs0_ok = [per_step("rs0_ok0", 1, 1), per_step("rs0_ok1", 1), per_step("rs0_ok2", 1)]
        ve_ok = [per_step("ve_ok0", 1, 1), per_step("ve_ok1", 1), per_step("ve_ok2", 1)]
        xn_ok = [per_step("xn1_ok", 1, 1), per_step("xn2_ok", 1), per_step("xn3_ok", 1)]
        rowterm_ok = per_step("rowterm_ok", 1, 1)
        hmean_ok = per_step("hmean_ok", 1, 1)
        gate_ok = per_step("gate_ok", 1)
        z_ok = per_step("z_ok", 1)
        xn3l_ok = per_step("xn3l_ok", 2)
        e_ok = per_step("e_ok", 2)
        t_ok = per_step("t_ok", 2)
        y_ok = per_step("y_ok", 1)
        csum_ok = per_step("csum_ok", 1)
        acs_ok = per_step("acs_ok", 1)
        parts_ok = per_step("parts_ok", 1)
        md_ok = per_step("md_ok", 1)
        emT_ok = per_step("emT_ok", 1)
        hi_ok = per_step("hi_ok", KH - HI_ACT)
        lo_ok = per_step("lo_ok", KH - LO_POOL)
        gs_ok = per_step("gs_ok", G)
        c_ok = per_step("c_ok", 2 * G)
        x2_ok = per_step("x2_ok", G)
        hred_ok = per_step("hred_ok", G)
        harg_ok = per_step("harg_ok", 1)
        x3_ok = per_step("x3_ok", 1)
        ot_ok = per_step("ot_ok", G)
        xb_ok = per_step("xb_ok", 1)
        vc_ok = per_step("vc_ok", 1)
        xg_ok = per_step("xg_ok", 1)
        xf_ok = per_step("xf_ok", 1)
        fill_ok = per_step("fill_ok", G)
        hl_ok = per_step("hl_ok", LO_POOL)
        ng_ok = per_step("ng_ok", G)
        v_chain = Chain(sem("dve_step"), 49)
        a_chain = Chain(sem("act_step"), 6)

        x_g = x.rearrange("(g b) s d -> g s b d", b=G)
        c_g = ctx_in.rearrange("(g b) s d -> g s b d", b=G)
        o_g = out.rearrange("(g b) s d -> g s b d", b=G)
        row = lambda a: a.rearrange("(o n) -> o n", o=1).broadcast_to([P, a.shape[0]])

        block = ctx.enter_context(nc.Block())

        @block.sync
        def _(sp):
            def load(dst, src, signal=s_load):
                sp.dma_start(dst, src, allow_slow_non_contiguous=True).then_inc(signal, 16)

            sp.dma_start(xin[:, :, :], x_g[0]).then_inc(x_loaded.h, 16)
            load(wn, W_qkv.rearrange("(k p) e -> p k e", p=P), s_load_a)
            load(wp, W_proj.rearrange("(k p) o -> p k o", p=P), s_load_a)
            load(bcol[:, :], b_qkv.rearrange("(n p) -> p n", p=P), s_load_a)
            load(bp_b, row(b_proj), s_load_a)
            load(wg3[0:8, :], Wi_w, s_load_a)
            load(wg3[8:16, :], Wf_w, s_load_a)
            for i in range(KD):
                load(w1n[i], W1[i * (HID // 2):(i + 1) * (HID // 2), :].rearrange("(q p) d -> p q d", p=P))
                load(w2n[i], W2[i * P:(i + 1) * P, :])
            for c in range(CB):
                load(b1c[64 * (c % 2):64 * (c % 2) + 64, c // 2:KH:2],
                     b1.rearrange("(r u c) -> u r c", r=R, c=CB)[:, :, c])
            load(gnw_b[:, :], row(gn_w))
            load(gnb_b[:, :], row(gn_b))
            load(b2_b[:, :], row(b2))
            load(sc_b[:, :], row(scale))
            sp.dma_start(ctxn[:, :, :], c_g[0]).then_inc(ctx_loaded.h, 16)
            sp.wait_ge(s_zero, 1)
            for b in range(G):
                for t, w in enumerate((Wi_b, Wf_b)):
                    load(gbias[32 * b + 8 * t:32 * b + 8 * t + 8, 0:1], w.rearrange("(n o) -> n o", o=1), s_gbias)
            sp.wait_ge(s_qpad, 1)

            def e_rows(it):
                sp.wait_ge(xn_ok[2].h, xn_ok[2].at(it, 1))
                sp.wait_ge(adapter_ok.h, adapter_ok.at(it, 1))
                for r in range(R):
                    sp.dma_start(Eraw[r::R, r * D:(r + 1) * D], xn3[1 + 2 * r:2 + 2 * r, :, :])\
                      .then_inc(e_loaded.h, 16)

            e_rows(-1)

            def ev_rows(it):
                sp.wait_ge(adapt_mm.h, adapt_mm.at(it, 0))
                for r in range(R):
                    for b in range(G):
                        sp.dma_start(Ev[r:R * CB:R, b, r * U:(r + 1) * U],
                                     xn3[9 + 2 * r:10 + 2 * r, b, :].rearrange("o (c u) -> o c u", c=CB))\
                          .then_inc(ev_loaded.h, 16)

            def step(it, nxt, cur, f):
                def q_rows(c):
                    for r in range(4):
                        sp.dma_start(qpad[32 * r:32 * r + 32, c, r, :], xn2T[32 * r:32 * r + 32, c, :])\
                          .then_inc(qpad_loaded.h, 16)

                sp.wait_ge(qk_mm.h, qk_mm.at(it, 0))
                sp.wait_ge(xn2T_ok.h, xn2T_ok.at(it, 0))
                q_rows(0)
                q_rows(1)
                ev_rows(it)
                sp.wait_ge(xb_ok.h, xb_ok.at(it, 1))
                sp.dma_start(xin[:, :, :], x_g[nxt]).then_inc(x_loaded.h, 16)
                sp.wait_ge(ctxT_mm.h, ctxT_mm.at(it, 0))
                sp.wait_ge(vc_ok.h, vc_ok.at(it, 1))
                sp.dma_start(ctxn[:, :, :], c_g[cur]).then_inc(ctx_loaded.h, 16)
                e_rows(it)
                sp.wait_ge(ot_ok.h, ot_ok.at(it, G))
                sp.dma_start(o_g[f], ot[:, :, :]).then_inc(stored.h, 16)

            for it in range(2):
                step(it, min(it + 1, NG - 1), it, 0)
            with sp.Fori(2, NG - 1) as it:
                step(it, it + 1, it, it - 2)
            for it in range(NG - 1, LAST):
                step(it, NG - 1, min(it, NG - 1), it - 2)
            ev_rows(LAST)
            sp.wait_ge(ot_ok.h, ot_ok.at(LAST, G))
            sp.dma_start(o_g[NG - 1], ot[:, :, :]).then_inc(stored.h, 16)
            sp.wait_ge(x_loaded.h, x_loaded.at(LAST, 0))
            sp.wait_ge(e_loaded.h, e_loaded.at(LAST, 0))
            sp.wait_ge(ctx_loaded.h, ctx_loaded.at(LAST, 0))
            sp.wait_ge(stored.h, stored.at(STEPS, 0))

        @block.gpsimd
        def _(pool):
            for c in opened:
                pool.sem_inc(c.h, 1)
            pool.memset(ident[:, :], 0.0).then_inc(s_idz, 1)
            pool.memset(sel_i[:, :], 0.0)
            pool.memset(ident_h[:, :], 0.0)
            pool.memset(later[:, :], 0.0)
            pool.memset(sel_f[:, :], 0.0)
            pool.memset(sel_nf[:, :], 0.0)
            pool.memset(pick[:, :], 0.0)
            pool.memset(onehot[:, :, :], 0.0).then_inc(s_idz, 1)
            pool.wait_ge(s_idz, 2)
            pool.affine_select(out=ident[:, :], in_=ident[:, :], compare_op=ALU.not_equal, fill=1.0,
                               base=0, pattern=[[-1, P]], channel_multiplier=1).then_inc(s_ident, 1)
            for t, base, val in ((sel_i, 0, 1.0), (sel_f, -8, 1.0), (sel_nf, -8, -1.0)):
                v = t[:, :].rearrange("p (b h) -> p b h", b=G)
                pool.affine_select(out=v, in_=v, compare_op=ALU.not_equal, fill=val, base=base,
                                   pattern=[[-32, G], [-1, 8]], channel_multiplier=1)
            pool.affine_select(out=pick[0:32, :], in_=pick[0:32, :], compare_op=ALU.not_equal, fill=1.0,
                               base=0, pattern=[[-1, 32]], channel_multiplier=1)
            pool.affine_select(out=ident_h[:, :], in_=ident_h[:, :], compare_op=ALU.not_equal, fill=1.0,
                               base=0, pattern=[[-1, P]], channel_multiplier=1)
            pool.affine_select(out=later[:, :], in_=later[:, :], compare_op=ALU.is_ge, fill=-1e30,
                               base=0, pattern=[[1, P]], channel_multiplier=-1)
            pool.memset(onehot[:, 0:4, 0:1], 1.0)
            pool.memset(onehot[:, 4:8, 1:2], 1.0)
            pool.memset(ones[:, :], 1.0)
            pool.memset(lntau[:, :], LN_TAU)
            for t in (WgT, x2, xn2, x3, Z, Eraw, Ev, gsT, em):
                pool.memset(t[tuple([slice(None)] * len(t.shape))], 0.0)
            for t in (Tt, Et):
                pool.memset(t[:, :].bitcast(F32), 0.0)
            pool.memset(gbias[:, :], 0.0).then_inc(s_zero, 1)

            pool.wait_ge(s_load, 16 * LOADS)
            pool.wait_ge(s_set_v, V_BIAS)
            pool.memset(stage, 0.0).then_inc(s_qpad, 1)
            pool.wait_ge(s_set_v, SETUP_V)

            def fill(it, b):
                if b == 0:
                    pool.wait_ge(xn3l_ok.h, xn3l_ok.at(it, 2))
                pool.wait_ge(down_mm.h, down_mm.at(it, b))
                unit = ones[:, 0:2 * R].rearrange("p (k r) -> p k r", k=2)
                for w, xt in ((W2h, xn3h), (W2l, xn3l)):
                    for c in range(CB):
                        ins = pool.tensor_tensor(w[:, 2 * c:2 * c + 2, D + R * c:D + R * c + R],
                                                 xt[:, :, b * S + 10:b * S + 10 + 2 * R:2].bitcast(F32), unit, ALU.mult)
                ins.then_inc(fill_ok.h, 1)

            def step(it, last=False):
                pool.wait_ge(x3_ok.h, x3_ok.at(it, 0))
                pool.wait_ge(stored.h, stored.at(it, 0))
                pool.tensor_tensor(ot[:, :, :], x3[:, :, :], b2_b[:, :].unsqueeze(1).broadcast_to([P, G, D]),
                                   ALU.add).then_inc(xf_ok.h, 1)
                if not last:
                    pool.wait_ge(x2_ok.h, x2_ok.at(it, 0))
                    pool.wait_ge(xn_ok[2].h, xn_ok[2].at(it, 0))
                    pool.wait_ge(xf_ok.h, xf_ok.at(it, 1))
                    pool.tensor_tensor(xg[:, :, :], x2[:, :, :], gnb_b[:, :].unsqueeze(1).broadcast_to([P, G, D]),
                                       ALU.add).then_inc(xg_ok.h, 1)
                fill(it, 0)
                for hc in range(LO_POOL):
                    pool.wait_ge(h_ok.h, h_ok.at(it, hc + 1))
                    if hc >= HI_ACT:
                        pool.wait_ge(hi_ok.h, hi_ok.at(it, hc - HI_ACT + 1))
                    pool.tensor_tensor(hl[:, hc, :], hraw[hc % 4], hh[:, hc, :].bitcast(F32), ALU.subtract)\
                        .then_inc(hl_ok.h, 1)
                if not last:
                    pool.wait_ge(x_loaded.h, x_loaded.at(it, 0))
                    pool.wait_ge(xn_ok[1].h, xn_ok[1].at(it, 0))
                    pool.wait_ge(xg_ok.h, xg_ok.at(it, 1))
                    pool.tensor_tensor(x2[:, :, :], xin[:, :, :], cvp[:, :].unsqueeze(1).broadcast_to([P, G, D]),
                                       ALU.add).then_inc(xb_ok.h, 1)
                    pool.wait_ge(hmean_ok.h, hmean_ok.at(it, 0))
                    pool.wait_ge(pv_mm.h, pv_mm.at(it, 0))
                    pool.tensor_tensor(vc[:, :, :].rearrange("p b (h d) -> p (b h) d", h=HEADS),
                                       ctxn[:, :, :].rearrange("p b (h d) -> p (b h) d", h=HEADS),
                                       hmean[:, :].unsqueeze(2).broadcast_to([P, G * HEADS, HD]),
                                       ALU.subtract).then_inc(vc_ok.h, 1)
                fill(it, 1)

                def weigh(b):
                    pool.wait_ge(HT_ok.h, HT_ok.at(it, b + 1))
                    pool.tensor_tensor(Ng[:, b, :], HT[:, b % 2, 0:D], gnw_b[:, :], ALU.mult).then_inc(ng_ok.h, 1)

                fill(it, 2)
                if not last:
                    for b in range(G):
                        weigh(b)
                fill(it, 3)

            with pool.Fori(0, LAST) as it:
                step(it)
            step(LAST, last=True)

        @block.scalar
        def _(act):
            a = a_chain

            def ln_root(i, it):
                act.wait_ge(ve_ok[i].h, ve_ok[i].at(it, 1))
                a.link(act, act.activation(lv[i][:, :], ve[i][:, :], ACT.Ln))
                act.activation(rs0[i][:, :], lv[i][:, :], ACT.Exp, scale=-0.5).then_inc(rs0_ok[i].h, 1)

            act.preload_act_table_set(EXP_SET)
            act.wait_ge(ve_ok[0].h, 1)
            act.activation(lv[0][:, :], ve[0][:, :], ACT.Ln).then_inc(s_pre_a, 1)
            act.wait_ge(s_pre_a, 1)
            act.activation(rs0[0][:, :], lv[0][:, :], ACT.Exp, scale=-0.5).then_inc(rs0_ok[0].h, 1)
            act.wait_ge(s_set_v, SETUP_V)

            def evac(it, mm, ok, banks, dst, free):
                for c in range(KD):
                    act.wait_ge(mm.h, mm.at(it, c + 1))
                    if c == 0:
                        for f in free:
                            act.wait_ge(f.h, f.at(it, f.per))
                    act.activation(dst[:, c, :], banks[c][:, :], ACT.Copy).then_inc(ok.h, 1)

            def evac_xn1T(it):
                evac(it, xn1T_mm, xn1T_ok, TAB, xn1T, [score_mm])

            def evac_xn2T(it):
                evac(it, xn2T_mm, xn2T_ok, TAB, xn2T, [gate_mm, qpad_loaded])

            def evac_ctxT(it):
                evac(it, ctxT_mm, ctxT_ok, [QQ, DD], ctxT, [qk_mm])

            def evac_qT(it, m):
                act.wait_ge(qT_mm.h, qT_mm.at(it, m + 1))
                act.wait_ge(score_mm.h, score_mm.at(it, 1))
                act.wait_ge(c_ok.h, c_ok.at(it, 2 * G))
                act.activation(qT[:, m, :], TAB[m][:, :], ACT.Identity, bias=cq[:, m:m + 1]).then_inc(qT_ok.h, 1)

            evac_xn1T(-1)
            evac_xn2T(-1)
            evac_ctxT(-1)
            evac_qT(-1, 0)
            evac_qT(-1, 1)

            def step(it, last=False):
                a.start(it)
                for c in range(KD):
                    act.wait_ge(xn3T_mm.h, xn3T_mm.at(it, c + 1))
                    if c == 0:
                        act.wait_ge(down_mm.h, down_mm.at(it, 0))
                    act.activation(xn3T[:, c, :], (QQ, DD)[c][:, :], ACT.Copy).then_inc(xn3T_ok.h, 1)
                for c in range(KD):
                    act.activation(xn3h[:, c, :], (QQ, DD)[c][:, :], ACT.Copy).then_inc(xn3h_ok.h, 1)
                if not last:
                    act.wait_ge(score_mm.h, score_mm.at(it, 1))
                    act.wait_ge(rowterm_ok.h, rowterm_ok.at(it, 0))
                    for b in range(G):
                        ins = act.activation(sc[:, b * S:(b + 1) * S], TAB[0][:, b * S:(b + 1) * S], ACT.Identity,
                                             bias=rowterm[:, b:b + 1], scale=SCALE)
                    ins.then_inc(sc_ok.h, 1)
                    act.wait_ge(gate_ok.h, gate_ok.at(it, 1))
                    a.link(act, act.activation(gabs[:, :], gate[:, :], ACT.Abs))
                    a.link(act, act.activation(lsig[:, :], gabs[:, :], ACT.Exp, scale=-1.0))
                    act.activation(gabs[:, :], lsig[:, :], ACT.Ln, bias=1.0).then_inc(lnsig_ok.h, 1)
                act.preload_act_table(ACT.Gelu)
                act.wait_ge(e_ok.h, e_ok.at(it, 1))
                act.activation(Et[64:80, :], Et[0:16, :].bitcast(F32), ACT.Copy)
                act.wait_ge(e_ok.h, e_ok.at(it, 2))
                act.activation(Et[96:112, :], Et[32:48, :].bitcast(F32), ACT.Copy)
                act.wait_ge(t_ok.h, t_ok.at(it, 1))
                act.activation(Tt[32:48, :], Tt[0:16, :].bitcast(F32), ACT.Copy)
                act.wait_ge(t_ok.h, t_ok.at(it, 2))
                act.activation(Tt[96:112, :], Tt[64:80, :].bitcast(F32), ACT.Copy).then_inc(adapter_ok.h, 1)
                for hc in range(KH):
                    act.wait_ge(up_mm.h, up_mm.at(it, hc + 1))
                    if hc >= 4:
                        act.wait_ge(hl_ok.h, hl_ok.at(it, hc - 3))
                    if hc == 3:
                        act.wait_ge(x3_ok.h, x3_ok.at(it, 0))
                    if hc < HI_ACT:
                        act.activation(hh[:, hc, :], UP[hc % 6][:, :], ACT.Gelu, bias=b1c[:, hc:hc + 1])
                    act.activation(hraw[hc % 4], UP[hc % 6][:, :], ACT.Gelu, bias=b1c[:, hc:hc + 1])\
                        .then_inc(h_ok.h, 1)

                def gsT_copy(b):
                    act.wait_ge(gsT_mm.h, gsT_mm.at(it, b + 1))
                    act.activation(gsT[0:EXTRA, :], GT[0:EXTRA, 0:S], ACT.Copy).then_inc(gsT_ok.h, 1)

                if last:
                    for b in range(G):
                        gsT_copy(b)
                    return

                act.preload_act_table_set(EXP_SET)

                def dexp(b, hf):
                    act.wait_ge(d_mm.h, d_mm.at(it, 2 * b + hf + 1))
                    act.wait_ge(c_ok.h, c_ok.at(it, max(2 * b + hf - 1, 0)))
                    act.activation(dx[hf], DD[:, :], ACT.Exp)\
                        .then_inc(dexp_ok.h, 1)

                def hs(b):
                    act.wait_ge(pv_mm.h, pv_mm.at(it, b + 1))
                    act.activation(HS[:, :], PV[:, 0:3 * P], ACT.Copy).then_inc(HS_ok.h, 1)

                def ht(b):
                    act.wait_ge(ht_mm.h, ht_mm.at(it, b + 1))
                    if b == 0:
                        act.wait_ge(x3_ok.h, x3_ok.at(it, 0))
                    elif b >= 2:
                        act.wait_ge(ng_ok.h, ng_ok.at(it, b - 1))
                        act.wait_ge(hred_ok.h, hred_ok.at(it, b - 1))
                    act.activation(HT[:, b % 2, :], PV[:, 0:3 * P], ACT.Copy).then_inc(HT_ok.h, 1)
                    act.wait_ge(HT_ok.h, HT_ok.at(it, b + 1))
                    act.wait_ge(hred_ok.h, hred_ok.at(it, b))
                    act.activation(sq[:, :], HT[:, b % 2, 0:D], ACT.Square).then_inc(sq_ok.h, 1)

                dexp(0, 0)
                act.wait_ge(y_ok.h, y_ok.at(it, 1))
                for b in range(G):
                    ins = act.activation(y[:, b * S:(b + 1) * S], y[:, b * S:(b + 1) * S], ACT.Exp,
                                         bias=nmx[:, b:b + 1], accum_out=psums[:, b:b + 1])
                ins.then_inc(probs_ok.h, 1)
                act.wait_ge(md_ok.h, md_ok.at(it, 1))
                act.activation(em[0:32, :], em[0:32, :], ACT.Exp, scale=-1.0, bias=lntau[0:32, :]).then_inc(em_ok.h, 1)
                dexp(0, 1)
                act.wait_ge(PT_mm.h, PT_mm.at(it, 1))
                act.activation(PT[:, :], TAB[1][:, :], ACT.Copy).then_inc(PT_ok.h, 1)
                gsT_copy(0)
                for m in range(KD):
                    act.wait_ge(px_mm.h, px_mm.at(it, m + 1))
                    act.activation(pxT[:, m, :], TAB[m][:, :], ACT.Copy).then_inc(px_ok.h, 1)
                ln_root(0, it)
                dexp(1, 0)
                hs(0)
                ht(0)
                dexp(1, 1)
                gsT_copy(1)
                dexp(2, 0)
                ln_root(1, it)
                hs(1)
                dexp(2, 1)
                ht(1)
                dexp(3, 0)
                hs(2)
                ht(2)
                dexp(3, 1)
                evac_xn1T(it)
                hs(3)
                ht(3)
                evac_xn2T(it)
                act.wait_ge(harg_ok.h, harg_ok.at(it, 1))
                a.link(act, act.activation(htmp[:, :], harg[:, :], ACT.Ln))
                act.activation(hrs0[:, :], htmp[:, :], ACT.Exp, scale=-0.5).then_inc(hrs0_ok.h, 1)
                evac_ctxT(it)
                evac_qT(it, 0)
                gsT_copy(2)
                gsT_copy(3)
                ln_root(2, it)
                evac_qT(it, 1)
                a.end()

            with act.Fori(0, LAST) as it:
                step(it)
            step(LAST, last=True)

        @block.vector
        def _(dve):
            v = v_chain
            setup = [0]

            def done(ins):
                setup[0] += 1
                ins.then_inc(s_set_v, 1)
                dve.wait_ge(s_set_v, setup[0])

            def ln_stats(i, X, link):
                for b in range(G):
                    ins = dve.bn_stats(stat[i][:, b, :], X[:, b, :])
                link(ins)
                ln_moments(i, link)

            def ln_moments(i, link):
                even, odd = stat[i][:, :, 0:3], stat[i][:, :, 3:6]
                dve.tensor_tensor(mean[i][:, :], even[:, :, 1], odd[:, :, 1], ALU.add)
                dve.tensor_tensor(half_gap[i][:, :], even[:, :, 1], odd[:, :, 1], ALU.subtract)
                link(dve.tensor_tensor(ve[i][:, :], even[:, :, 2], odd[:, :, 2], ALU.add))
                dve.tensor_scalar(mean[i][:, :], mean[i][:, :], 0.5, None, ALU.mult)
                dve.tensor_scalar(ve[i][:, :], ve[i][:, :], 1.0 / D, EPS, ALU.mult, ALU.add)
                link(dve.scalar_tensor_tensor(half_gap[i][:, :], half_gap[i][:, :], 0.25, half_gap[i][:, :],
                                              ALU.mult, ALU.mult))
                dve.tensor_tensor(ve[i][:, :], ve[i][:, :], half_gap[i][:, :], ALU.add).then_inc(ve_ok[i].h, 1)

            def ln_scale(i, link):
                link(dve.tensor_tensor(nt[i][:, :], rs0[i][:, :], rs0[i][:, :], ALU.mult))
                link(dve.tensor_tensor(nt[i][:, :], nt[i][:, :], ve[i][:, :], ALU.mult))
                link(dve.tensor_scalar(nt[i][:, :], nt[i][:, :], -0.5, 1.5, ALU.mult, ALU.add))
                link(dve.tensor_tensor(rs[i][:, :], nt[i][:, :], rs0[i][:, :], ALU.mult))

            def ln_apply(i, X, Xn):
                for b in range(G):
                    src, dst = X[:, b, :], Xn[:, b, :]
                    if i == 2:
                        src = src.rearrange("p (u c) -> p c u", c=CB)
                        dst = dst.rearrange("p (c u) -> p c u", c=CB)
                    ins = dve.tensor_scalar(dst, src, mean[i][:, b:b + 1], rs[i][:, b:b + 1], ALU.subtract, ALU.mult)
                ins.then_inc(xn_ok[i].h, 1)

            dve.wait_ge(x_loaded.h, 16)
            ln_stats(0, xin, done)
            dve.wait_ge(rs0_ok[0].h, 1)
            ln_scale(0, done)
            ln_apply(0, xin, xn1)
            dve.wait_ge(s_load_a, 16 * LOADS_A)
            done(dve.tensor_copy(bB, bcol[:, 2:6].rearrange("p (w k) -> p w k", w=2).unsqueeze(3)
                                 .broadcast_to([P, 2, KD, P])))
            done(dve.tensor_tensor(wgn[0:16, 0:D], wg3[:, D:2 * D], wg3[:, 2 * D:3 * D], ALU.add))
            n = 0
            for w in range(3):
                n += 1
                dve.wait_ge(s_set_pe, n)
                done(dve.tensor_copy(wT[:, w, :, :].rearrange("p k d -> p (k d)"), TAB[w % 2][:, :]))
            for k in range(KD):
                n += 1
                dve.wait_ge(s_set_pe, n)
                done(dve.tensor_copy(A_w[:, k, :], UAB[k][:, 0:D]))
            for k in range(KD):
                n += 1
                dve.wait_ge(s_set_pe, n)
                done(dve.tensor_copy(Wvp[:, k, :], UAB[k][:, 0:D]))
            n += 1
            dve.wait_ge(s_set_pe, n)
            done(dve.tensor_scalar(wrow[:, :], DD[:, 0:D], SCALE, None, ALU.mult))
            done(dve.tensor_tensor(cvp[:, :], DD[:, D:2 * D], bp_b, ALU.add))
            done(dve.tensor_copy(cq[:, :], QQ[:, 0:KD]))
            done(dve.tensor_scalar(c0[:, :], QQ[:, KD:KD + 1], SCALE, None, ALU.mult))
            dve.wait_ge(s_load, 16 * LOADS)
            for i in range(4):
                done(dve.tensor_copy(
                    w1p[i].rearrange("p (q c u) -> p q c u", q=4, c=2),
                    w1n[i % 2].rearrange("p q (u c) -> p q c u", c=CB)[:, :, 2 * (i // 2):2 * (i // 2) + 2, :]))
            for i in range(4):
                for o in range(KD):
                    done(dve.tensor_copy(w2p[i][:, o * D:(o + 1) * D].rearrange("p (c u) -> p c u", c=CB),
                                         w2n[o][:, i * D:(i + 1) * D].rearrange("p (u c) -> p c u", c=CB)))
            n += 1
            dve.wait_ge(s_set_pe, n)
            dve.wait_ge(s_zero, 1)
            dve.wait_ge(s_gbias, 16 * 2 * G)
            done(dve.tensor_copy(WgT[:, :, 0:16], PV[:, 0:64].rearrange("p (k n) -> p k n", k=4)))
            done(dve.tensor_copy(pick[32:64, :], pick[0:32, :]))
            done(dve.tensor_copy(pick[64:96, :], pick[0:32, :]))
            done(dve.memset(W2h[:, :, D:WD].bitcast(F32), 0.0))
            done(dve.memset(W2l[:, :, D:WD].bitcast(F32), 0.0))
            for i in range(4):
                n += 1
                dve.wait_ge(s_set_pe, n)
                half = slice((i % 2) * 512, (i % 2) * 512 + 512)
                src = TAB[i % 2][:, :].rearrange("p (r u c) -> p r u c", r=2, c=CB)
                hi, lo = (w[:, i // 2, half].rearrange("p (r c u) -> p r u c", r=2, c=CB) for w in (W1h, W1l))
                done(dve.tensor_copy(hi, src))
                done(dve.tensor_tensor(lo, src, hi.bitcast(F32), ALU.subtract))
            for i in range(4):
                n += 1
                dve.wait_ge(s_set_pe, n)
                src = TAB[i % 2][:, :].rearrange("p (k o) -> p k o", k=2)
                done(dve.tensor_copy(W2h[:, 2 * i:2 * i + 2, 0:D], src))
                done(dve.tensor_tensor(W2l[:, 2 * i:2 * i + 2, 0:D], src, W2h[:, 2 * i:2 * i + 2, 0:D].bitcast(F32),
                                       ALU.subtract))

            def value_means(it, link):
                dve.wait_ge(ctx_loaded.h, ctx_loaded.at(it, 16))
                dve.wait_ge(vc_ok.h, vc_ok.at(it, 1))
                link(dve.tensor_reduce(hmean[:, :], ctxn[:, :, :].rearrange("p b (h d) -> p (b h) d", h=HEADS),
                                       AX_X, ALU.add))
                dve.tensor_scalar(hmean[:, :], hmean[:, :], 1.0 / HD, None, ALU.mult).then_inc(hmean_ok.h, 1)

            def row_terms(it, link):
                dve.wait_ge(sc_ok.h, sc_ok.at(it, 1))
                for b in range(G):
                    product = (sc, band_a)[b // 2][:, (b % 2) * D:(b % 2) * D + D]
                    ins = dve.tensor_tensor_reduce(product, xn1[:, b, :], wrow[:, :], 1.0, 0.0, ALU.mult, ALU.add,
                                                   rowterm[:, b:b + 1])
                link(ins)
                dve.tensor_scalar(rowterm[:, :], rowterm[:, :], c0[:, 0:1], None, ALU.add).then_inc(rowterm_ok.h, 1)

            value_means(-1, done)
            row_terms(-1, done)
            assert setup[0] == SETUP_V, setup[0]

            def step(it, last=False):
                v.start(it)
                link = lambda ins: v.link(dve, ins)
                if not last:
                    dve.wait_ge(gate_mm.h, gate_mm.at(it, 1))
                    dve.tensor_scalar(gate[:, :], GT[:, 0:P], gbias[:, 0:1], None, ALU.add).then_inc(gate_ok.h, 1)
                dve.wait_ge(xn3T_ok.h, xn3T_ok.at(it, 2))
                for b in range(G):
                    ins = dve.tensor_copy(Z[:, :, b, R * b:R * b + R],
                                          xn3T[:, :, b * S + 2:b * S + 2 + 2 * R:2])
                ins.then_inc(z_ok.h, 1)
                for c in range(KD):
                    dve.wait_ge(xn3h_ok.h, xn3h_ok.at(it, c + 1))
                    dve.tensor_tensor(xn3l[:, c, :], xn3T[:, c, :], xn3h[:, c, :].bitcast(F32), ALU.subtract)\
                       .then_inc(xn3l_ok.h, 1)
                dve.wait_ge(e_loaded.h, e_loaded.at(it, 0))
                dve.wait_ge(up_mm.h, up_mm.at(it, 0))
                dve.tensor_copy(Et[0:16, :], Eraw[:, :]).then_inc(e_ok.h, 1)
                dve.wait_ge(e_ok.h, e_ok.at(it, 1))
                dve.tensor_tensor(Et[32:48, :], Eraw[:, :], Et[0:16, :].bitcast(F32), ALU.subtract)\
                   .then_inc(e_ok.h, 1)
                if not last:
                    dve.wait_ge(lnsig_ok.h, lnsig_ok.at(it, 1))
                    link(dve.scalar_tensor_tensor(lsig[:, :], gate[:, :], 0.0, gabs[:, :], ALU.min, ALU.subtract))
                    dve.tensor_tensor_scan(csum[:, :], ones[:, :], lsig[:, :], 0.0, ALU.mult, ALU.add)\
                       .then_inc(csum_ok.h, 1)
                dve.wait_ge(gram_mm.h, gram_mm.at(it, 1))
                for b in range(G):
                    cols = slice(b * S, (b + 1) * S)
                    ins = dve.tensor_scalar(Tt[0:16, cols], GT[32 * b:32 * b + 16, 0:S], sc_b[0:16, 0:1], None, ALU.mult)
                ins.then_inc(t_ok.h, 1)
                dve.wait_ge(t_ok.h, t_ok.at(it, 1))
                for b in range(G):
                    cols = slice(b * S, (b + 1) * S)
                    ins = dve.scalar_tensor_tensor(Tt[64:80, cols], GT[32 * b:32 * b + 16, 0:S], sc_b[0:16, 0:1],
                                                   Tt[0:16, cols].bitcast(F32), ALU.mult, ALU.subtract)
                ins.then_inc(t_ok.h, 1)
                if not last:
                    dve.wait_ge(sc_ok.h, sc_ok.at(it, 1))
                    band_lo = v.mark(dve.tensor_scalar(band_a[:, :], sc[:, :], BANDS[0], 0.3, ALU.is_ge, ALU.mult))
                    band_hi = v.mark(dve.tensor_scalar(band_b[:, :], sc[:, :], BANDS[3], None, ALU.is_gt))
                    dve.wait_ge(sel_mm.h, sel_mm.at(it, 1))
                    dve.tensor_copy(acs[:, :], DD[0:32, 0:2 * P]).then_inc(acs_ok.h, 1)
                    dve.wait_ge(v.h, v.upto(band_lo))
                    band_lo = v.mark(dve.scalar_tensor_tensor(band_a[:, :], sc[:, :], BANDS[1], band_a[:, :],
                                                              ALU.is_ge, ALU.max))
                    dve.wait_ge(acs_ok.h, acs_ok.at(it, 1))
                    run_max = v.mark(dve.tensor_tensor_scan(am[:, 1, :], acs[:, 0:P], acs[:, 0:P], -3e38,
                                                            ALU.max, ALU.max))
                    dve.tensor_copy(am[:, 0, :], acs[:, 0:P])
                    dve.wait_ge(v.h, v.upto(band_hi))
                    band_hi = v.mark(dve.scalar_tensor_tensor(band_b[:, :], sc[:, :], BANDS[2], band_b[:, :],
                                                              ALU.is_gt, ALU.add))
                    dve.wait_ge(v.h, v.upto(run_max))
                    dve.wait_ge(em_mm.h, em_mm.at(it, 0))
                    arg = v.mark(dve.tensor_tensor(em[0:32, :], am[:, 1, :], acs[:, P:2 * P], ALU.add))
                    dve.wait_ge(v.h, v.upto(band_hi))
                    band = v.mark(dve.scalar_tensor_tensor(band_a[:, :], band_b[:, :], 0.5, band_a[:, :],
                                                           ALU.mult, ALU.add))
                    dve.wait_ge(v.h, v.upto(arg))
                    neg = v.mark(dve.tensor_scalar(am[:, 1, :], am[:, 1, :], -1.0, None, ALU.mult))
                    dve.tensor_scalar(em[0:32, :], em[0:32, :], -25.0, None, ALU.max).then_inc(md_ok.h, 1)
                    dve.wait_ge(v.h, v.upto(band))
                    scores = v.mark(dve.scalar_tensor_tensor(y[:, :], band_a[:, :], 0.1, sc[:, :], ALU.max, ALU.mult))
                    dve.wait_ge(d_mm.h, d_mm.at(it, 0))
                    dve.wait_ge(v.h, v.upto(neg))
                    hi = v.mark(dve.tensor_copy(parts[0:32, :, :], am[:, :, :]))
                    dve.wait_ge(v.h, v.upto(scores))
                    top = v.mark(dve.tensor_reduce(nmx[:, :], y[:, :].rearrange("p (b t) -> p b t", b=G), AX_X, ALU.max))
                    dve.wait_ge(v.h, v.upto(hi))
                    rest = v.mark(dve.tensor_tensor(amr[:, :, :], am[:, :, :], parts[0:32, :, :], ALU.subtract))
                    dve.wait_ge(v.h, v.upto(top))
                    dve.tensor_scalar(nmx[:, :], nmx[:, :], -1.0, None, ALU.mult).then_inc(y_ok.h, 1)
                    dve.wait_ge(v.h, v.upto(rest))
                    link(dve.tensor_copy(am2[:, :, :], amr[:, :, :]))
                    dve.tensor_copy(parts[32:64, :, :], am2[:, :, :])
                    dve.tensor_tensor(parts[64:96, :, :], amr[:, :, :], am2[:, :, :], ALU.subtract)\
                       .then_inc(parts_ok.h, 1)
                for hc in range(HI_ACT, KH):
                    dve.wait_ge(h_ok.h, h_ok.at(it, hc + 1))
                    dve.tensor_copy(hh[:, hc, :], hraw[hc % 4]).then_inc(hi_ok.h, 1)
                for hc in range(LO_POOL, KH):
                    dve.wait_ge(hi_ok.h, hi_ok.at(it, hc - HI_ACT + 1))
                    dve.tensor_tensor(hl[:, hc, :], hraw[hc % 4], hh[:, hc, :].bitcast(F32),
                                      ALU.subtract).then_inc(lo_ok.h, 1)

                def g_out(b):
                    dve.wait_ge(down_mm.h, down_mm.at(it, b + 1))
                    dve.wait_ge(gsT_mm.h, gsT_mm.at(it, b))
                    dve.tensor_scalar(gs[:, :], UAB[b % 2][:, D:WD], sc_b[:, 0:1], None, ALU.mult)\
                        .then_inc(gs_ok.h, 1)

                def o_out(b):
                    dve.wait_ge(adapt_mm.h, adapt_mm.at(it, b + 1))
                    if b == 0:
                        dve.wait_ge(xf_ok.h, xf_ok.at(it, 1))
                    dve.tensor_tensor(ot[:, b, :], UAB[b % 2][:, 0:D], ot[:, b, :], ALU.add).then_inc(ot_ok.h, 1)

                if last:
                    for b in range(0, G, 2):
                        g_out(b)
                        g_out(b + 1)
                        o_out(b)
                        o_out(b + 1)
                    return

                def weigh_qk(b, hf):
                    k = 2 * b + hf
                    dve.wait_ge(dexp_ok.h, dexp_ok.at(it, k + 1))
                    dve.wait_ge(qk_mm.h, qk_mm.at(it, k + 1))
                    dve.wait_ge(pv_mm.h, pv_mm.at(it, b))
                    dve.tensor_tensor(C[:, 4 * hf:4 * hf + 4, :].rearrange("p h i -> p (h i)"),
                                      dx[hf], QQ[:, :], ALU.mult)\
                        .then_inc(c_ok.h, 1)

                def head_sums(b):
                    dve.wait_ge(HT_ok.h, HT_ok.at(it, b + 1))
                    cd = cden[:, 8 * b:8 * b + 8].rearrange("p (e g) -> p e g", e=2)
                    sums = HT[:, b % 2, D:D + P].rearrange("p (g e) -> p e g", g=4)[:, 0:2, :]
                    link(dve.scalar_tensor_tensor(cd, sums, -1.0,
                                                  emT[:, 8 * b:8 * b + 8].rearrange("p (e g) -> p e g", e=2),
                                                  ALU.mult, ALU.max))
                    dve.tensor_tensor(cd, cd, sums, ALU.max)
                    dve.wait_ge(sq_ok.h, sq_ok.at(it, b + 1))
                    dve.tensor_reduce(v32[:, 8 * b:8 * b + 8], sq[:, :].rearrange("p (h d) -> p h d", h=HEADS),
                                      AX_X, ALU.add).then_inc(hred_ok.h, 1)

                weigh_qk(0, 0)
                dve.wait_ge(probs_ok.h, probs_ok.at(it, 1))
                link(dve.reciprocal(rinv[:, :], psums[:, :]))
                g_out(0)
                weigh_qk(0, 1)
                dve.wait_ge(em_mm.h, em_mm.at(it, 1))
                dve.tensor_copy(emT[:, :], GT[:, 0:32]).then_inc(emT_ok.h, 1)
                dve.wait_ge(emT_ok.h, emT_ok.at(it, 1))
                dve.wait_ge(x_loaded.h, x_loaded.at(it, 16))
                ln_stats(0, xin, link)
                o_out(0)
                dve.wait_ge(rs0_ok[0].h, rs0_ok[0].at(it, 1))
                ln_scale(0, link)
                dve.wait_ge(score_mm.h, score_mm.at(it, 1))
                dve.wait_ge(px_mm.h, px_mm.at(it, 2))
                ln_apply(0, xin, xn1)
                weigh_qk(1, 0)
                g_out(1)
                dve.wait_ge(xb_ok.h, xb_ok.at(it, 1))
                dve.wait_ge(xg_ok.h, xg_ok.at(it, 1))
                for b in range(G):
                    dve.wait_ge(wv_mm.h, wv_mm.at(it, b // 2 + 1))
                    ins = dve.scalar_tensor_tensor(x2[:, b, :], TAB[b // 2][:, (b % 2) * D:(b % 2) * D + D],
                                                   rinv[:, b:b + 1], x2[:, b, :], ALU.mult, ALU.add)
                    ins.then_inc(x2_ok.h, 1)
                head_sums(0)
                weigh_qk(1, 1)
                dve.wait_ge(x2_ok.h, x2_ok.at(it, G))
                ln_stats(1, x2, link)
                weigh_qk(2, 0)
                value_means(it, link)
                weigh_qk(2, 1)
                head_sums(1)
                o_out(1)
                row_terms(it, link)
                weigh_qk(3, 0)
                dve.wait_ge(rs0_ok[1].h, rs0_ok[1].at(it, 1))
                ln_scale(1, link)
                weigh_qk(3, 1)
                dve.wait_ge(e_loaded.h, e_loaded.at(it, 0))
                dve.wait_ge(ev_loaded.h, ev_loaded.at(it, R * G * 16))
                ln_apply(1, x2, xn2)
                head_sums(2)

                head_sums(3)
                dve.wait_ge(hred_ok.h, hred_ok.at(it, G))
                link(dve.tensor_scalar(cden[:, :], cden[:, :], TAU * 1e-6, CLAMP, ALU.add, ALU.min))
                link(dve.scalar_tensor_tensor(cden[:, :], cden[:, :], EPS, cden[:, :], ALU.mult, ALU.mult))
                dve.scalar_tensor_tensor(harg[:, :], v32[:, :], 1.0 / HD, cden[:, :], ALU.mult, ALU.add)\
                   .then_inc(harg_ok.h, 1)
                dve.wait_ge(hrs0_ok.h, hrs0_ok.at(it, 1))
                link(dve.tensor_tensor(hrs[:, :], hrs0[:, :], hrs0[:, :], ALU.mult))
                link(dve.tensor_tensor(hrs[:, :], hrs[:, :], harg[:, :], ALU.mult))
                link(dve.tensor_scalar(hrs[:, :], hrs[:, :], -0.5, 1.5, ALU.mult, ALU.add))
                link(dve.tensor_tensor(hrs[:, :], hrs[:, :], hrs0[:, :], ALU.mult))
                g_out(2)
                dve.wait_ge(ng_ok.h, ng_ok.at(it, G))
                heads = Ng[:, :, :].rearrange("p b (h d) -> p (b h) d", h=HEADS)
                normed = v.mark(dve.tensor_tensor(heads, heads, hrs[:, :].unsqueeze(2).broadcast_to(
                    [P, G * HEADS, HD]), ALU.mult))
                dve.wait_ge(xg_ok.h, xg_ok.at(it, 1))
                dve.wait_ge(v.h, v.upto(normed))
                dve.tensor_tensor(x3[:, :, :], Ng[:, :, :], xg[:, :, :], ALU.add).then_inc(x3_ok.h, 1)
                dve.wait_ge(x3_ok.h, x3_ok.at(it, 1))
                for b in range(G):
                    ins = dve.bn_stats(stat[2][:, b, :], x3[:, b, :])
                link(ins)
                g_out(3)
                ln_moments(2, link)
                dve.wait_ge(rs0_ok[2].h, rs0_ok[2].at(it, 1))
                ln_scale(2, link)
                dve.wait_ge(xn2T_mm.h, xn2T_mm.at(it, 2))
                ln_apply(2, x3, xn3)
                o_out(2)
                o_out(3)
                v.end()

            with dve.Fori(0, LAST) as it:
                step(it)
            step(LAST, last=True)

        @block.tensor
        def _(pe):
            def transposes(it, src, banks, mm, waits, chunks=range(KD)):
                for w, k in waits:
                    pe.wait_ge(w.h, w.at(it, k))
                for c in chunks:
                    for b in range(G):
                        ins = pe.transpose(banks[c][:, b * S:(b + 1) * S], src[:, b, c * P:(c + 1) * P], ident[:, :])
                    ins.then_inc(mm.h, 1)

            def turn_xn1(it):
                transposes(it, xn1, TAB, xn1T_mm, [(xn_ok[0], 1), (x2_ok, G)])

            def turn_xn2(it, c):
                transposes(it, xn2, TAB, xn2T_mm, [(xn_ok[1], 1), (xn1T_ok, 2)], [c])

            def turn_ctx(it):
                transposes(it, ctxn, [QQ, DD], ctxT_mm, [(ctx_loaded, 16), (dexp_ok, 2 * G), (c_ok, 2 * G)])

            def project_q(it, m, k):
                pe.wait_ge(xn2T_ok.h, xn2T_ok.at(it, m + 1))
                ins = pe.matmul(TAB[m][:, :], A_w[:, k, m * P:(m + 1) * P], xn1T[:, k, :],
                                start=(k == 0), stop=(k == 1))
                if k == 1:
                    ins.then_inc(qT_mm.h, 1)

            pe.wait_ge(s_ident, 1)
            pe.wait_ge(s_load_a, 16 * LOADS_A)
            for w in range(3):
                if w == 2:
                    pe.wait_ge(s_set_v, V_WT)
                for ec in range(KD):
                    for kd in range(KD):
                        ins = pe.transpose(TAB[w % 2][:, ec * D + kd * P:ec * D + kd * P + P],
                                           wn[:, kd, w * D + ec * P:w * D + ec * P + P], ident[:, :])
                ins.then_inc(s_set_pe, 1)
            pe.wait_ge(s_set_v, V_WT + 2)
            for k in range(KD):
                for ec in range(KD):
                    ins = pe.matmul(UAB[k][:, 0:D], wT[:, 0, ec, k * P:(k + 1) * P], wT[:, 1, ec, :],
                                    start=(ec == 0), stop=(ec == 1))
                ins.then_inc(s_set_pe, 1)
            for k in range(KD):
                pe.wait_ge(s_set_v, V_WT + 3 + k)
                for ec in range(KD):
                    ins = pe.matmul(UAB[k][:, 0:D], wT[:, 2, ec, k * P:(k + 1) * P], wp[:, ec, :],
                                    start=(ec == 0), stop=(ec == 1))
                ins.then_inc(s_set_pe, 1)
            for ec in range(KD):
                pe.matmul(DD[:, 0:D], bB[:, 0, ec, :], wT[:, 0, ec, :], start=(ec == 0), stop=(ec == 1))
            for ec in range(KD):
                pe.matmul(DD[:, D:2 * D], bB[:, 1, ec, :], wp[:, ec, :], start=(ec == 0), stop=(ec == 1))
            for m in range(KD):
                for ec in range(KD):
                    pe.matmul(QQ[:, m:m + 1], wT[:, 1, ec, m * P:(m + 1) * P], bcol[:, ec:ec + 1],
                              start=(ec == 0), stop=(ec == 1))
            for ec in range(KD):
                ins = pe.matmul(QQ[:, KD:KD + 1], bB[:, 0, ec, :], bcol[:, ec:ec + 1], start=(ec == 0), stop=(ec == 1))
            ins.then_inc(s_set_pe, 1)
            for k in range(4):
                src = wg3[0:16, k * P:(k + 1) * P] if k < 2 else wgn[0:16, (k - 2) * P:(k - 1) * P]
                ins = pe.transpose(PV[:, 16 * k:16 * k + 16], src, ident[0:16, 0:16])
            ins.then_inc(s_set_pe, 1)
            for i in range(4):
                pe.wait_ge(s_set_v, V_W1 if i < 2 else V_TAB + 2 * (i - 1))
                for q in range(4):
                    src = w1p[i][:, q * P:(q + 1) * P]
                    ins = pe.transpose(TAB[i % 2][:, q * P:(q + 1) * P], src, ident[:, :])
                ins.then_inc(s_set_pe, 1)
            for i in range(4):
                pe.wait_ge(s_set_v, V_TAB + 8 + 2 * (i - 1))
                for kk in range(2):
                    for oc in range(KD):
                        src = w2p[i][:, oc * D + kk * P:oc * D + kk * P + P]
                        ins = pe.transpose(TAB[i % 2][:, kk * D + oc * P:kk * D + oc * P + P], src, ident[:, :])
                ins.then_inc(s_set_pe, 1)
            pe.wait_ge(s_set_v, SETUP_V)

            turn_xn1(-1)
            turn_xn2(-1, 0)
            turn_xn2(-1, 1)
            turn_ctx(-1)
            for m in range(KD):
                for k in range(KD):
                    project_q(-1, m, k)

            def step(it, last=False):
                pe.wait_ge(gsT_ok.h, gsT_ok.at(it, 0))
                pe.wait_ge(xn2T_ok.h, xn2T_ok.at(it, 0))
                pe.wait_ge(ctxT_ok.h, ctxT_ok.at(it, 0))
                if not last:
                    for k in range(4):
                        src = xn2T if k < 2 else ctxT
                        for b in range(G):
                            ins = pe.matmul(GT[32 * b:32 * b + 32, 0:S], WgT[:, k, :], src[:, k % 2, b * S:(b + 1) * S],
                                            start=(k == 0), stop=(k == 3))
                    ins.then_inc(gate_mm.h, 1)
                pe.wait_ge(qT_ok.h, qT_ok.at(it, 0))

                def score(b):
                    for k in range(KD):
                        ins = pe.matmul(TAB[0][:, b * S:(b + 1) * S], qT[:, k, b * S:(b + 1) * S],
                                        xn1T[:, k, b * S:(b + 1) * S], start=(k == 0), stop=(k == 1))
                    return ins

                if not last:
                    for b in range(1):
                        score(b)
                transposes(it, xn3, [QQ, DD], xn3T_mm, [(xn_ok[2], 0)])
                if not last:
                    for b in range(1, G):
                        ins = score(b)
                    ins.then_inc(score_mm.h, 1)
                if not last:
                    pe.wait_ge(gate_ok.h, gate_ok.at(it, 1))
                pe.wait_ge(z_ok.h, z_ok.at(it, 1))
                for k in range(KD):
                    for b in range(G):
                        ins = pe.matmul(GT[32 * b:32 * b + 32, 0:S], Z[:, k, b, :], xn3T[:, k, b * S:(b + 1) * S],
                                        start=(k == 0), stop=(k == 1))
                ins.then_inc(gram_mm.h, 1)

                def up(hc):
                    if hc == 0:
                        pe.wait_ge(HT_ok.h, HT_ok.at(it, 0))
                        pe.wait_ge(xn3h_ok.h, xn3h_ok.at(it, 2))
                    elif hc == 2:
                        pe.wait_ge(ot_ok.h, ot_ok.at(it, 0))
                    elif hc == 5:
                        pe.wait_ge(t_ok.h, t_ok.at(it, 2))
                    elif hc >= 6:
                        pe.wait_ge(h_ok.h, h_ok.at(it, hc - 5))
                    for w, xt in ((W1h, xn3h), (W1l, xn3h), (W1h, xn3l)):
                        for k in range(KD):
                            if hc == 0 and xt is xn3l:
                                pe.wait_ge(xn3l_ok.h, xn3l_ok.at(it, k + 1))
                            pe.matmul(UP[hc % 6][:, :], w[:, k, hc * P:(hc + 1) * P], xt[:, k, :],
                                      start=(w is W1h and xt is xn3h and k == 0), stop=False)

                def up_adapter(hc):
                    if hc == 0:
                        pe.wait_ge(adapter_ok.h, adapter_ok.at(it, 1))
                    pe.matmul(UP[hc % 6][:, :], Et[:, hc * P:(hc + 1) * P], Tt[:, :], start=False, stop=True)\
                      .then_inc(up_mm.h, 1)

                for hc in range(3):
                    up(hc)
                if not last:
                    pe.wait_ge(csum_ok.h, csum_ok.at(it, 1))
                    pe.matmul(DD[0:32, 0:P], sel_i[:, :], gate[:, :], start=True, stop=False)
                    pe.matmul(DD[0:32, 0:P], sel_nf[:, :], csum[:, :], start=False, stop=True)
                    pe.matmul(DD[0:32, P:2 * P], sel_f[:, :], csum[:, :], start=True, stop=True).then_inc(sel_mm.h, 1)
                up(3)
                up(4)
                up_adapter(0)
                up_adapter(1)
                for hc in range(5, KH):
                    up(hc)
                    up_adapter(hc - 3)
                for hc in range(KH - 3, KH):
                    up_adapter(hc)

                def down(b):
                    pe.wait_ge(fill_ok.h, fill_ok.at(it, b + 1))
                    if b == 0:
                        pe.wait_ge(h_ok.h, h_ok.at(it, HI_ACT))
                    elif b >= 2:
                        pe.wait_ge(ot_ok.h, ot_ok.at(it, b - 1))
                    for i, (ht, w) in enumerate(((hh, W2h), (hh, W2l), (hl, W2h))):
                        for k in range(KH):
                            if b == 0 and i == 0 and k >= HI_ACT:
                                pe.wait_ge(hi_ok.h, hi_ok.at(it, k - HI_ACT + 1))
                            if b == 0 and ht is hl and k == 0:
                                pe.wait_ge(hl_ok.h, hl_ok.at(it, LO_POOL))
                            if b == 0 and ht is hl and k >= LO_POOL:
                                pe.wait_ge(lo_ok.h, lo_ok.at(it, k - LO_POOL + 1))
                            ins = pe.matmul(UAB[b % 2][:, 0:WD], ht[:, k, b * S:(b + 1) * S], w[:, k, :],
                                            start=(i == 0 and k == 0), stop=(i == 2 and k == KH - 1))
                    ins.then_inc(down_mm.h, 1)

                def turn_g(b, w, k):
                    pe.wait_ge(w.h, w.at(it, k))
                    pe.wait_ge(gs_ok.h, gs_ok.at(it, b + 1))
                    pe.transpose(GT[0:EXTRA, 0:S], gs[:, :], ident[:, :]).then_inc(gsT_mm.h, 1)

                def adapt(b):
                    pe.wait_ge(gsT_ok.h, gsT_ok.at(it, b + 1))
                    if b == 0:
                        pe.wait_ge(ev_loaded.h, ev_loaded.at(it, R * G * 16))
                    pe.matmul(UAB[b % 2][:, 0:D], gsT[:, :], Ev[:, b, :], start=False, stop=True,
                              skip_group_check=True).then_inc(adapt_mm.h, 1)

                if last:
                    down(0)
                    turn_g(0, h_ok, 6)
                    for b in range(1, G):
                        if b == 2:
                            adapt(1)
                        down(b)
                        if b != 2:
                            adapt(b - 1)
                        turn_g(b, gsT_ok, b)
                    adapt(G - 1)
                    return

                def decay(b, hf):
                    k = 2 * b + hf
                    pe.wait_ge(dexp_ok.h, dexp_ok.at(it, k))
                    if k == 0:
                        pe.wait_ge(parts_ok.h, parts_ok.at(it, 1))
                    h0 = HEADS * b + 4 * hf
                    pe.matmul(DD[:, :], parts[:, 0, :], pick[:, h0:h0 + 4].unsqueeze(2).broadcast_to([96, 4, P]),
                              start=True, stop=True)
                    pe.matmul(DD[:, :], ident_h[:, :], later[:, :].unsqueeze(1).broadcast_to([P, 4, P]),
                              start=False, stop=True, skip_group_check=True)
                    for h in range(4):
                        ins = pe.matmul(DD[:, h * P:(h + 1) * P], pick[:, h0 + h:h0 + h + 1].broadcast_to([96, P]), parts[:, 1, :],
                                        start=False, stop=True, skip_group_check=True)
                    ins.then_inc(d_mm.h, 1)

                def qk(b, hf):
                    pe.wait_ge(c_ok.h, c_ok.at(it, 2 * b + hf))
                    if b == 0 and hf == 0:
                        pe.wait_ge(qpad_loaded.h, qpad_loaded.at(it, 8 * 16))
                    pe.matmul(QQ[:, :], ctxT[:, hf, b * S:(b + 1) * S], qpad[:, hf, :, b * S:(b + 1) * S],
                              start=True, stop=True).then_inc(qk_mm.h, 1)

                def pv(b):
                    pe.wait_ge(HT_ok.h, HT_ok.at(it, b))
                    pe.wait_ge(c_ok.h, c_ok.at(it, 2 * b + 2))
                    if b == 0:
                        pe.wait_ge(vc_ok.h, vc_ok.at(it, 1))
                    for h in range(HEADS):
                        q = 32 * (h % 4)
                        pe.matmul(PV[q:q + 32, 2 * P:3 * P], onehot[:, h, :], C[:, h, :],
                                  start=(h < 4), stop=(h >= 4))
                    for h in range(HEADS):
                        q = 32 * (h % 4)
                        ins = pe.matmul(PV[q:q + 32, (h // 4) * P:(h // 4 + 1) * P], vc[:, b, HD * h:HD * h + HD],
                                        C[:, h, :], start=True, stop=True)
                    ins.then_inc(pv_mm.h, 1)

                def turn_h(b):
                    pe.wait_ge(HS_ok.h, HS_ok.at(it, b + 1))
                    for k in range(3):
                        ins = pe.transpose(PV[:, k * P:(k + 1) * P], HS[:, k * P:(k + 1) * P], ident[:, :])
                    ins.then_inc(ht_mm.h, 1)

                decay(0, 0)
                pe.wait_ge(h_ok.h, h_ok.at(it, 5))
                qk(0, 0)
                down(0)
                decay(0, 1)
                pe.wait_ge(probs_ok.h, probs_ok.at(it, 1))
                for b in range(G):
                    ins = pe.transpose(TAB[1][:, b * S:(b + 1) * S], y[:, b * S:(b + 1) * S], ident[:, :])
                ins.then_inc(PT_mm.h, 1)
                qk(0, 1)
                turn_g(0, h_ok, 6)
                pe.wait_ge(PT_ok.h, PT_ok.at(it, 1))
                pe.wait_ge(sc_ok.h, sc_ok.at(it, 1))
                for m in range(KD):
                    for b in range(G):
                        ins = pe.matmul(TAB[m][:, b * S:(b + 1) * S], xn1[:, b, m * P:(m + 1) * P],
                                        PT[:, b * S:(b + 1) * S], start=True, stop=True)
                    ins.then_inc(px_mm.h, 1)
                pe.wait_ge(em_ok.h, em_ok.at(it, 1))
                pe.wait_ge(gsT_ok.h, gsT_ok.at(it, 1))
                pe.transpose(GT[:, 0:P], em[:, :], ident[:, :]).then_inc(em_mm.h, 1)
                adapt(0)
                decay(1, 0)
                pv(0)
                qk(1, 0)
                down(1)
                pe.wait_ge(px_ok.h, px_ok.at(it, 2))
                for b in range(G):
                    for k in range(KD):
                        ins = pe.matmul(TAB[b // 2][:, (b % 2) * D:(b % 2) * D + D], pxT[:, k, b * S:(b + 1) * S],
                                        Wvp[:, k, :], start=(k == 0), stop=(k == 1))
                    if b % 2 == 1:
                        ins.then_inc(wv_mm.h, 1)
                turn_h(0)
                decay(1, 1)
                qk(1, 1)
                turn_g(1, emT_ok, 1)
                decay(2, 0)
                pv(1)
                qk(2, 0)
                adapt(1)
                decay(2, 1)
                turn_h(1)
                qk(2, 1)
                decay(3, 0)
                pv(2)
                qk(3, 0)
                turn_h(2)
                decay(3, 1)
                qk(3, 1)
                turn_xn1(it)
                pv(3)
                turn_xn2(it, 0)
                turn_h(3)
                turn_xn2(it, 1)
                down(2)
                turn_ctx(it)
                project_q(it, 0, 0)
                project_q(it, 0, 1)
                turn_g(2, gsT_ok, 2)
                down(3)
                adapt(2)
                project_q(it, 1, 0)
                turn_g(3, gsT_ok, 3)
                project_q(it, 1, 1)
                adapt(3)

            with pe.Fori(0, LAST) as it:
                step(it)
            step(LAST, last=True)


LOADS_A = 6
LOADS = 2 * KD + CB + 4
V_WT = 7 + 2 + 1
V_BIAS = V_WT + 2 + 2 + 2 + 4
V_W1 = V_BIAS + 4
V_TAB = V_W1 + 8 + 1 + 2 + 2
SETUP_V = V_TAB + 8 + 8 + 2


def kernel(**inputs):
    import concourse.bacc as bacc
    from concourse.bass_utils import run_bass_kernel_spmd

    nc = bacc.Bacc("TRN2", target_bir_lowering=False, num_devices=1)
    names = ["x", "ctx_1024", "L0_attn_W_qkv", "L0_attn_b_qkv", "L0_attn_W_proj", "L0_attn_b_proj",
             "L0_xattn_Wi_w", "L0_xattn_Wi_b", "L0_xattn_Wf_w", "L0_xattn_Wf_b", "L0_xattn_gn_w",
             "L0_xattn_gn_b", "L0_ffn_W1", "L0_ffn_b1", "L0_ffn_W2", "L0_ffn_b2", "L0_ffn_scale"]
    arrays, args = {}, []
    for name in names:
        a = np.ascontiguousarray(inputs[name])
        if a.ndim == 0:
            a = a.reshape(1)
        arrays[name] = a
        args.append(nc.dram_tensor(name, a.shape, mybir.dt.from_np(a.dtype), kind="ExternalInput").ap())
    out = nc.dram_tensor("out", arrays["x"].shape, F32, kind="ExternalOutput").ap()
    build(nc, *args, out)
    r = run_bass_kernel_spmd(nc, [arrays], core_ids=[0])
    return r.results[0]["out"]
```
